# Optimizing a Trainium2 kernel written in Bass

```python
import numpy as np
import jax
import jax.numpy as jnp

def _softmax(x, axis=-1):
    return jax.nn.softmax(x, axis=axis)

def _gelu(x):
    return jax.nn.gelu(x, approximate=True)

def _silu(x):
    return jax.nn.silu(x)

def _sigmoid(x):
    return jax.nn.sigmoid(x)

def _layernorm(x, axis=-1, eps=1e-05):
    m = jnp.mean(x, axis=axis, keepdims=True)
    v = jnp.var(x, axis=axis, keepdims=True)
    return (x - m) / jnp.sqrt(v + eps)

def _scatter_add(tgt, idx, src, axis=0):
    return tgt.at[idx].add(src)

def _segment_sum(src, seg, n):
    return jax.ops.segment_sum(src, seg, n)
kernel_name = 'mk_decoder_preln_d1_seqx_r4_e74665'

def setup_inputs(seed: int=0):
    np.random.seed(seed)
    _w = jnp.asarray

    def _rec_inputs():
        import jax
        import jax.numpy as jnp
        _rk = jax.random.key(seed)
        x = -0.000125 + 0.9999 * jax.random.normal(jax.random.fold_in(_rk, 1), (4, 512, 512), jnp.float32)
        _lenS = 512 - jax.random.randint(jax.random.fold_in(_rk, 7), (4,), 0, max(1, 512 // 4) + 1, jnp.int32)
        _lenS2 = 512 - jax.random.randint(jax.random.fold_in(_rk, 8), (4,), 0, max(1, 512 // 4) + 1, jnp.int32)
        fside_BxS2xS2_0 = -3.05549e-07 + 0.0199987 * jax.random.normal(jax.random.fold_in(_rk, 11), (4, 512, 512), jnp.float32)
        _ctx_1024P = jax.random.normal(jax.random.fold_in(_rk, 12), (4, 16, 256), jnp.float32)
        _ctx_1024c = jax.random.dirichlet(jax.random.fold_in(_rk, 512), 0.3 * jnp.ones((16,), jnp.float32), (4, 512))
        _ctx_1024t = jnp.einsum('bsk,bkd->bsd', _ctx_1024c, _ctx_1024P)
        _ctx_1024t = _ctx_1024t * jax.lax.rsqrt(jnp.mean(jnp.square(_ctx_1024t)) + 1e-12) * 0.953939
        ctx_1024 = 6.82029e-06 + 0.0200006 * (_ctx_1024t + 0.3 * jax.random.normal(jax.random.fold_in(_rk, 612), (4, 512, 256), jnp.float32))
        return (x, fside_BxS2xS2_0, ctx_1024)
    x, fside_BxS2xS2_0, ctx_1024 = _rec_inputs()

    def _L0_attn_setup():
        import jax, jax.numpy as jnp
        import numpy as np
        D_MODEL = 512
        HEADS = 16
        HEAD_DIM = D_MODEL // HEADS
        key = jax.random.key(seed)
        k1, k2, k3 = jax.random.split(key, 3)
        B, S = (1, 512)
        x = jax.random.normal(k1, (B, S, D_MODEL), dtype=jnp.float32)
        Wqkv_w = jax.random.normal(k2, (D_MODEL + 2 * HEAD_DIM, D_MODEL), dtype=jnp.float32) * D_MODEL ** (-0.5)
        Wqkv_b = jnp.zeros((D_MODEL + 2 * HEAD_DIM,), dtype=jnp.float32)
        out_w = jax.random.normal(k3, (D_MODEL, D_MODEL), dtype=jnp.float32) * D_MODEL ** (-0.5)
        out_b = jnp.zeros((D_MODEL,), dtype=jnp.float32)
        return {'x': x, 'Wqkv_w': Wqkv_w, 'Wqkv_b': Wqkv_b, 'out_w': out_w, 'out_b': out_b}
    _L0_attn_all = _L0_attn_setup()
    _L0_attn_in = {k: v for k, v in _L0_attn_all.items() if k in ('Wqkv_w', 'Wqkv_b', 'out_w', 'out_b')}
    del _L0_attn_all

    def _L0_xattn_setup():
        import jax, jax.numpy as jnp
        import numpy as np
        EPS = 1e-06
        QMAX = 127.0

        def _smooth_quant_linear(x, w):
            amax_x = jnp.max(jnp.abs(x), axis=0)
            amax_w = jnp.max(jnp.abs(w), axis=0)
            s = jnp.sqrt(jnp.maximum(amax_x, EPS) / jnp.maximum(amax_w, EPS))
            s = jnp.maximum(s, EPS)
            xs = x / s
            ws = w * s
            x_scale = jnp.maximum(jnp.max(jnp.abs(xs), axis=-1, keepdims=True), EPS) / QMAX
            w_scale = jnp.maximum(jnp.max(jnp.abs(ws), axis=-1, keepdims=True), EPS) / QMAX
            x_q = jnp.clip(jnp.round(xs / x_scale), -QMAX, QMAX)
            w_q = jnp.clip(jnp.round(ws / w_scale), -QMAX, QMAX)
            return x_q @ w_q.T * x_scale * w_scale.T

        def _expert_forward(xe, guw, dw):
            h = _smooth_quant_linear(xe, guw)
            gate, up = jnp.split(h, 2, axis=-1)
            a = jax.nn.silu(gate) * up
            return _smooth_quant_linear(a, dw)
        key = jax.random.key(seed)
        k1, k2, k3 = jax.random.split(key, 3)
        E, T, D, I = (8, 512, 512, 256)
        x = jax.random.normal(k1, (E, T, D), dtype=jnp.float32)
        gate_up_weight = jax.random.normal(k2, (E, 2 * I, D), dtype=jnp.float32) * 0.02
        down_weight = jax.random.normal(k3, (E, D, I), dtype=jnp.float32) * 0.02
        return {'x': x, 'gate_up_weight': gate_up_weight, 'down_weight': down_weight}
    _L0_xattn_all = _L0_xattn_setup()
    _L0_xattn_in = {k: v for k, v in _L0_xattn_all.items() if k in ()}
    del _L0_xattn_all

    def _L0_ffn_setup():
        import jax, jax.numpy as jnp
        import numpy as np
        B, L, D = (2, 256, 512)
        E, TOP_K, RANK, DFF = (8, 2, 8, 1376)

        def _lora(x, A, Bm, scale):
            return x @ A @ Bm * scale

        def _expert_lora(x, A, Bm, w, scale):
            xA = jnp.einsum('bld,edr->bler', x, A)
            xAB = jnp.einsum('bler,erd->bled', xA, Bm) * scale
            return (xAB * w).sum(axis=2)
        key = jax.random.key(seed)
        ks = jax.random.split(key, 18)
        r = lambda k, s, sc: jax.random.normal(k, s, dtype=jnp.float32) * sc
        inv_d = 1.0 / np.sqrt(D)
        inv_f = 1.0 / np.sqrt(DFF)
        return {'x': r(ks[0], (B, L, D), 1.0), 'W_router': r(ks[1], (D, E), inv_d), 'W_gate': r(ks[2], (D, DFF), inv_d), 'W_up': r(ks[3], (D, DFF), inv_d), 'W_down': r(ks[4], (DFF, D), inv_f), 'sA_gate': r(ks[5], (D, RANK), inv_d), 'sB_gate': r(ks[6], (RANK, DFF), 0.02), 'sA_up': r(ks[7], (D, RANK), inv_d), 'sB_up': r(ks[8], (RANK, DFF), 0.02), 'sA_down': r(ks[9], (DFF, RANK), inv_f), 'sB_down': r(ks[10], (RANK, D), 0.02), 'A_gate': r(ks[11], (E, D, RANK), inv_d), 'B_gate': r(ks[12], (E, RANK, DFF), 0.02), 'A_up': r(ks[13], (E, D, RANK), inv_d), 'B_up': r(ks[14], (E, RANK, DFF), 0.02), 'A_down': r(ks[15], (E, DFF, RANK), inv_f), 'B_down': r(ks[16], (E, RANK, D), 0.02), 'expert_bias': jnp.zeros((E,), dtype=jnp.float32)}
    _L0_ffn_all = _L0_ffn_setup()
    _L0_ffn_in = {k: v for k, v in _L0_ffn_all.items() if k in ('W_router', 'W_gate', 'W_up', 'W_down', 'sA_gate', 'sB_gate', 'sA_up', 'sB_up', 'sA_down', 'sB_down', 'A_gate', 'B_gate', 'A_up', 'B_up', 'A_down', 'B_down', 'expert_bias')}
    del _L0_ffn_all
    return {'x': x, 'fside_BxS2xS2_0': fside_BxS2xS2_0, 'ctx_1024': ctx_1024, 'L0_attn_Wqkv_w': _L0_attn_in['Wqkv_w'], 'L0_attn_Wqkv_b': _L0_attn_in['Wqkv_b'], 'L0_attn_out_w': _L0_attn_in['out_w'], 'L0_attn_out_b': _L0_attn_in['out_b'], 'L0_ffn_W_router': _L0_ffn_in['W_router'], 'L0_ffn_W_gate': _L0_ffn_in['W_gate'], 'L0_ffn_W_up': _L0_ffn_in['W_up'], 'L0_ffn_W_down': _L0_ffn_in['W_down'], 'L0_ffn_sA_gate': _L0_ffn_in['sA_gate'], 'L0_ffn_sB_gate': _L0_ffn_in['sB_gate'], 'L0_ffn_sA_up': _L0_ffn_in['sA_up'], 'L0_ffn_sB_up': _L0_ffn_in['sB_up'], 'L0_ffn_sA_down': _L0_ffn_in['sA_down'], 'L0_ffn_sB_down': _L0_ffn_in['sB_down'], 'L0_ffn_A_gate': _L0_ffn_in['A_gate'], 'L0_ffn_B_gate': _L0_ffn_in['B_gate'], 'L0_ffn_A_up': _L0_ffn_in['A_up'], 'L0_ffn_B_up': _L0_ffn_in['B_up'], 'L0_ffn_A_down': _L0_ffn_in['A_down'], 'L0_ffn_B_down': _L0_ffn_in['B_down'], 'L0_ffn_expert_bias': _L0_ffn_in['expert_bias']}

def reference(x, fside_BxS2xS2_0, ctx_1024, L0_attn_Wqkv_w, L0_attn_Wqkv_b, L0_attn_out_w, L0_attn_out_b, L0_ffn_W_router, L0_ffn_W_gate, L0_ffn_W_up, L0_ffn_W_down, L0_ffn_sA_gate, L0_ffn_sB_gate, L0_ffn_sA_up, L0_ffn_sB_up, L0_ffn_sA_down, L0_ffn_sB_down, L0_ffn_A_gate, L0_ffn_B_gate, L0_ffn_A_up, L0_ffn_B_up, L0_ffn_A_down, L0_ffn_B_down, L0_ffn_expert_bias):
    import jax
    import jax.numpy as jnp

    def _L0_attn_ref(x, Wqkv_w, Wqkv_b, out_w, out_b):
        import jax, jax.numpy as jnp
        import numpy as np
        D_MODEL = 512
        HEADS = 16
        HEAD_DIM = D_MODEL // HEADS
        B, S, _ = x.shape
        qkv = jnp.einsum('bsd,ed->bse', x, Wqkv_w) + Wqkv_b
        q = qkv[..., :D_MODEL]
        k = qkv[..., D_MODEL:D_MODEL + HEAD_DIM]
        v = qkv[..., D_MODEL + HEAD_DIM:]
        q = q.reshape(B, S, HEADS, HEAD_DIM)
        scale = 1.0 / np.sqrt(HEAD_DIM)
        scores = jnp.einsum('bqhd,bkd->bhqk', q, k) * scale
        min_val = jnp.finfo(scores.dtype).min
        causal = jnp.tril(jnp.ones((S, S), dtype=bool))
        scores = jnp.where(causal[None, None], scores, min_val)
        attn = jax.nn.softmax(scores, axis=-1)
        ctx = jnp.einsum('bhqk,bkd->bqhd', attn, v)
        ctx = ctx.reshape(B, S, D_MODEL)
        out = jnp.einsum('bsd,ed->bse', ctx, out_w) + out_b
        return out

    def _L0_xattn_ref(x, gate_up_weight, down_weight):
        import jax, jax.numpy as jnp
        import numpy as np
        EPS = 1e-06
        QMAX = 127.0

        def _smooth_quant_linear(x, w):
            amax_x = jnp.max(jnp.abs(x), axis=0)
            amax_w = jnp.max(jnp.abs(w), axis=0)
            s = jnp.sqrt(jnp.maximum(amax_x, EPS) / jnp.maximum(amax_w, EPS))
            s = jnp.maximum(s, EPS)
            xs = x / s
            ws = w * s
            x_scale = jnp.maximum(jnp.max(jnp.abs(xs), axis=-1, keepdims=True), EPS) / QMAX
            w_scale = jnp.maximum(jnp.max(jnp.abs(ws), axis=-1, keepdims=True), EPS) / QMAX
            x_q = jnp.clip(jnp.round(xs / x_scale), -QMAX, QMAX)
            w_q = jnp.clip(jnp.round(ws / w_scale), -QMAX, QMAX)
            return x_q @ w_q.T * x_scale * w_scale.T

        def _expert_forward(xe, guw, dw):
            h = _smooth_quant_linear(xe, guw)
            gate, up = jnp.split(h, 2, axis=-1)
            a = jax.nn.silu(gate) * up
            return _smooth_quant_linear(a, dw)
        return jax.vmap(_expert_forward)(x, gate_up_weight, down_weight)

    def _L0_ffn_ref(x, W_router, W_gate, W_up, W_down, sA_gate, sB_gate, sA_up, sB_up, sA_down, sB_down, A_gate, B_gate, A_up, B_up, A_down, B_down, expert_bias):
        import jax, jax.numpy as jnp
        import numpy as np
        B, L, D = (2, 256, 512)
        E, TOP_K, RANK, DFF = (8, 2, 8, 1376)

        def _lora(x, A, Bm, scale):
            return x @ A @ Bm * scale

        def _expert_lora(x, A, Bm, w, scale):
            xA = jnp.einsum('bld,edr->bler', x, A)
            xAB = jnp.einsum('bler,erd->bled', xA, Bm) * scale
            return (xAB * w).sum(axis=2)
        scale = 1.0 / RANK
        logits = x @ W_router
        scores = jax.nn.sigmoid(logits)
        biased = scores + expert_bias
        _, topk_idx = jax.lax.top_k(biased, TOP_K)
        topk_scores = jnp.take_along_axis(scores, topk_idx, axis=-1)
        topk_w = topk_scores / (topk_scores.sum(-1, keepdims=True) + 1e-08)
        one_hot = jax.nn.one_hot(topk_idx, E, dtype=x.dtype)
        expert_weights = (one_hot * topk_w[..., None]).sum(axis=2)
        w = expert_weights[..., None]
        gate = x @ W_gate + _lora(x, sA_gate, sB_gate, scale) + _expert_lora(x, A_gate, B_gate, w, scale)
        up = x @ W_up + _lora(x, sA_up, sB_up, scale) + _expert_lora(x, A_up, B_up, w, scale)
        hidden = jax.nn.silu(gate) * up
        out = hidden @ W_down + _lora(hidden, sA_down, sB_down, scale) + _expert_lora(hidden, A_down, B_down, w, scale)
        return out
    x = x + _L0_attn_ref(_layernorm(x, axis=-1), L0_attn_Wqkv_w, L0_attn_Wqkv_b, L0_attn_out_w, L0_attn_out_b)
    x = x + _L0_xattn_ref(_layernorm(x, axis=-1), fside_BxS2xS2_0, ctx_1024)
    x = x + _L0_ffn_ref(_layernorm(x, axis=-1), L0_ffn_W_router, L0_ffn_W_gate, L0_ffn_W_up, L0_ffn_W_down, L0_ffn_sA_gate, L0_ffn_sB_gate, L0_ffn_sA_up, L0_ffn_sB_up, L0_ffn_sA_down, L0_ffn_sB_down, L0_ffn_A_gate, L0_ffn_B_gate, L0_ffn_A_up, L0_ffn_B_up, L0_ffn_A_down, L0_ffn_B_down, L0_ffn_expert_bias)
    return x

_drawn_inputs = setup_inputs


def setup_inputs(seed=0):
    import zlib

    import numpy as np

    out = dict(_drawn_inputs(seed))
    spreads = {'L0_attn_Wqkv_b': (0.0, 0.1),
     'L0_attn_out_b': (0.0, 0.1),
     'L0_ffn_expert_bias': (0.0, 0.8)}
    factors = {'L0_ffn_W_router': 8.0,
     'L0_ffn_sA_gate': 8.0,
     'L0_ffn_sB_gate': 8.0,
     'L0_ffn_sA_up': 8.0,
     'L0_ffn_sB_up': 8.0,
     'L0_ffn_sA_down': 8.0,
     'L0_ffn_sB_down': 8.0,
     'L0_ffn_A_gate': 8.0,
     'L0_ffn_B_gate': 8.0,
     'L0_ffn_A_up': 8.0,
     'L0_ffn_B_up': 8.0,
     'L0_ffn_A_down': 8.0,
     'L0_ffn_B_down': 8.0}
    for name, (base, spread) in spreads.items():
        noise = np.random.default_rng([zlib.crc32(name.encode()), seed]).standard_normal(out[name].shape)
        drawn = base * np.exp(spread * noise) if base else spread * noise
        out[name] = jnp.asarray(drawn.astype(out[name].dtype))
    for name, factor in factors.items():
        out[name] = (out[name] * factor).astype(out[name].dtype)
    return out
```

```python
from contextlib import ExitStack

import numpy as np

import concourse.bass as bass
from concourse import mybir

F32 = mybir.dt.float32
F32R = mybir.dt.float32r
BF16 = mybir.dt.bfloat16
ALU = mybir.AluOpType
ACT = mybir.ActivationFunctionType
AX = mybir.AxisListType

P = 128
BATCH, T, D = 4, 512, 512
HEADS, HD = 16, 32
KT = D // P
TT = T // P
QKV = D + 2 * HD
INNER = 256
IT = INNER // P
DFF, RANK, EXPERTS = 1376, 8, 8
FT = -(-DFF // P)
FLAST = DFF - (FT - 1) * P
ER = EXPERTS * RANK
LR = ER + RANK
ROUTE = 96
LA = ROUTE + EXPERTS
LN_EPS, QEPS, QMAX = 1e-5, 1e-6, 127.0
MAGIC = 1.5 * 2.0 ** 23
NEG = -1e38
SCALE = HD ** -0.5
KROWS = 3 * HD


DVE_LINKS = 2 + 1 + 2 * (4 + 3)


def f_rows(f):
    return P if f < FT - 1 else FLAST


class Signal:

    def __init__(self, ctx, nc, name, per):
        self.sem, self.per = ctx.enter_context(nc.semaphore(name)), per

    def at(self, b, n):
        assert 1 <= n <= self.per
        return b * self.per + n


class Link:

    def __init__(self, eng, signal, b):
        self.eng, self.chain, self.b, self.n = eng, signal, b, 0

    def __call__(self, ins):
        self.n += 1
        ins.then_inc(self.chain.sem, 1)
        self.eng.wait_ge(self.chain.sem, self.chain.at(self.b, self.n))

    def done(self):
        assert self.n == self.chain.per, (self.n, self.chain.per)


def separate(eng, passed):
    eng.sem_inc(passed.sem, 1)


class Tenants:

    def __init__(self, slots):
        self.slots, self.last, self.n = slots, {}, 0

    def new_batch(self, first):
        self.n, self.old, self.last = 0, dict(self.last), {}

    def claim(self, eng, b, signal, count):
        slot = self.n % self.slots
        self.n += 1
        if slot in self.last:
            before, at = self.last[slot]
            eng.wait_ge(before.sem, before.at(b, at))
        elif slot in self.old:
            before, at = self.old[slot]
            eng.wait_ge(before.sem, before.at(b - 1, at))
        self.last[slot] = (signal, count)
        return slot


def attention_and_mlp(nc, x, wqkv, bq, bkv, wo, bo, mlp_w, mlp_wT, mlp_d, mlp_dT, consts, x2):
    with ExitStack() as ctx:
        def sb(name, shape, dt=F32):
            return ctx.enter_context(nc.sbuf_tensor(name, shape, dt))

        def sig(name, per=1):
            return Signal(ctx, nc, name, per)

        cst = sb("cst", [P, 3, P])
        ident = cst[:, 0, :]
        mask_bf = sb("mask_bf", [P, 3, P], BF16)
        ones = sb("ones", [P, HD])
        half = sb("half", [P, 2 * KT])
        ln_eps, magic = sb("ln_eps", [P, TT]), sb("magic", [P, 1])
        stage = sb("stage", [P, QKV])
        wqkv_h, wqkv_l = sb("wqkv_h", [P, KT, QKV], F32R), sb("wqkv_l", [P, KT, QKV], F32R)
        wo_h, wo_l = sb("wo_h", [P, KT, D], F32R), sb("wo_l", [P, KT, D], F32R)
        bq_sb, bkv_sb = sb("bq_sb", [P, KT]), sb("bkv_sb", [2 * HD, 1])
        bo_bc = sb("bo_bc", [P, D])
        x_in = sb("x_in", [P, TT, D])
        stats, mv = sb("stats", [P, TT, 6]), sb("mv", [P, TT, 2])
        veps, rstd = sb("veps", [P, TT]), sb("rstd", [P, TT])
        xn = sb("xn", [P, TT, D])
        hT_h, hT_l = sb("hT_h", [P, KT, T], F32R), sb("hT_l", [P, KT, T], F32R)
        qT_h, qT_l = sb("qT_h", [P, KT, T], F32R), sb("qT_l", [P, KT, T], F32R)
        kst = sb("kst", [P, T], F32R)
        vT = sb("vT", [2 * HD, T])
        v = sb("v", [P, TT, HD])
        negm = sb("negm", [P, HEADS, TT])
        negm_h, negm_l = sb("negm_h", [HD, 2, P], F32R), sb("negm_l", [HD, 2, P], F32R)
        probs = sb("probs", [P, 4, 2, T])
        rden, cx = sb("rden", [P, T]), sb("cx", [P, 2, T])
        x1 = sb("x1", [P, TT, D])
        attn_ctx = ExitStack()
        qst = attn_ctx.enter_context(nc.sbuf_tensor("qst", [P, HEADS, T], F32R))
        attn_ctx.close()
        w_raw, wT_raw = sb("w_raw", [P, TT, D]), sb("wT_raw", [P, KT, D])
        d_raw, dT_raw = sb("d_raw", [P, TT, INNER]), sb("dT_raw", [P, IT, D])
        w_bf, wT_bf = sb("w_bf", [P, TT, D], BF16), sb("wT_bf", [P, KT, D], BF16)
        a_bf, aT_bf = sb("a_bf", [P, TT, D], BF16), sb("aT_bf", [P, KT, D], BF16)
        hid = sb("hid", [P, TT, D])
        th = sb("th", [P, TT, INNER])
        amax, sc = sb("amax", [P, 2, KT]), sb("sc", [P, 6, KT])
        rows, wrow = sb("rows", [P, 2, D]), sb("wrow", [P, D])
        qm, qs, qi = sb("qm", [P, 2, TT]), sb("qs", [P, 2, TT]), sb("qi", [P, 2, TT])

        slots = [ctx.enter_context(nc.psum_tensor(f"slot{i}", [P, 2, T], F32)) for i in range(3)]
        av = ctx.enter_context(nc.psum_tensor("av", [P, T], F32))
        den = ctx.enter_context(nc.psum_tensor("den", [P, T], F32))
        slots_bf = [s[:, :, :].bitcast(BF16) for s in slots]

        c_loaded = sig("c_loaded")
        w_loaded, w_used = sig("w_loaded", 16), sig("w_used", 1)
        masks_ready, consts_ready, halves_ready = sig("masks_ready"), sig("consts_ready", 6), sig("halves_ready", 16)
        x_loaded, mw_loaded, mwT_loaded = sig("x_loaded", 16), sig("mw_loaded", 16), sig("mwT_loaded", 16)
        md_loaded, mdT_loaded = sig("md_loaded", 16), sig("mdT_loaded", 16)
        ln_stats, rstd_ready, xn_ready = sig("ln_stats", 2), sig("rstd_ready", 2), sig("xn_ready", 2 * TT)
        xT_ps, xT_hi, xT_lo = sig("xT_ps", 4), sig("xT_hi", 2), sig("xT_lo", 2)
        xb_ready = sig("xb_ready")
        kv_ps, kv_act, kv_lo = sig("kv_ps"), sig("kv_act", 3), sig("kv_lo")
        q_ps, q_hi, q_lo = sig("q_ps", KT), sig("q_hi", KT), sig("q_lo", KT)
        v_ps, v_ready = sig("v_ps"), sig("v_ready")
        q_moved = [sig(f"q_moved{i}", 16 * 12) for i in range(2)]
        s_ps, s_max = sig("s_ps", 22), sig("s_max", 22)
        m_ps, m_hi, m_lo = sig("m_ps", 2), sig("m_hi", 2), sig("m_lo", 2)
        m_moved = [sig(f"m_moved{i}", 32) for i in range(2)]
        t_ps, p_ready, pv_done = sig("t_ps", 32), sig("p_ready", 32), sig("pv_done", 16)
        rden_ready, cx_ready, cx_hi, cx_lo = sig("rden_ready", 4), sig("cx_ready", 4), sig("cx_hi", 4), sig("cx_lo", 4)
        o_ps, x1_ready = sig("o_ps", 2), sig("x1_ready", 2)
        colmax = sig("colmax", 3)
        aT_ps = sig("aT_ps", 1)
        ratio, root, s_cols = sig("ratio", 2), sig("root", 2), sig("s_cols", 2)
        s_rows_ps, s_rows = sig("s_rows_ps", 2), sig("s_rows", 2)
        w_scaled, q_scale = sig("w_scaled", 2), sig("q_scale", 2)
        y_act, a_q, w_q = sig("y_act", 16), sig("a_q", 2), sig("w_q", 2)
        aq_ps, aqT, wq_ps, wqT = sig("aq_ps", 2), sig("aqT", 2), sig("wq_ps", 2), sig("wqT", 2)
        wrow_ps, wrow_ready = sig("wrow_ps", 2), sig("wrow_ready", 2)
        h_ps, h_ready, th_ready, act_ready = sig("h_ps", 4), sig("h_ready", 8), sig("th_ready"), sig("act_ready")
        x2_ready, x2_stored = sig("x2_ready", TT), sig("x2_stored", 16)
        dve_link, pool_link = sig("dve_link", DVE_LINKS), sig("pool_link", 2)
        passed = [sig(f"passed_{e}") for e in ("sp", "pe", "dve")]

        weight_rows = [(wqkv, wqkv_h, wqkv_l, k, QKV) for k in range(KT)] + [(wo, wo_h, wo_l, k, D) for k in range(KT)]

        block = ctx.enter_context(nc.Block())

        @block.sync
        def _(sp):
            sp.dma_start(cst[:, :, :], consts).then_inc(c_loaded.sem, 16)
            sp.dma_start(bq_sb[:, :], bq).then_inc(c_loaded.sem, 16)
            sp.dma_start(bkv_sb[:, :], bkv).then_inc(c_loaded.sem, 16)
            sp.dma_start(bo_bc[:, :], bo.partition_broadcast(P)).then_inc(c_loaded.sem, 16)

            def batch(b, first):
                if not first:
                    sp.wait_ge(x1_ready.sem, x1_ready.at(b - 1, 2))
                sp.dma_start(x_in[:, :, :], x[b].rearrange("(a p) d -> p a d", p=P)).then_inc(x_loaded.sem, 16)
                if first:
                    for n, (src, _, _, k, width) in enumerate(weight_rows):
                        if n:
                            sp.wait_ge(w_used.sem, n)
                        sp.dma_start(stage[:, 0:width], src[:, k, :]).then_inc(w_loaded.sem, 16)
                qst_by_quadrant = qst[:, :, :].rearrange("p (e j) t -> p e j t", j=4)
                for ep in range(2):
                    if not first:
                        sp.wait_ge(pv_done.sem, pv_done.at(b - 1, 16))
                        separate(sp, passed[0])
                    sp.wait_ge(q_hi.sem, q_hi.at(b, 2 * ep + 2))
                    sp.wait_ge(q_lo.sem, q_lo.at(b, 2 * ep + 2))
                    for j in range(4):
                        for src, row in ((qT_h, 0), (qT_l, HD), (qT_h, 2 * HD)):
                            sp.dma_start(qst_by_quadrant[row:row + HD, 2 * ep:2 * ep + 2, j, :].bitcast(F32),
                                         src[HD * j:HD * j + HD, 2 * ep:2 * ep + 2, :].bitcast(F32))\
                              .then_inc(q_moved[ep].sem, 16)
                for hf in range(2):
                    sp.wait_ge(m_hi.sem, m_hi.at(b, hf + 1))
                    sp.wait_ge(m_lo.sem, m_lo.at(b, hf + 1))
                    for src, row in ((negm_h, KROWS), (negm_l, KROWS + 1)):
                        sp.dma_start(qst[row:row + 1, 8 * hf:8 * hf + 8, :].bitcast(F32), src[:, hf, :].bitcast(F32))\
                          .then_inc(m_moved[hf].sem, 16)
                sp.wait_ge(pv_done.sem, pv_done.at(b, 16))
                for dst, src, loaded in ((w_raw, mlp_w, mw_loaded), (wT_raw, mlp_wT, mwT_loaded),
                                         (d_raw, mlp_d, md_loaded), (dT_raw, mlp_dT, mdT_loaded)):
                    sp.dma_start(dst[:, :, :], src[b].rearrange("(a p) d -> p a d", p=P)).then_inc(loaded.sem, 16)

            batch(0, True)
            with sp.Fori(1, BATCH) as b:
                batch(b, False)
            sp.wait_ge(x2_stored.sem, 16 * BATCH)

        @block.gpsimd
        def _(pool):
            for n, (dst, value) in enumerate(((ones[:, :], 1.0), (half[:, 0:KT], 0.5), (half[:, KT:2 * KT], -0.5),
                                              (kst[KROWS:P, :].bitcast(F32), 1.0), (ln_eps[:, :], LN_EPS),
                                              (magic[:, :], MAGIC))):
                pool.memset(dst, value).then_inc(consts_ready.sem, 1)
                pool.wait_ge(consts_ready.sem, n + 1)
            for n, (_, hi, lo, k, width) in enumerate(weight_rows):
                pool.wait_ge(w_loaded.sem, 16 * (n + 1))
                pool.tensor_copy(hi[:, k, :], stage[:, 0:width]).then_inc(halves_ready.sem, 1)
                pool.wait_ge(halves_ready.sem, n + 1)
                pool.tensor_tensor(lo[:, k, :], stage[:, 0:width], hi[:, k, :].bitcast(F32), ALU.subtract)\
                    .then_inc(w_used.sem, 1)

            def batch(b, first):
                link = Link(pool, pool_link, b)

                def inverse_deviation(n):
                    pool.wait_ge(ln_stats.sem, ln_stats.at(b, n))
                    link(pool.tensor_tensor(veps[:, :], mv[:, :, 1], ln_eps[:, :], ALU.add))
                    pool.tensor_tensor(rstd[:, :], veps[:, :], half[:, KT:2 * KT], ALU.pow).then_inc(rstd_ready.sem, 1)

                inverse_deviation(1)
                pool.wait_ge(xn_ready.sem, xn_ready.at(b, TT))
                pool.tensor_tensor(x_in[:, :, :], x_in[:, :, :], bo_bc[:, :].unsqueeze(1).to_broadcast([P, TT, D]),
                                   ALU.add).then_inc(xb_ready.sem, 1)
                for g in range(4):
                    pool.wait_ge(cx_hi.sem, cx_hi.at(b, g + 1))
                    pool.tensor_tensor(hT_l[:, g, :], cx[:, g % 2, :], hT_h[:, g, :].bitcast(F32), ALU.subtract)\
                        .then_inc(cx_lo.sem, 1)
                inverse_deviation(2)
                for n, (nk, width, w_loaded_, raw) in enumerate(((KT, D, mw_loaded, w_raw), (IT, INNER, md_loaded, d_raw))):
                    pool.wait_ge(ratio.sem, ratio.at(b, n + 1))
                    pool.tensor_tensor(sc[:, 2, 0:nk], sc[:, 1, 0:nk], half[:, 0:nk], ALU.pow).then_inc(root.sem, 1)
                    pool.wait_ge(s_rows.sem, s_rows.at(b, n + 1))
                    pool.wait_ge(w_loaded_.sem, w_loaded_.at(b, 16))
                    pool.tensor_tensor(raw[:, :, :], raw[:, :, :],
                                       rows[:, 0, 0:width].unsqueeze(1).to_broadcast([P, TT, width]),
                                       ALU.mult).then_inc(w_scaled.sem, 1)
                    pool.wait_ge(y_act.sem, y_act.at(b, 8 * n + 8))
                    pool.tensor_tensor(w_bf[:, :, 0:width], raw[:, :, :],
                                       magic[:, :].unsqueeze(1).to_broadcast([P, TT, width]), ALU.subtract)\
                        .then_inc(w_q.sem, 1)
                for tt in range(TT):
                    pool.wait_ge(h_ready.sem, h_ready.at(b, TT + tt + 1))
                    pool.tensor_tensor(hid[:, tt, :], hid[:, tt, :], x1[:, tt, :], ALU.add).then_inc(x2_ready.sem, 1)
                link.done()

            batch(0, True)
            with pool.Fori(1, BATCH) as b:
                batch(b, False)

        @block.scalar
        def _(act):
            act.wait_ge(c_loaded.sem, 64)
            act.activation(mask_bf[:, :, :], cst[:, :, :], ACT.Copy).then_inc(masks_ready.sem, 1)

            def batch(b, first):
                use = [0]

                def slot():
                    use[0] += 1
                    return slots[(use[0] - 1) % 3]

                for s in range(2):
                    act.wait_ge(xT_ps.sem, xT_ps.at(b, s + 1))
                    if not first and s == 0:
                        act.wait_ge(o_ps.sem, o_ps.at(b - 1, 2))
                    act.activation(hT_h[:, 2 * s:2 * s + 2, :], slot()[:, :, :], ACT.Copy).then_inc(xT_hi.sem, 1)
                act.wait_ge(kv_ps.sem, kv_ps.at(b, 1))
                kv = slot()
                act.activation(kst[0:HD, :], kv[0:HD, 0, :], ACT.Identity, bias=bkv_sb[0:HD, :]).then_inc(kv_act.sem, 1)
                act.activation(kst[HD:2 * HD, :], kv[0:HD, 0, :], ACT.Identity, bias=bkv_sb[0:HD, :])\
                    .then_inc(kv_act.sem, 1)
                act.activation(vT[HD:2 * HD, :], kv[HD:2 * HD, 0, :], ACT.Identity, bias=bkv_sb[HD:2 * HD, :])\
                    .then_inc(kv_act.sem, 1)
                for e in range(KT):
                    if e % 2 == 0:
                        ps = slot()
                    act.wait_ge(q_ps.sem, q_ps.at(b, e + 1))
                    if not first and e == 0:
                        for q in q_moved:
                            act.wait_ge(q.sem, q.at(b - 1, q.per))
                    act.activation(qT_h[:, e, :], ps[:, e % 2, :], ACT.Identity, bias=bq_sb[:, e:e + 1])\
                        .then_inc(q_hi.sem, 1)
                slot()
                for hf in range(2):
                    use[0] += 11
                    act.wait_ge(m_ps.sem, m_ps.at(b, hf + 1))
                    if not first:
                        act.wait_ge(m_moved[hf].sem, m_moved[hf].at(b - 1, 32))
                    act.activation(negm_h[:, hf, :], slot()[0:HD, 0, 0:P], ACT.Copy).then_inc(m_hi.sem, 1)
                step = 0
                for g in range(4):
                    for kt in reversed(range(TT)):
                        for pr in range(2):
                            act.wait_ge(t_ps.sem, t_ps.at(b, 2 * step + pr + 1))
                            if step >= 2:
                                act.wait_ge(pv_done.sem, pv_done.at(b, step - 1))
                            n = T - kt * P
                            act.activation(probs[:, 2 * (step % 2) + pr, :, 0:n], slot()[:, :, 0:n], ACT.Exp,
                                           scale=SCALE).then_inc(p_ready.sem, 1)
                        step += 1
                        if kt == 2 and g:
                            act.wait_ge(cx_ready.sem, cx_ready.at(b, g))
                            act.activation(hT_h[:, g - 1, :], cx[:, (g - 1) % 2, :], ACT.Copy).then_inc(cx_hi.sem, 1)
                act.wait_ge(cx_ready.sem, cx_ready.at(b, 4))
                act.activation(hT_h[:, 3, :], cx[:, 1, :], ACT.Copy).then_inc(cx_hi.sem, 1)
                use[0] += 4
                for n, (nk, width) in enumerate(((KT, D), (IT, INNER))):
                    if n:
                        act.wait_ge(h_ready.sem, h_ready.at(b, TT))
                        act.activation(th[:, :, :], hid[:, :, 0:INNER], ACT.Tanh, scale=0.5).then_inc(th_ready.sem, 1)
                        slot()
                    act.wait_ge(s_rows_ps.sem, s_rows_ps.at(b, n + 1))
                    act.activation(rows[:, :, 0:width], slot()[:, :, 0:width], ACT.Copy).then_inc(s_rows.sem, 1)
                    act.wait_ge(q_scale.sem, q_scale.at(b, n + 1))
                    a, w = ((xn, w_raw), (hid[:, :, 0:INNER], d_raw))[n]
                    for i, y in enumerate((a, w)):
                        for tt in range(TT):
                            act.activation(y[:, tt, :], y[:, tt, :], ACT.Copy, scale=qi[:, i, tt:tt + 1], bias=MAGIC)\
                                .then_inc(y_act.sem, 1)
                    for i, (ps_ready, dst, ready) in enumerate(((aq_ps, aT_bf, aqT), (wq_ps, wT_bf, wqT))):
                        ps = slots_bf[use[0] % 3]
                        use[0] += 1
                        act.wait_ge(ps_ready.sem, ps_ready.at(b, n + 1))
                        act.activation(dst[:, 0:nk, :], ps[:, 0:(nk + 1) // 2, :].rearrange("p a (c t) -> p (a c) t", c=2),
                                       ACT.Copy).then_inc(ready.sem, 1)
                    act.wait_ge(wrow_ps.sem, wrow_ps.at(b, n + 1))
                    act.activation(wrow[:, :], slot()[:, 0, :], ACT.Copy).then_inc(wrow_ready.sem, 1)
                    use[0] += 2
                act.wait_ge(x2_ready.sem, x2_ready.at(b, TT))
                act.dma_start(x2[b].rearrange("(a p) d -> p a d", p=P), hid[:, :, :]).then_inc(x2_stored.sem, 16)

            batch(0, True)
            with act.Fori(1, BATCH) as b:
                batch(b, False)

        @block.tensor
        def _(pe):
            tenants = Tenants(3)
            pe.wait_ge(c_loaded.sem, 64)
            pe.wait_ge(masks_ready.sem, 1)
            pe.wait_ge(consts_ready.sem, 6)

            def three(out, w_hi, w_lo, m_hi_, m_lo_, start, stop):
                pe.matmul(out, w_hi, m_hi_, start=start, stop=False)
                pe.matmul(out, w_hi, m_lo_, start=False, stop=False)
                return pe.matmul(out, w_lo, m_hi_, start=False, stop=stop)

            def batch(b, first):
                tenants.new_batch(first)
                for s in range(2):
                    ps = slots[tenants.claim(pe, b, xT_lo, s + 1)]
                    for j in range(2):
                        for tt in range(TT):
                            if s == 0 and j == 0:
                                pe.wait_ge(xn_ready.sem, xn_ready.at(b, tt + 1))
                            k = 2 * s + j
                            mm = pe.transpose(ps[:, j, tt * P:(tt + 1) * P], xn[:, tt, k * P:(k + 1) * P], ident)
                    mm.then_inc(xT_ps.sem, 1)
                if first:
                    pe.wait_ge(halves_ready.sem, 8)
                    pe.wait_ge(w_used.sem, 8)
                ps = slots[tenants.claim(pe, b, kv_lo, 1)]
                for k in range(KT):
                    if k % 2 == 0:
                        pe.wait_ge(xT_lo.sem, xT_lo.at(b, k // 2 + 1))
                    mm = three(ps[0:2 * HD, 0, :], wqkv_h[:, k, D:QKV], wqkv_l[:, k, D:QKV], hT_h[:, k, :], hT_l[:, k, :],
                               k == 0, k == KT - 1)
                mm.then_inc(kv_ps.sem, 1)
                for ep in range(2):
                    ps = slots[tenants.claim(pe, b, q_lo, 2 * ep + 2)]
                    for j in range(2):
                        e = 2 * ep + j
                        for k in range(KT):
                            mm = three(ps[:, j, :], wqkv_h[:, k, e * P:(e + 1) * P], wqkv_l[:, k, e * P:(e + 1) * P],
                                       hT_h[:, k, :], hT_l[:, k, :], k == 0, k == KT - 1)
                        mm.then_inc(q_ps.sem, 1)
                ps = slots[tenants.claim(pe, b, v_ready, 1)]
                pe.wait_ge(kv_act.sem, kv_act.at(b, 3))
                separate(pe, passed[1])
                for kt in range(TT):
                    mm = pe.transpose(ps[:, 0, kt * HD:(kt + 1) * HD], vT[HD:2 * HD, kt * P:(kt + 1) * P],
                                      cst[HD:2 * HD, 0, HD:2 * HD])
                mm.then_inc(v_ps.sem, 1)
                pe.wait_ge(kv_lo.sem, kv_lo.at(b, 1))
                group = 0
                for hf in range(2):
                    pe.wait_ge(q_moved[hf].sem, q_moved[hf].at(b, q_moved[hf].per))
                    for qt in range(TT):
                        n = (qt + 1) * P
                        per_bank = T // n if qt != 2 else 1
                        for h0 in range(8 * hf, 8 * hf + 8, 2 * per_bank):
                            group += 1
                            ps = slots[tenants.claim(pe, b, s_max, group)]
                            for i in range(2 * per_bank):
                                bank, c = i // per_bank, i % per_bank
                                pe.matmul(ps[:, bank, (c + 1) * n - P:(c + 1) * n], mask_bf[:, 0, :],
                                          mask_bf[:, 1, :], start=True, stop=False, skip_group_check=True)
                                mm = pe.matmul(ps[:, bank, c * n:(c + 1) * n], qst[0:KROWS, h0 + i, qt * P:(qt + 1) * P],
                                               kst[0:KROWS, 0:n], start=False, stop=True, skip_group_check=True)
                            mm.then_inc(s_ps.sem, 1)
                    ps = slots[tenants.claim(pe, b, m_lo, hf + 1)]
                    pe.wait_ge(s_max.sem, s_max.at(b, 11 * hf + 11))
                    pe.transpose(ps[0:HD, 0, 0:P], negm[:, 8 * hf:8 * hf + 8, :].rearrange("p h q -> p (h q)"), ident)\
                        .then_inc(m_ps.sem, 1)

                def scores(g, kt, step):
                    n = T - kt * P
                    for pr in range(2):
                        ps = slots[tenants.claim(pe, b, p_ready, 2 * step + pr + 1)]
                        for j in range(2):
                            pe.matmul(ps[:, j, 0:P], mask_bf[:, 0, :], mask_bf[:, 2, :], start=True, stop=False,
                                      skip_group_check=True)
                            mm = pe.matmul(ps[:, j, 0:n], kst[0:KROWS + 2, kt * P:(kt + 1) * P],
                                           qst[0:KROWS + 2, 4 * g + 2 * pr + j, kt * P:T], start=False, stop=True,
                                           skip_group_check=True)
                        mm.then_inc(t_ps.sem, 1)

                def values(g, kt, step):
                    n = T - kt * P
                    pe.wait_ge(p_ready.sem, p_ready.at(b, 2 * step + 2))
                    if kt == TT - 1 and g:
                        pe.wait_ge(cx_ready.sem, cx_ready.at(b, g))
                    for out, weights in ((av, v[:, kt, :]), (den, ones[:, :])):
                        for c in range(4):
                            mm = pe.matmul(out[HD * c:HD * c + HD, kt * P:T], weights,
                                           probs[:, 2 * (step % 2) + c // 2, c % 2, 0:n], start=(kt == TT - 1),
                                           stop=(kt == 0), skip_group_check=True)
                    mm.then_inc(pv_done.sem, 1)

                pe.wait_ge(v_ready.sem, v_ready.at(b, 1))
                if not first:
                    pe.wait_ge(cx_ready.sem, cx_ready.at(b - 1, 4))
                steps = [(g, kt) for g in range(4) for kt in reversed(range(TT))]
                for step, (g, kt) in enumerate(steps):
                    if kt == TT - 1 and g % 2 == 0:
                        pe.wait_ge(m_moved[g // 2].sem, m_moved[g // 2].at(b, 32))
                    scores(g, kt, step)
                    if step:
                        values(*steps[step - 1], step - 1)
                values(*steps[-1], len(steps) - 1)
                for s in range(2):
                    ps = slots[tenants.claim(pe, b, x1_ready, s + 1)]
                    for j in range(2):
                        tt = 2 * s + j
                        for g in range(4):
                            if tt == 0:
                                pe.wait_ge(cx_lo.sem, cx_lo.at(b, g + 1))
                            mm = three(ps[:, j, :], hT_h[:, g, tt * P:(tt + 1) * P], hT_l[:, g, tt * P:(tt + 1) * P],
                                       wo_h[:, g, :], wo_l[:, g, :], g == 0, g == 3)
                    mm.then_inc(o_ps.sem, 1)
                for s in range(2):
                    ps = slots[tenants.claim(pe, b, colmax, s + 1)]
                    for j in range(2):
                        for tt in range(TT):
                            if s == 0 and j == 0:
                                pe.wait_ge(xn_ready.sem, xn_ready.at(b, TT + tt + 1))
                            k = 2 * s + j
                            mm = pe.transpose(ps[:, j, tt * P:(tt + 1) * P], xn[:, tt, k * P:(k + 1) * P], ident)
                    mm.then_inc(xT_ps.sem, 1)
                for n, nk in enumerate((KT, IT)):
                    if n:
                        ps = slots[tenants.claim(pe, b, colmax, 3)]
                        pe.wait_ge(act_ready.sem, act_ready.at(b, 1))
                        for k in range(IT):
                            for tt in range(TT):
                                mm = pe.transpose(ps[:, k, tt * P:(tt + 1) * P], hid[:, tt, k * P:(k + 1) * P], ident)
                        mm.then_inc(aT_ps.sem, 1)
                    ps = slots[tenants.claim(pe, b, s_rows, n + 1)]
                    pe.wait_ge(s_cols.sem, s_cols.at(b, n + 1))
                    for i in range(2):
                        for k in range(nk):
                            mm = pe.transpose(ps[:, i, k * P:(k + 1) * P],
                                              sc[:, 3 + i, k:k + 1].to_broadcast([P, P]), ident)
                    mm.then_inc(s_rows_ps.sem, 1)
                    for src, quantised, signal, freed in ((a_bf, a_q, aq_ps, aqT), (w_bf, w_q, wq_ps, wqT)):
                        ps = slots_bf[tenants.claim(pe, b, freed, n + 1)]
                        pe.wait_ge(quantised.sem, quantised.at(b, n + 1))
                        for k in range(nk):
                            for tt in range(TT):
                                at = (k % 2) * T + tt * P
                                mm = pe.transpose(ps[:, k // 2, at:at + P], src[:, tt, k * P:(k + 1) * P], mask_bf[:, 0, :])
                        mm.then_inc(signal.sem, 1)
                    ps = slots[tenants.claim(pe, b, wrow_ready, n + 1)]
                    for ot in range(TT):
                        mm = pe.transpose(ps[:, 0, ot * P:(ot + 1) * P], qs[:, 1, ot:ot + 1].to_broadcast([P, P]), ident)
                    mm.then_inc(wrow_ps.sem, 1)
                    pe.wait_ge(aqT.sem, aqT.at(b, n + 1))
                    pe.wait_ge(wqT.sem, wqT.at(b, n + 1))
                    for s in range(2):
                        ps = slots[tenants.claim(pe, b, h_ready, TT * n + 2 * s + 2)]
                        for j in range(2):
                            tt = 2 * s + j
                            for k in range(nk):
                                mm = pe.matmul(ps[:, j, :], aT_bf[:, k, tt * P:(tt + 1) * P], wT_bf[:, k, :],
                                               start=(k == 0), stop=(k == nk - 1))
                        mm.then_inc(h_ps.sem, 1)

            batch(0, True)
            with pe.Fori(1, BATCH) as b:
                batch(b, False)

        @block.vector
        def _(dve):
            dve.wait_ge(c_loaded.sem, 64)

            def batch(b, first):
                link = Link(dve, dve_link, b)
                use = [0]

                def slot():
                    use[0] += 1
                    return slots[(use[0] - 1) % 3]

                def layernorm(src, n):
                    for tt in range(TT):
                        ins = dve.bn_stats(stats[:, tt, :], src[:, tt, :])
                    link(ins)
                    separate(dve, passed[2])
                    for tt in range(TT):
                        ins = dve.bn_aggr(mv[:, tt, :], stats[:, tt, :])
                    ins.then_inc(ln_stats.sem, 1)
                    dve.wait_ge(ln_stats.sem, ln_stats.at(b, n + 1))
                    dve.wait_ge(rstd_ready.sem, rstd_ready.at(b, n + 1))
                    for tt in range(TT):
                        dve.tensor_scalar(xn[:, tt, :], src[:, tt, :], mv[:, tt, 0:1], rstd[:, tt:tt + 1],
                                          ALU.subtract, ALU.mult).then_inc(xn_ready.sem, 1)

                dve.wait_ge(x_loaded.sem, x_loaded.at(b, 16))
                layernorm(x_in, 0)
                for s in range(2):
                    dve.wait_ge(xT_hi.sem, xT_hi.at(b, s + 1))
                    dve.tensor_tensor(hT_l[:, 2 * s:2 * s + 2, :], slot()[:, :, :],
                                      hT_h[:, 2 * s:2 * s + 2, :].bitcast(F32), ALU.subtract).then_inc(xT_lo.sem, 1)
                dve.wait_ge(kv_act.sem, kv_act.at(b, 3))
                dve.scalar_tensor_tensor(kst[2 * HD:KROWS, :], slot()[0:HD, 0, :], bkv_sb[0:HD, :],
                                         kst[0:HD, :].bitcast(F32), ALU.add, ALU.subtract).then_inc(kv_lo.sem, 1)
                for e in range(KT):
                    if e % 2 == 0:
                        ps = slot()
                    dve.wait_ge(q_hi.sem, q_hi.at(b, e + 1))
                    dve.scalar_tensor_tensor(qT_l[:, e, :], ps[:, e % 2, :], bq_sb[:, e:e + 1],
                                             qT_h[:, e, :].bitcast(F32), ALU.add, ALU.subtract).then_inc(q_lo.sem, 1)
                dve.wait_ge(v_ps.sem, v_ps.at(b, 1))
                dve.tensor_copy(v[:, :, :], slot()[:, 0, 0:TT * HD].rearrange("p (a d) -> p a d", d=HD))\
                    .then_inc(v_ready.sem, 1)
                group = 0
                for hf in range(2):
                    for qt in range(TT):
                        n = (qt + 1) * P
                        per_bank = T // n if qt != 2 else 1
                        for h0 in range(8 * hf, 8 * hf + 8, 2 * per_bank):
                            group += 1
                            dve.wait_ge(s_ps.sem, s_ps.at(b, group))
                            dve.tensor_reduce(negm[:, h0:h0 + 2 * per_bank, qt].rearrange("p (a c) -> p a c", a=2),
                                              slot()[:, :, 0:per_bank * n].rearrange("p a (c n) -> p a c n", n=n),
                                              AX.X, ALU.max, negate=True).then_inc(s_max.sem, 1)
                    dve.wait_ge(m_hi.sem, m_hi.at(b, hf + 1))
                    dve.tensor_tensor(negm_l[:, hf, :], slot()[0:HD, 0, 0:P], negm_h[:, hf, :].bitcast(F32),
                                      ALU.subtract).then_inc(m_lo.sem, 1)
                use[0] += 32
                for g in range(4):
                    dve.wait_ge(pv_done.sem, pv_done.at(b, 4 * g + 4))
                    dve.reciprocal(rden[:, :], den[:, :]).then_inc(rden_ready.sem, 1)
                    dve.wait_ge(rden_ready.sem, rden_ready.at(b, g + 1))
                    if g >= 2:
                        dve.wait_ge(cx_lo.sem, cx_lo.at(b, g - 1))
                    dve.tensor_tensor(cx[:, g % 2, :], av[:, :], rden[:, :], ALU.mult).then_inc(cx_ready.sem, 1)
                dve.wait_ge(xb_ready.sem, xb_ready.at(b, 1))
                if not first:
                    dve.wait_ge(x2_ready.sem, x2_ready.at(b - 1, TT))
                for s in range(2):
                    dve.wait_ge(o_ps.sem, o_ps.at(b, s + 1))
                    dve.tensor_tensor(x1[:, 2 * s:2 * s + 2, :], slot()[:, :, :], x_in[:, 2 * s:2 * s + 2, :], ALU.add)\
                        .then_inc(x1_ready.sem, 1)
                dve.wait_ge(x1_ready.sem, x1_ready.at(b, 2))
                layernorm(x1, 1)
                for s in range(2):
                    dve.wait_ge(xT_ps.sem, xT_ps.at(b, 2 + s + 1))
                    dve.tensor_reduce(amax[:, 0, 2 * s:2 * s + 2], slot()[:, :, :], AX.X, ALU.max,
                                      apply_absolute_value=True).then_inc(colmax.sem, 1)

                for n, (nk, width, a, w, wT, wT_ok) in enumerate(((KT, D, xn, w_raw, wT_raw, mwT_loaded),
                                                                  (IT, INNER, hid[:, :, 0:INNER], d_raw, dT_raw, mdT_loaded))):
                    if n:
                        dve.wait_ge(th_ready.sem, th_ready.at(b, 1))
                        link(dve.scalar_tensor_tensor(th[:, :, :], th[:, :, :], 1.0, a, ALU.add, ALU.mult))
                        dve.scalar_tensor_tensor(a, th[:, :, :], 0.5, hid[:, :, INNER:D], ALU.mult, ALU.mult)\
                            .then_inc(act_ready.sem, 1)
                        dve.wait_ge(aT_ps.sem, aT_ps.at(b, 1))
                        dve.tensor_reduce(amax[:, 0, 0:IT], slot()[:, :, :], AX.X, ALU.max,
                                          apply_absolute_value=True).then_inc(colmax.sem, 1)
                    dve.wait_ge(wT_ok.sem, wT_ok.at(b, 16))
                    link(dve.tensor_reduce(amax[:, 1, 0:nk], wT[:, :, :], AX.X, ALU.max, apply_absolute_value=True))
                    dve.wait_ge(colmax.sem, colmax.at(b, 2 + n))
                    link(dve.tensor_scalar(amax[:, :, 0:nk], amax[:, :, 0:nk], QEPS, None, ALU.max))
                    link(dve.reciprocal(sc[:, 0, 0:nk], amax[:, 1, 0:nk]))
                    dve.tensor_tensor(sc[:, 1, 0:nk], amax[:, 0, 0:nk], sc[:, 0, 0:nk], ALU.mult).then_inc(ratio.sem, 1)
                    dve.wait_ge(root.sem, root.at(b, n + 1))
                    link(dve.tensor_scalar(sc[:, 3, 0:nk], sc[:, 2, 0:nk], QEPS, None, ALU.max))
                    dve.reciprocal(sc[:, 4, 0:nk], sc[:, 3, 0:nk]).then_inc(s_cols.sem, 1)
                    dve.wait_ge(s_rows.sem, s_rows.at(b, n + 1))
                    use[0] += 1
                    link(dve.tensor_tensor(a[:, :, :], a[:, :, :],
                                           rows[:, 1, 0:width].unsqueeze(1).to_broadcast([P, TT, width]), ALU.mult))
                    dve.tensor_reduce(qm[:, 0, :], a[:, :, :], AX.X, ALU.max, apply_absolute_value=True)
                    dve.wait_ge(w_scaled.sem, w_scaled.at(b, n + 1))
                    link(dve.tensor_reduce(qm[:, 1, :], w[:, :, :], AX.X, ALU.max, apply_absolute_value=True))
                    link(dve.tensor_scalar(qs[:, :, :], qm[:, :, :], QEPS, 1.0 / QMAX, ALU.max, ALU.mult))
                    dve.reciprocal(qi[:, :, :], qs[:, :, :]).then_inc(q_scale.sem, 1)
                    dve.wait_ge(y_act.sem, y_act.at(b, 8 * n + 4))
                    dve.tensor_scalar(a_bf[:, :, 0:width], a[:, :, :], MAGIC, None, ALU.subtract).then_inc(a_q.sem, 1)
                    use[0] += 3
                    dve.wait_ge(wrow_ready.sem, wrow_ready.at(b, n + 1))
                    for s in range(2):
                        ps = slot()
                        dve.wait_ge(h_ps.sem, h_ps.at(b, 2 * n + s + 1))
                        for j in range(2):
                            tt = 2 * s + j
                            if n == 0 and s == 0 and j == 0 and not first:
                                dve.wait_ge(x2_stored.sem, x2_stored.at(b - 1, 16))
                            dve.scalar_tensor_tensor(hid[:, tt, :], ps[:, j, :], qs[:, 0, tt:tt + 1], wrow[:, :],
                                                     ALU.mult, ALU.mult).then_inc(h_ready.sem, 1)
                link.done()

            batch(0, True)
            with dve.Fori(1, BATCH) as b:
                batch(b, False)


def feed_forward(nc, x2, wg, wu, wd, ga, ua, da, gb, ub, db, expert_bias, consts, out):
    with ExitStack() as ctx:
        def sb(name, shape, dt=F32):
            return ctx.enter_context(nc.sbuf_tensor(name, shape, dt))

        def sig(name, per=1):
            return Signal(ctx, nc, name, per)

        cst = sb("f_cst", [P, 4, P])
        ident, lower = cst[:, 0, :], cst[:, 3, 0:EXPERTS * EXPERTS]
        half, ln_eps = sb("f_half", [P, TT]), sb("f_ln_eps", [P, TT])
        bias_bc = sb("bias_bc", [P, EXPERTS])
        wg_sb, wu_sb, wd_sb = sb("wg_sb", [P, KT, DFF]), sb("wu_sb", [P, KT, DFF]), sb("wd_sb", [P, FT, D])
        g_h, g_l = sb("g_h", [P, 2, KT, P], F32R), sb("g_l", [P, 2, KT, P], F32R)
        u_h, u_l = sb("u_h", [P, 2, KT, P], F32R), sb("u_l", [P, 2, KT, P], F32R)
        d_h, d_l = sb("d_h", [P, 2, D], F32R), sb("d_l", [P, 2, D], F32R)
        ga_h, ga_l = sb("ga_h", [P, KT, LA], F32R), sb("ga_l", [P, KT, LA], F32R)
        ua_h, ua_l = sb("ua_h", [P, KT, LR], F32R), sb("ua_l", [P, KT, LR], F32R)
        da_h, da_l = sb("da_h", [P, FT, LR], F32R), sb("da_l", [P, FT, LR], F32R)
        gb_h, gb_l = sb("gb_h", [LR, DFF], F32R), sb("gb_l", [LR, DFF], F32R)
        ub_h, ub_l = sb("ub_h", [LR, DFF], F32R), sb("ub_l", [LR, DFF], F32R)
        db_h, db_l = sb("db_h", [LR, D], F32R), sb("db_l", [LR, D], F32R)
        x2_in, x2_res = sb("x2_in", [P, TT, D]), sb("x2_res", [P, TT, D])
        stats, mv = sb("f_stats", [P, TT, 6]), sb("f_mv", [P, TT, 2])
        veps, rstd = sb("f_veps", [P, TT]), sb("f_rstd", [P, TT])
        xT_h, xT_l = sb("xT_h", [P, KT, T], F32R), sb("xT_l", [P, KT, T], F32R)
        a_gate, a_up = sb("a_gate", [LA, T]), sb("a_up", [LR, T])
        prob = sb("prob", [P, TT, EXPERTS])
        biased = sb("biased", [P, TT, EXPERTS])
        beats, ties = sb("beats", [P, TT, EXPERTS, EXPERTS]), sb("ties", [P, TT, EXPERTS, EXPERTS])
        rank, wsum = sb("rank", [P, TT, EXPERTS]), sb("wsum", [P, 2, TT])
        wx, wxT = sb("wx", [P, TT, LR]), sb("wxT", [LR, T])
        y = sb("y", [LR, T])
        yg_h, yg_l = sb("yg_h", [LR, T], F32R), sb("yg_l", [LR, T], F32R)
        yu_h, yu_l = sb("yu_h", [LR, T], F32R), sb("yu_l", [LR, T], F32R)
        work = sb("work", [P, 3, T])
        th, gated, hd = work[:, 0, :], work[:, 1, :], work[:, 2, :]
        hd_h, hd_l = sb("hd_h", [P, 2, T], F32R), sb("hd_l", [P, 2, T], F32R)

        ring = [ctx.enter_context(nc.psum_tensor(f"ring{i}", [P, T], F32)) for i in range(3)]
        down = ctx.enter_context(nc.psum_tensor("down", [P, TT, D], F32))
        adps = ctx.enter_context(nc.psum_tensor("adps", [P, T], F32))

        f_c = sig("f_c")
        ff_loaded = [sig(f"ff_loaded{c}") for c in range(3)]
        lora_loaded, lora_hi, lora_lo = [sig(f"lora_loaded{n}") for n in range(7)], sig("lora_hi"), sig("lora_lo")
        f_consts = sig("f_consts")
        x2_loaded, res_loaded, stored = sig("x2_loaded", 16), sig("res_loaded", 16), sig("stored", 16)
        ln_stats, rstd_ready, xn_ready = sig("f_ln_stats"), sig("f_rstd_ready"), sig("f_xn_ready", TT)
        xT_ps, xT_hi, xT_lo = sig("f_xT_ps", KT), sig("f_xT_hi", KT), sig("f_xT_lo", KT)
        a_ps, a_copied = sig("a_ps", 2), sig("a_copied", 2)
        logits_ps, prob_tanh, wx_ready, wx_ps, wxT_ready = (sig("logits_ps"), sig("prob_tanh"), sig("wx_ready"),
                                                            sig("wx_ps"), sig("wxT_ready"))
        y_ready, y_hi, y_lo = sig("y_ready", 3), sig("y_hi", 3), sig("y_lo", 3)
        gu_hi, gu_lo = sig("gu_hi", 2 * FT), sig("gu_lo", 2 * FT)
        d_hi, d_lo = sig("d_hi", FT), sig("d_lo", FT)
        g_ps, u_ps = sig("g_ps", FT), sig("u_ps", FT)
        tanh_done, gated_done, hd_ready = sig("tanh_done", FT), sig("gated_done", FT), sig("hd_ready", FT)
        hd_hi, hd_lo = sig("hd_hi", FT), sig("hd_lo", FT)
        tile_done = sig("tile_done", FT)
        out_ps, out_ready = sig("out_ps", TT), sig("out_ready", TT)
        dve_link, pool_link = sig("f_dve_link", FF_DVE_LINKS), sig("f_pool_link", 1)
        passed = [sig(f"f_passed_{e}") for e in ("pool", "pe", "dve")]

        ga_end, ua_end, da_end = KT * LA, KT * (LA + LR), KT * (LA + LR) + FT * LR
        res_flat, work_flat = (t[:, :, :].rearrange("p a d -> p (a d)") for t in (x2_res, work))
        last = da_end - LR
        lora = [(ga.rearrange("(k p) n -> p k n", p=P), res_flat[:, 0:ga_end].rearrange("p (k n) -> p k n", k=KT),
                 ga_h[:, :, :], ga_l[:, :, :]),
                (ua.rearrange("(k p) n -> p k n", p=P), res_flat[:, ga_end:ua_end].rearrange("p (k n) -> p k n", k=KT),
                 ua_h[:, :, :], ua_l[:, :, :]),
                (gb, work_flat[0:LR, 0:DFF], gb_h[:, :], gb_l[:, :]),
                (da[0:(FT - 1) * P, :].rearrange("(f p) n -> p f n", p=P),
                 res_flat[:, ua_end:last].rearrange("p (f n) -> p f n", n=LR), da_h[:, 0:FT - 1, :], da_l[:, 0:FT - 1, :]),
                (da[(FT - 1) * P:DFF, :], res_flat[0:FLAST, last:da_end], da_h[0:FLAST, FT - 1, :], da_l[0:FLAST, FT - 1, :]),
                (db, res_flat[0:LR, da_end:da_end + D], db_h[:, :], db_l[:, :]),
                (ub, work_flat[0:LR, 0:DFF], ub_h[:, :], ub_l[:, :])]
        GB, UB = 2, len(lora) - 1

        def weight_parts(f):
            m, at, s = f_rows(f), f * P, f % 2
            return ((wg_sb[:, :, at:at + m], g_h[:, s, :, 0:m], g_l[:, s, :, 0:m]),
                    (wu_sb[:, :, at:at + m], u_h[:, s, :, 0:m], u_l[:, s, :, 0:m]),
                    (wd_sb[0:m, f, :], d_h[0:m, s, :], d_l[0:m, s, :]))

        block = ctx.enter_context(nc.Block())

        @block.sync
        def _(sp):
            sp.dma_start(x2_in[:, :, :], x2[0].rearrange("(a p) d -> p a d", p=P)).then_inc(x2_loaded.sem, 16)
            sp.dma_start(cst[:, :, :], consts).then_inc(f_c.sem, 16)
            sp.dma_start(bias_bc[:, :], expert_bias.partition_broadcast(P)).then_inc(f_c.sem, 16)
            for n, (src, raw, _, _) in enumerate(lora):
                if n == UB:
                    sp.wait_ge(lora_lo.sem, GB + 1)
                sp.dma_start(raw, src).then_inc(lora_loaded[n].sem, 16)

            def batch(b, first):
                if not first:
                    sp.wait_ge(xn_ready.sem, xn_ready.at(b - 1, TT))
                    sp.wait_ge(xT_ps.sem, xT_ps.at(b - 1, KT))
                    sp.dma_start(x2_in[:, :, :], x2[b].rearrange("(a p) d -> p a d", p=P)).then_inc(x2_loaded.sem, 16)
                if first:
                    sp.wait_ge(lora_lo.sem, len(lora))
                else:
                    sp.wait_ge(stored.sem, stored.at(b - 1, 16))
                sp.dma_start(x2_res[:, :, :], x2[b].rearrange("(a p) d -> p a d", p=P)).then_inc(res_loaded.sem, 16)
                sp.wait_ge(out_ready.sem, out_ready.at(b, TT))
                sp.dma_start(out[b].rearrange("(a p) d -> p a d", p=P), x2_res[:, :, :]).then_inc(stored.sem, 16)

            batch(0, True)
            with sp.Fori(1, BATCH) as b:
                batch(b, False)
            sp.wait_ge(stored.sem, 16 * BATCH)

        @block.gpsimd
        def _(pool):
            for n, (dst, value) in enumerate(((half[:, :], -0.5), (wx[:, :, ER:LR], 1.0 / RANK),
                                              (ln_eps[:, :], LN_EPS))):
                pool.memset(dst, value).then_inc(f_consts.sem, 1)
                pool.wait_ge(f_consts.sem, n + 1)

            def batch(b, first):
                link = Link(pool, pool_link, b)
                pool.wait_ge(ln_stats.sem, ln_stats.at(b, 1))
                link(pool.tensor_tensor(veps[:, :], mv[:, :, 1], ln_eps[:, :], ALU.add))
                pool.tensor_tensor(rstd[:, :], veps[:, :], half[:, :], ALU.pow).then_inc(rstd_ready.sem, 1)

                def split_gate_up(f):
                    for i, (w, hi, lo) in enumerate(weight_parts(f)[0:2]):
                        pool.wait_ge(gu_hi.sem, gu_hi.at(b, 2 * f + i + 1))
                        pool.tensor_tensor(lo, w, hi.bitcast(F32), ALU.subtract).then_inc(gu_lo.sem, 1)

                def split_down(f):
                    w, hi, lo = weight_parts(f)[2]
                    pool.wait_ge(d_hi.sem, d_hi.at(b, f + 1))
                    pool.tensor_tensor(lo, w, hi.bitcast(F32), ALU.subtract).then_inc(d_lo.sem, 1)

                split_gate_up(0)
                split_gate_up(1)
                split_down(0)
                for f in range(FT):
                    if f + 2 < FT:
                        split_gate_up(f + 2)
                    pool.wait_ge(hd_hi.sem, hd_hi.at(b, f + 1))
                    m = f_rows(f)
                    pool.tensor_tensor(hd_l[0:m, f % 2, :], hd[0:m, :], hd_h[0:m, f % 2, :].bitcast(F32), ALU.subtract)\
                        .then_inc(hd_lo.sem, 1)
                    if f + 1 < FT:
                        split_down(f + 1)
                link.done()

            batch(0, True)
            with pool.Fori(1, BATCH) as b:
                batch(b, False)

        @block.scalar
        def _(act):
            for c in range(3):
                cols = slice(4 * P * c, min(4 * P * (c + 1), DFF))
                act.dma_start(wg_sb[:, :, cols], wg[:, :, cols]).then_inc(ff_loaded[c].sem, 16)
                act.dma_start(wu_sb[:, :, cols], wu[:, :, cols]).then_inc(ff_loaded[c].sem, 16)
                full = min(4 * (c + 1), FT - 1)
                act.dma_start(wd_sb[:, 4 * c:full, :], wd[4 * c * P:full * P, :].rearrange("(f p) d -> p f d", p=P))\
                   .then_inc(ff_loaded[c].sem, 16)
            act.dma_start(wd_sb[0:FLAST, FT - 1, :], wd[(FT - 1) * P:DFF, :]).then_inc(ff_loaded[2].sem, 16)
            for n, (_, raw, hi, _) in enumerate(lora):
                act.wait_ge(lora_loaded[n].sem, 16)
                act.activation(hi, raw, ACT.Copy).then_inc(lora_hi.sem, 1)

            def batch(b, first):
                def split(f, i):
                    w, hi, _ = weight_parts(f)[i]
                    done, ready = ((g_ps, gu_hi), (u_ps, gu_hi), (tile_done, d_hi))[i]
                    if f >= 2:
                        act.wait_ge(done.sem, done.at(b, f - 1))
                    elif not first:
                        act.wait_ge(done.sem, done.at(b - 1, FT - (FT - 1 - f) % 2))
                    if first:
                        act.wait_ge(ff_loaded[f // 4].sem, 64 if f >= 8 else 48)
                    act.activation(hi, w, ACT.Copy).then_inc(ready.sem, 1)

                for f, i in ((0, 0), (0, 1), (1, 0), (1, 1), (0, 2)):
                    split(f, i)
                for k in range(KT):
                    act.wait_ge(xT_ps.sem, xT_ps.at(b, k + 1))
                    act.activation(xT_h[:, k, :], ring[k % 3][:, :], ACT.Copy).then_inc(xT_hi.sem, 1)
                act.wait_ge(a_ps.sem, a_ps.at(b, 1))
                act.activation(a_gate[:, :], ring[KT % 3][0:LA, :], ACT.Copy).then_inc(a_copied.sem, 1)
                act.wait_ge(a_ps.sem, a_ps.at(b, 2))
                act.activation(a_up[:, :], ring[(KT + 1) % 3][0:LR, :], ACT.Copy).then_inc(a_copied.sem, 1)
                act.wait_ge(logits_ps.sem, logits_ps.at(b, 1))
                act.activation(prob[:, :, :], adps[:, 0:TT * EXPERTS].rearrange("p (a e) -> p a e", e=EXPERTS),
                               ACT.Tanh, scale=0.5).then_inc(prob_tanh.sem, 1)
                act.wait_ge(wx_ps.sem, wx_ps.at(b, 1))
                act.activation(wxT[:, :], adps[0:LR, :], ACT.Copy).then_inc(wxT_ready.sem, 1)
                for n, hi in enumerate((yg_h, yu_h)):
                    act.wait_ge(y_ready.sem, y_ready.at(b, n + 1))
                    act.activation(hi[:, :], y[:, :], ACT.Copy).then_inc(y_hi.sem, 1)
                for f in range(FT):
                    m = f_rows(f)
                    act.wait_ge(g_ps.sem, g_ps.at(b, f + 1))
                    if f:
                        act.wait_ge(gated_done.sem, gated_done.at(b, f))
                    act.activation(th[0:m, :], ring[(KT + 2 + 2 * f) % 3][0:m, :], ACT.Tanh, scale=0.5)\
                        .then_inc(tanh_done.sem, 1)
                    if f + 2 < FT:
                        split(f + 2, 0)
                        split(f + 2, 1)
                    act.wait_ge(hd_ready.sem, hd_ready.at(b, f + 1))
                    if f >= 2:
                        act.wait_ge(tile_done.sem, tile_done.at(b, f - 1))
                    act.activation(hd_h[0:m, f % 2, :], hd[0:m, :], ACT.Copy).then_inc(hd_hi.sem, 1)
                    if f + 1 < FT:
                        split(f + 1, 2)
                act.wait_ge(y_ready.sem, y_ready.at(b, 3))
                act.activation(yg_h[:, :], y[:, :], ACT.Copy).then_inc(y_hi.sem, 1)

            batch(0, True)
            with act.Fori(1, BATCH) as b:
                batch(b, False)

        @block.tensor
        def _(pe):
            tenants = Tenants(3)
            pe.wait_ge(f_c.sem, 32)

            def three(out_, w_hi, w_lo, m_hi, m_lo, start, stop):
                pe.matmul(out_, w_hi, m_hi, start=start, stop=False, skip_group_check=True)
                pe.matmul(out_, w_hi, m_lo, start=False, stop=False, skip_group_check=True)
                return pe.matmul(out_, w_lo, m_hi, start=False, stop=stop, skip_group_check=True)

            def batch(b, first):
                tenants.new_batch(first)
                for k in range(KT):
                    ps = ring[tenants.claim(pe, b, xT_lo, k + 1)]
                    for tt in range(TT):
                        if k == 0:
                            pe.wait_ge(xn_ready.sem, xn_ready.at(b, tt + 1))
                        mm = pe.transpose(ps[:, tt * P:(tt + 1) * P], x2_in[:, tt, k * P:(k + 1) * P], ident)
                    mm.then_inc(xT_ps.sem, 1)
                if first:
                    pe.wait_ge(lora_lo.sem, len(lora))
                for n, (hi, lo, width) in enumerate(((ga_h, ga_l, LA), (ua_h, ua_l, LR))):
                    ps = ring[tenants.claim(pe, b, a_copied, n + 1)]
                    for k in range(KT):
                        pe.wait_ge(xT_lo.sem, xT_lo.at(b, k + 1))
                        mm = three(ps[0:width, :], hi[:, k, :], lo[:, k, :], xT_h[:, k, :], xT_l[:, k, :],
                                   k == 0, k == KT - 1)
                    mm.then_inc(a_ps.sem, 1)
                pe.wait_ge(a_copied.sem, a_copied.at(b, 1))
                if not first:
                    pe.wait_ge(y_ready.sem, y_ready.at(b - 1, 3))
                separate(pe, passed[1])
                for tt in range(TT):
                    mm = pe.transpose(adps[:, tt * EXPERTS:(tt + 1) * EXPERTS], a_gate[ROUTE:LA, tt * P:(tt + 1) * P],
                                      cst[ROUTE:LA, 0, ROUTE:LA])
                mm.then_inc(logits_ps.sem, 1)

                held = {}

                def base(side, f):
                    m = f_rows(f)
                    hi, lo, freed = ((g_h, g_l, gated_done), (u_h, u_l, hd_ready))[side]
                    ps = held[side, f] = ring[tenants.claim(pe, b, freed, f + 1)]
                    pe.wait_ge(gu_lo.sem, gu_lo.at(b, 2 * f + side + 1))
                    for k in range(KT):
                        three(ps[0:m, :], hi[:, f % 2, k, 0:m], lo[:, f % 2, k, 0:m], xT_h[:, k, :], xT_l[:, k, :],
                              k == 0, False)

                def low_rank(side, f):
                    m = f_rows(f)
                    hi, lo, yh, yl, ready = ((gb_h, gb_l, yg_h, yg_l, g_ps), (ub_h, ub_l, yu_h, yu_l, u_ps))[side]
                    cols = slice(f * P, f * P + m)
                    if f == 0:
                        pe.wait_ge(y_lo.sem, y_lo.at(b, side + 1))
                    three(held[side, f][0:m, :], hi[:, cols], lo[:, cols], yh[:, :], yl[:, :], False, True)\
                        .then_inc(ready.sem, 1)

                def project(f):
                    m, s = f_rows(f), f % 2
                    pe.wait_ge(hd_lo.sem, hd_lo.at(b, f + 1))
                    pe.wait_ge(d_lo.sem, d_lo.at(b, f + 1))
                    if f == 0 and not first:
                        pe.wait_ge(out_ready.sem, out_ready.at(b - 1, TT))
                    for tt in range(TT):
                        cols = slice(tt * P, (tt + 1) * P)
                        three(down[:, tt, :], hd_h[0:m, s, cols], hd_l[0:m, s, cols], d_h[0:m, s, :], d_l[0:m, s, :],
                              f == 0, False)
                    three(adps[0:LR, :], da_h[0:m, f, :], da_l[0:m, f, :], hd_h[0:m, s, :], hd_l[0:m, s, :],
                          f == 0, f == FT - 1).then_inc(tile_done.sem, 1)

                base(0, 0)
                base(1, 0)
                pe.wait_ge(wx_ready.sem, wx_ready.at(b, 1))
                for tt in range(TT):
                    mm = pe.transpose(adps[0:LR, tt * P:(tt + 1) * P], wx[:, tt, :], ident)
                mm.then_inc(wx_ps.sem, 1)
                base(0, 1)
                low_rank(0, 0)
                low_rank(1, 0)
                low_rank(0, 1)
                base(1, 1)
                low_rank(1, 1)
                project(0)
                for f in range(2, FT):
                    for side in range(2):
                        base(side, f)
                        low_rank(side, f)
                    project(f - 1)
                project(FT - 1)
                pe.wait_ge(y_lo.sem, y_lo.at(b, 3))
                for tt in range(TT):
                    cols = slice(tt * P, (tt + 1) * P)
                    three(down[:, tt, :], yg_h[:, cols], yg_l[:, cols], db_h[:, :], db_l[:, :], False, True)\
                        .then_inc(out_ps.sem, 1)

            batch(0, True)
            with pe.Fori(1, BATCH) as b:
                batch(b, False)

        @block.vector
        def _(dve):
            dve.wait_ge(f_c.sem, 32)
            dve.wait_ge(f_consts.sem, 3)
            for n, (_, raw, hi, lo) in enumerate(lora):
                dve.wait_ge(lora_hi.sem, n + 1)
                dve.tensor_tensor(lo, raw, hi.bitcast(F32), ALU.subtract).then_inc(lora_lo.sem, 1)

            def batch(b, first):
                link = Link(dve, dve_link, b)
                dve.wait_ge(x2_loaded.sem, x2_loaded.at(b, 16))
                for tt in range(TT):
                    ins = dve.bn_stats(stats[:, tt, :], x2_in[:, tt, :])
                link(ins)
                separate(dve, passed[2])
                for tt in range(TT):
                    ins = dve.bn_aggr(mv[:, tt, :], stats[:, tt, :])
                ins.then_inc(ln_stats.sem, 1)
                dve.wait_ge(ln_stats.sem, ln_stats.at(b, 1))
                dve.wait_ge(rstd_ready.sem, rstd_ready.at(b, 1))
                for tt in range(TT):
                    dve.tensor_scalar(x2_in[:, tt, :], x2_in[:, tt, :], mv[:, tt, 0:1], rstd[:, tt:tt + 1],
                                      ALU.subtract, ALU.mult).then_inc(xn_ready.sem, 1)
                for k in range(KT):
                    dve.wait_ge(xT_hi.sem, xT_hi.at(b, k + 1))
                    dve.tensor_tensor(xT_l[:, k, :], ring[k % 3][:, :], xT_h[:, k, :].bitcast(F32), ALU.subtract)\
                        .then_inc(xT_lo.sem, 1)
                dve.wait_ge(prob_tanh.sem, prob_tanh.at(b, 1))
                link(dve.tensor_scalar(prob[:, :, :], prob[:, :, :], 0.5, 0.5, ALU.mult, ALU.add))
                link(dve.tensor_tensor(biased[:, :, :], prob[:, :, :],
                                       bias_bc[:, :].unsqueeze(1).to_broadcast([P, TT, EXPERTS]), ALU.add))
                shape = [P, TT, EXPERTS, EXPERTS]
                others, own = biased[:, :, :].unsqueeze(2).to_broadcast(shape), biased[:, :, :].unsqueeze(3).to_broadcast(shape)
                dve.tensor_tensor(beats[:, :, :, :], others, own, ALU.is_gt)
                link(dve.tensor_tensor(ties[:, :, :, :], others, own, ALU.is_equal))
                pairs = ties[:, :, :, :].rearrange("p a e j -> p a (e j)")
                link(dve.tensor_tensor(pairs, pairs, lower.unsqueeze(1).to_broadcast([P, TT, EXPERTS * EXPERTS]), ALU.mult))
                link(dve.tensor_tensor(beats[:, :, :, :], beats[:, :, :, :], ties[:, :, :, :], ALU.add))
                link(dve.tensor_reduce(rank[:, :, :], beats[:, :, :, :], AX.X, ALU.add))
                link(dve.scalar_tensor_tensor(prob[:, :, :], rank[:, :, :], 1.5, prob[:, :, :], ALU.is_lt, ALU.mult))
                link(dve.tensor_reduce(wsum[:, 0, :], prob[:, :, :], AX.X, ALU.add))
                link(dve.tensor_scalar(wsum[:, 0, :], wsum[:, 0, :], 1e-8, float(RANK), ALU.add, ALU.mult))
                link(dve.reciprocal(wsum[:, 1, :], wsum[:, 0, :]))
                dve.tensor_tensor(wx[:, :, 0:ER].rearrange("p a (e r) -> p a e r", r=RANK),
                                  prob[:, :, :].unsqueeze(3).to_broadcast([P, TT, EXPERTS, RANK]),
                                  wsum[:, 1, :].unsqueeze(2).unsqueeze(3).to_broadcast([P, TT, EXPERTS, RANK]),
                                  ALU.mult).then_inc(wx_ready.sem, 1)
                dve.wait_ge(wxT_ready.sem, wxT_ready.at(b, 1))
                for n, (a, hi, lo) in enumerate(((a_gate, yg_h, yg_l), (a_up, yu_h, yu_l))):
                    dve.wait_ge(a_copied.sem, a_copied.at(b, n + 1))
                    dve.tensor_tensor(y[:, :], a[0:LR, :], wxT[:, :], ALU.mult).then_inc(y_ready.sem, 1)
                    dve.wait_ge(y_hi.sem, y_hi.at(b, n + 1))
                    dve.tensor_tensor(lo[:, :], y[:, :], hi[:, :].bitcast(F32), ALU.subtract).then_inc(y_lo.sem, 1)
                    dve.wait_ge(y_lo.sem, y_lo.at(b, n + 1))
                for f in range(FT):
                    m = f_rows(f)
                    dve.wait_ge(tanh_done.sem, tanh_done.at(b, f + 1))
                    dve.scalar_tensor_tensor(gated[0:m, :], th[0:m, :], 1.0, ring[(KT + 2 + 2 * f) % 3][0:m, :],
                                             ALU.add, ALU.mult).then_inc(gated_done.sem, 1)
                    dve.wait_ge(gated_done.sem, gated_done.at(b, f + 1))
                    dve.wait_ge(u_ps.sem, u_ps.at(b, f + 1))
                    if f:
                        dve.wait_ge(hd_lo.sem, hd_lo.at(b, f))
                    elif not first:
                        dve.wait_ge(hd_lo.sem, hd_lo.at(b - 1, FT))
                    dve.scalar_tensor_tensor(hd[0:m, :], gated[0:m, :], 0.5, ring[(KT + 3 + 2 * f) % 3][0:m, :],
                                             ALU.mult, ALU.mult).then_inc(hd_ready.sem, 1)
                dve.wait_ge(tile_done.sem, tile_done.at(b, FT))
                dve.tensor_tensor(y[:, :], adps[0:LR, :], wxT[:, :], ALU.mult).then_inc(y_ready.sem, 1)
                dve.wait_ge(y_hi.sem, y_hi.at(b, 3))
                dve.tensor_tensor(yg_l[:, :], y[:, :], yg_h[:, :].bitcast(F32), ALU.subtract).then_inc(y_lo.sem, 1)
                dve.wait_ge(res_loaded.sem, res_loaded.at(b, 16))
                for tt in range(TT):
                    dve.wait_ge(out_ps.sem, out_ps.at(b, tt + 1))
                    dve.tensor_tensor(x2_res[:, tt, :], down[:, tt, :], x2_res[:, tt, :], ALU.add)\
                        .then_inc(out_ready.sem, 1)
                link.done()

            batch(0, True)
            with dve.Fori(1, BATCH) as b:
                batch(b, False)


FF_DVE_LINKS = 1 + 10


def build(nc, arrays):
    ap = {n: nc.dram_tensor(n, a.shape, F32, kind="ExternalInput").ap() for n, a in arrays.items()}
    x2 = nc.dram_tensor("x2", (BATCH, T, D), F32, kind="Internal").ap()
    out = nc.dram_tensor("out", (BATCH, T, D), F32, kind="ExternalOutput").ap()
    attention_and_mlp(nc, ap["x"], ap["wqkvT"].rearrange("(k p) e -> p k e", p=P), ap["bq"], ap["bkv"],
                      ap["woT"].rearrange("(k p) e -> p k e", p=P), ap["bo"], ap["w"], ap["wT"], ap["d"], ap["dT"],
                      ap["consts"][:, 0:3, :], x2)
    feed_forward(nc, x2, ap["wg"].rearrange("(k p) f -> p k f", p=P), ap["wu"].rearrange("(k p) f -> p k f", p=P),
                 ap["wd"], ap["ga"], ap["ua"], ap["da"], ap["gb"], ap["ub"], ap["db"], ap["expert_bias"],
                 ap["consts"], out)


def kernel(x, fside_BxS2xS2_0, ctx_1024, L0_attn_Wqkv_w, L0_attn_Wqkv_b, L0_attn_out_w, L0_attn_out_b,
           L0_ffn_W_router, L0_ffn_W_gate, L0_ffn_W_up, L0_ffn_W_down, L0_ffn_sA_gate, L0_ffn_sB_gate,
           L0_ffn_sA_up, L0_ffn_sB_up, L0_ffn_sA_down, L0_ffn_sB_down, L0_ffn_A_gate, L0_ffn_B_gate,
           L0_ffn_A_up, L0_ffn_B_up, L0_ffn_A_down, L0_ffn_B_down, L0_ffn_expert_bias):
    import concourse.bacc as bacc
    from concourse.bass_utils import run_bass_kernel_spmd

    def host(a):
        return np.ascontiguousarray(np.asarray(a))

    def lora_in(routed, shared, *more):
        routed = host(routed)
        return host(np.concatenate([routed.transpose(1, 0, 2).reshape(routed.shape[1], ER), host(shared), *more], axis=1))

    def lora_out(routed, shared):
        return host(np.concatenate([host(routed).reshape(ER, -1), host(shared)], axis=0))

    consts = np.zeros((P, 4, P), np.float32)
    consts[:, 0, :] = np.eye(P, dtype=np.float32)
    consts[:, 1, :] = np.triu(np.full((P, P), NEG, np.float32), 1)
    consts[:, 2, :] = np.tril(np.full((P, P), NEG, np.float32), -1)
    consts[:, 3, 0:EXPERTS * EXPERTS] = np.tril(np.ones((EXPERTS, EXPERTS), np.float32), -1).reshape(-1)
    bqkv = host(L0_attn_Wqkv_b)
    arrays = {
        "x": host(x), "wqkvT": host(host(L0_attn_Wqkv_w).T), "woT": host(host(L0_attn_out_w).T),
        "bq": host(bqkv[0:D].reshape(KT, P).T), "bkv": host(bqkv[D:QKV].reshape(2 * HD, 1)), "bo": host(L0_attn_out_b),
        "w": host(fside_BxS2xS2_0), "wT": host(host(fside_BxS2xS2_0).transpose(0, 2, 1)),
        "d": host(ctx_1024), "dT": host(host(ctx_1024).transpose(0, 2, 1)),
        "wg": host(L0_ffn_W_gate), "wu": host(L0_ffn_W_up), "wd": host(L0_ffn_W_down),
        "ga": lora_in(L0_ffn_A_gate, L0_ffn_sA_gate, np.zeros((D, ROUTE - LR), np.float32), host(L0_ffn_W_router)),
        "ua": lora_in(L0_ffn_A_up, L0_ffn_sA_up), "da": lora_in(L0_ffn_A_down, L0_ffn_sA_down),
        "gb": lora_out(L0_ffn_B_gate, L0_ffn_sB_gate), "ub": lora_out(L0_ffn_B_up, L0_ffn_sB_up),
        "db": lora_out(L0_ffn_B_down, L0_ffn_sB_down), "expert_bias": host(L0_ffn_expert_bias), "consts": consts,
    }
    nc = bacc.Bacc("TRN2", target_bir_lowering=False, num_devices=1)
    build(nc, arrays)
    got = run_bass_kernel_spmd(nc, [arrays], core_ids=[0])
    return got.results[0]["out"]
```

```python
from contextlib import ExitStack

import numpy as np

import concourse.bass as bass
from concourse import mybir

F32 = mybir.dt.float32
F32R = mybir.dt.float32r
BF16 = mybir.dt.bfloat16
ALU = mybir.AluOpType
ACT = mybir.ActivationFunctionType
AX = mybir.AxisListType

P = 128
BATCH, T, D = 4, 512, 512
HEADS, HD = 16, 32
KT = D // P
TT = T // P
QKV = D + 2 * HD
INNER = 256
IT = INNER // P
DFF, RANK, EXPERTS = 1376, 8, 8
FT = -(-DFF // P)
FLAST = DFF - (FT - 1) * P
ER = EXPERTS * RANK
LR = ER + RANK
ROUTE = 96
LA = ROUTE + EXPERTS
LN_EPS, QEPS, QMAX = 1e-5, 1e-6, 127.0
MAGIC = 1.5 * 2.0 ** 23
NEG = -1e38
SCALE = HD ** -0.5
KROWS = 3 * HD


MLP_LINKS = 1 + 4 + 2 * (1 + 1 + 2) + 1


def f_rows(f):
    return P if f < FT - 1 else FLAST


class Signal:

    def __init__(self, ctx, nc, name, per):
        self.sem, self.per = ctx.enter_context(nc.semaphore(name)), per

    def at(self, b, n):
        assert 1 <= n <= self.per
        return b * self.per + n


class Link:

    def __init__(self, eng, signal, b):
        self.eng, self.chain, self.b, self.n = eng, signal, b, 0

    def __call__(self, ins):
        self.n += 1
        ins.then_inc(self.chain.sem, 1)
        self.eng.wait_ge(self.chain.sem, self.chain.at(self.b, self.n))

    def done(self):
        assert self.n == self.chain.per, (self.n, self.chain.per)


def separate(eng, passed):
    eng.sem_inc(passed.sem, 1)


class Tenants:

    def __init__(self, slots):
        self.slots, self.last, self.n = slots, {}, 0

    def new_batch(self, first):
        self.n, self.old, self.last = 0, dict(self.last), {}

    def claim(self, eng, b, signal, count):
        slot = self.n % self.slots
        self.n += 1
        if slot in self.last:
            before, at = self.last[slot]
            eng.wait_ge(before.sem, before.at(b, at))
        elif slot in self.old:
            before, at = self.old[slot]
            eng.wait_ge(before.sem, before.at(b - 1, at))
        self.last[slot] = (signal, count)
        return slot


MLP_AMONG = {
    ("q", 0): ((0, "stats"),), ("q", 1): ((0, "normalise"),), ("q", 2): ((0, "turn0"),), ("q", 3): ((0, "colmax0"),),
    ("max", 1): ((0, "turn1"),), ("max", 3): ((0, "colmax1"),), ("max", 5): ((0, "wmax"),), ("max", 7): ((0, "ratio"),),
    ("max", 9): ((0, "s_cols"),), ("max", 11): ((0, "s_rows_ps"),), ("max", 12): ((0, "s_rows"),),
    ("max", 14): ((0, "scale"),), ("max", 18): ((0, "rowmax_a"),), ("max", 22): ((0, "rowmax_w"),),
    ("exp", 0, 1): ((0, "round_a"),), ("exp", 1, 0): ((0, "integer_a"),), ("exp", 1, 1): ((0, "round_w"),),
    ("exp", 2, 0): ((0, "turn_a"),), ("exp", 2, 1): ((0, "copy_a"),), ("exp", 3, 1): ((0, "turn_w"),),
    ("exp", 4, 0): ((0, "copy_w"), (0, "w_row_ps")), ("exp", 4, 1): ((0, "w_row"),), ("exp", 5, 0): ((0, "product0"),),
    ("exp", 5, 1): ((0, "undo0"),), ("exp", 6, 0): ((0, "product1"),), ("exp", 6, 1): ((0, "undo1"),),
    ("exp", 7, 0): ((1, "tanh"),), ("exp", 7, 1): ((1, "act"),), ("exp", 8, 0): ((1, "turn"),),
    ("exp", 8, 1): ((1, "colmax"), (1, "wmax")), ("exp", 9, 0): ((1, "ratio"),), ("exp", 9, 1): ((1, "s_cols"),),
    ("exp", 10, 0): ((1, "s_rows_ps"), (1, "s_rows")), ("exp", 10, 1): ((1, "scale"),),
    ("exp", 11, 0): ((1, "rowmax_a"), (1, "rowmax_w")), ("exp", 11, 1): ((1, "round_a"), (1, "integer_a")),
    ("exp", 12, 0): ((1, "round_w"), (1, "turn_a")), ("exp", 12, 1): ((1, "copy_a"),), ("exp", 13, 0): ((1, "turn_w"),),
    ("exp", 13, 1): ((1, "copy_w"), (1, "w_row_ps")), ("exp", 14, 0): ((1, "w_row"), (1, "product0")),
    ("exp", 14, 1): ((1, "undo0"),), ("exp", 15, 0): ((1, "product1"),), ("exp", 15, 1): ((1, "undo1"), (1, "residual")),
}


def mlp_among(mlp, c, *where):
    if c is not None:
        for n, step in MLP_AMONG.get(where, ()):
            mlp(c, n, step)


def mlp_alone(mlp, c):
    for steps in MLP_AMONG.values():
        for n, step in steps:
            mlp(c, n, step)


def attention_and_mlp(nc, x, wqkv, bq, bkv, wo, bo, mlp_w, mlp_wT, mlp_d, mlp_dT, consts, x2):
    with ExitStack() as ctx:
        def sb(name, shape, dt=F32):
            return ctx.enter_context(nc.sbuf_tensor(name, shape, dt))

        def sig(name, per=1):
            return Signal(ctx, nc, name, per)

        cst = sb("cst", [P, 3, P])
        ident = cst[:, 0, :]
        mask_bf = sb("mask_bf", [P, 3, P], BF16)
        ones = sb("ones", [P, HD])
        half = sb("half", [P, 2 * KT])
        ln_eps, magic = sb("ln_eps", [P, TT]), sb("magic", [P, 1])
        wqkv_h, wqkv_l = sb("wqkv_h", [P, KT, QKV], F32R), sb("wqkv_l", [P, KT, QKV], F32R)
        wo_h, wo_l = sb("wo_h", [P, KT, D], F32R), sb("wo_l", [P, KT, D], F32R)
        bq_sb, bkv_sb = sb("bq_sb", [P, KT]), sb("bkv_sb", [2 * HD, 1])
        bo_bc = sb("bo_bc", [P, D])
        x_in = sb("x_in", [P, TT, D])
        stats, mv = sb("stats", [P, 2, TT, 6]), sb("mv", [P, 2, TT, 2])
        veps, rstd = sb("veps", [P, 2, TT]), sb("rstd", [P, 2, TT])
        hT_h, hT_l = sb("hT_h", [P, KT, T], F32R), sb("hT_l", [P, KT, T], F32R)
        with ExitStack() as early:
            qT_h = early.enter_context(nc.sbuf_tensor("qT_h", [P, KT, T], F32R))
            qT_l = early.enter_context(nc.sbuf_tensor("qT_l", [P, KT, T], F32R))
        probs = sb("probs", [P, 4, 2, T])
        kst = sb("kst", [P, T], F32R)
        qst = sb("qst", [P, HEADS, T], F32R)
        v = sb("v", [P, TT, HD])
        negm = sb("negm", [P, HEADS, TT])
        negm_h, negm_l = sb("negm_h", [HD, 2, P], F32R), sb("negm_l", [HD, 2, P], F32R)
        rden, cx = sb("rden", [P, T]), sb("cx", [P, 2, T])
        vT = rden
        x1 = sb("x1", [P, TT, D])
        xn = sb("xn", [P, TT, D])
        w_raw, d_raw = sb("w_raw", [P, TT, D]), sb("d_raw", [P, TT, INNER])
        hid = sb("hid", [P, TT, D])
        wT_raw = hid
        th_flat = sb("th", [P, TT * INNER])
        th = th_flat[:, :].rearrange("p (a i) -> p a i", i=INNER)
        dT_raw = th_flat[:, :].rearrange("p (k d) -> p k d", d=D)
        a_bf, wT_bf, aT_bf = sb("a_bf", [P, TT, D], BF16), sb("wT_bf", [P, KT, D], BF16), sb("aT_bf", [P, KT, D], BF16)
        w_bf = a_bf
        amax, wmax, sc = sb("amax", [P, 1, KT]), sb("wmax", [P, KT + IT]), sb("sc", [P, 5, KT])
        rows, wrow = sb("rows", [P, 2, D]), sb("wrow", [P, D])
        qm, qs, qi = sb("qm", [P, 2, TT]), sb("qs", [P, 2, TT]), sb("qi", [P, 2, TT])

        slots = [ctx.enter_context(nc.psum_tensor(f"slot{i}", [P, 2, T], F32)) for i in range(2)]
        mlp_ps = ctx.enter_context(nc.psum_tensor("mlp_ps", [P, 2, T], F32))
        mlp_ps_bf = mlp_ps[:, :, :].bitcast(BF16)
        av = ctx.enter_context(nc.psum_tensor("av", [P, T], F32))
        den = ctx.enter_context(nc.psum_tensor("den", [P, T], F32))

        c_loaded, w_loaded = sig("c_loaded"), [sig(f"w_loaded{i}") for i in range(3)]
        masks_ready, consts_ready = sig("masks_ready"), sig("consts_ready", 6)
        w_hi, w_lo = sig("w_hi", 8), sig("w_lo", 8)
        x_loaded, res_loaded = sig("x_loaded", 16), sig("xres_loaded", 16)
        ln_stats, rstd_ready, xn_ready = sig("ln_stats"), sig("rstd_ready"), sig("xn_ready", TT)
        xT_ps, xT_hi, xT_lo = sig("xT_ps", 2), sig("xT_hi", 2), sig("xT_lo", 2)
        xb_ready = sig("xb_ready")
        kv_ps, kv_act, kv_lo = sig("kv_ps"), sig("kv_act", 3), sig("kv_lo")
        q_ps, q_hi, q_lo = sig("q_ps", KT), sig("q_hi", KT), sig("q_lo", KT)
        v_ps, v_ready = sig("v_ps"), sig("v_ready")
        q_moved = [sig(f"q_moved{i}", 16 * 12) for i in range(2)]
        s_ps, s_max = sig("s_ps", 22), sig("s_max", 22)
        m_ps, m_hi, m_lo = sig("m_ps", 2), sig("m_hi", 2), sig("m_lo", 2)
        m_moved = [sig(f"m_moved{i}", 32) for i in range(2)]
        t_ps, p_ready, pv_done = sig("t_ps", 32), sig("p_ready", 32), sig("pv_done", 16)
        av_out, den_out, rden_ready = sig("av_out", 4), sig("den_out", 4), sig("rden_ready", 4)
        cx_ready, cx_hi, cx_lo = sig("cx_ready", 4), sig("cx_hi", 4), sig("cx_lo", 4)
        o_ps, x1_ready = sig("o_ps", 2), sig("x1_ready", 2)
        ln_link = sig("ln_link")
        mw_loaded, mwT_loaded = sig("mw_loaded", 16), sig("mwT_loaded", 16)
        md_loaded, mdT_loaded = sig("md_loaded", 16), sig("mdT_loaded", 16)
        ln2_stats, rstd2_ready, xn2_ready = sig("ln2_stats"), sig("rstd2_ready"), sig("xn2_ready", TT)
        turned, colmax = sig("turned", 3), sig("colmax", 3)
        ratio, root, s_cols = sig("ratio", 2), sig("root", 2), sig("s_cols", 2)
        s_rows_ps, s_rows = sig("s_rows_ps", 2), sig("s_rows", 2)
        w_scaled, q_scale = sig("w_scaled", 2), sig("q_scale", 2)
        rounded, a_q, w_q = sig("rounded", 16), sig("a_q", 2), sig("w_q", 2)
        aq_ps, aqT, wq_ps, wqT = sig("aq_ps", 2), sig("aqT", 2), sig("wq_ps", 2), sig("wqT", 2)
        wrow_ps, wrow_ready = sig("wrow_ps", 2), sig("wrow_ready", 2)
        h_ps, h_ready, th_ready, act_ready = sig("h_ps", 4), sig("h_ready", 8), sig("th_ready"), sig("act_ready")
        x2_ready, x2_stored = sig("x2_ready", TT), sig("x2_stored", 16)
        mlp_link, pool_link = sig("mlp_link", MLP_LINKS), [sig("pool_link1"), sig("pool_link2")]
        passed = [sig(f"passed_{e}") for e in ("sp", "pe", "dve")]

        hid_flat, d_flat = hid[:, :, :].rearrange("p a d -> p (a d)"), d_raw[:, :, :].rearrange("p a d -> p (a d)")
        wq_stage, wq_last = hid_flat[:, 0:3 * QKV].rearrange("p (k n) -> p k n", n=QKV), d_flat[:, 0:QKV]
        weights = ([(wq_stage[:, k, :], wqkv_h[:, k, :], wqkv_l[:, k, :], 0) for k in range(3)]
                   + [(wq_last, wqkv_h[:, 3, :], wqkv_l[:, 3, :], 1)]
                   + [(w_raw[:, k, :], wo_h[:, k, :], wo_l[:, k, :], 2) for k in range(KT)])
        products = ((KT, D, xn, w_raw), (IT, INNER, hid[:, :, 0:INNER], d_raw))

        block = ctx.enter_context(nc.Block())

        @block.sync
        def _(sp):
            def load_x(b):
                return sp.dma_start(x_in[:, :, :], x[b].rearrange("(a p) d -> p a d", p=P))

            load_x(0).then_inc(x_loaded.sem, 16)
            sp.dma_start(cst[:, :, :], consts).then_inc(c_loaded.sem, 16)
            sp.dma_start(wq_stage, wqkv[:, 0:3, :]).then_inc(w_loaded[0].sem, 16)
            sp.dma_start(wq_last, wqkv[:, 3, :]).then_inc(w_loaded[1].sem, 16)
            sp.dma_start(bq_sb[:, :], bq).then_inc(c_loaded.sem, 16)
            sp.dma_start(bkv_sb[:, :], bkv).then_inc(c_loaded.sem, 16)
            sp.dma_start(bo_bc[:, :], bo.partition_broadcast(P)).then_inc(c_loaded.sem, 16)
            sp.dma_start(w_raw[:, :, :], wo).then_inc(w_loaded[2].sem, 16)

            def batch(b, first):
                if not first:
                    sp.wait_ge(xT_ps.sem, xT_ps.at(b - 1, 2))
                    load_x(b).then_inc(x_loaded.sem, 16)
                qst_by_quadrant = qst[:, :, :].rearrange("p (e j) t -> p e j t", j=4)
                for ep in range(2):
                    if not first:
                        sp.wait_ge(pv_done.sem, pv_done.at(b - 1, 16))
                        separate(sp, passed[0])
                    sp.wait_ge(q_hi.sem, q_hi.at(b, 2 * ep + 2))
                    sp.wait_ge(q_lo.sem, q_lo.at(b, 2 * ep + 2))
                    for j in range(4):
                        for src, row in ((qT_h, 0), (qT_l, HD), (qT_h, 2 * HD)):
                            sp.dma_start(qst_by_quadrant[row:row + HD, 2 * ep:2 * ep + 2, j, :].bitcast(F32),
                                         src[HD * j:HD * j + HD, 2 * ep:2 * ep + 2, :].bitcast(F32))\
                              .then_inc(q_moved[ep].sem, 16)
                for hf in range(2):
                    sp.wait_ge(m_hi.sem, m_hi.at(b, hf + 1))
                    sp.wait_ge(m_lo.sem, m_lo.at(b, hf + 1))
                    for src, row in ((negm_h, KROWS), (negm_l, KROWS + 1)):
                        sp.dma_start(qst[row:row + 1, 8 * hf:8 * hf + 8, :].bitcast(F32), src[:, hf, :].bitcast(F32))\
                          .then_inc(m_moved[hf].sem, 16)
                if first:
                    sp.wait_ge(w_lo.sem, 8)
                else:
                    sp.wait_ge(x2_ready.sem, x2_ready.at(b - 1, TT))
                sp.dma_start(x1[:, :, :], x[b].rearrange("(a p) d -> p a d", p=P)).then_inc(res_loaded.sem, 16)
                for dst, src, loaded in ((w_raw, mlp_w, mw_loaded), (d_raw, mlp_d, md_loaded)):
                    sp.dma_start(dst[:, :, :], src[b].rearrange("(a p) d -> p a d", p=P)).then_inc(loaded.sem, 16)
                if not first:
                    sp.wait_ge(x2_stored.sem, x2_stored.at(b - 1, 16))
                sp.dma_start(wT_raw[:, :, :], mlp_wT[b].rearrange("(a p) d -> p a d", p=P)).then_inc(mwT_loaded.sem, 16)
                sp.dma_start(dT_raw, mlp_dT[b].rearrange("(a p) d -> p a d", p=P)).then_inc(mdT_loaded.sem, 16)

            batch(0, True)
            with sp.Fori(1, BATCH) as b:
                batch(b, False)

        @block.gpsimd
        def _(pool):
            for n, (dst, value) in enumerate(((ones[:, :], 1.0), (half[:, 0:KT], 0.5), (half[:, KT:2 * KT], -0.5),
                                              (kst[KROWS:P, :].bitcast(F32), 1.0), (ln_eps[:, :], LN_EPS),
                                              (magic[:, :], MAGIC))):
                pool.memset(dst, value).then_inc(consts_ready.sem, 1)
                pool.wait_ge(consts_ready.sem, n + 1)

            def inverse_deviation(c, n, stats_ready, link, ready):
                pool.wait_ge(stats_ready.sem, stats_ready.at(c, 1))
                pool.tensor_tensor(veps[:, n, :], mv[:, n, :, 1], ln_eps[:, :], ALU.add).then_inc(link.sem, 1)
                pool.wait_ge(link.sem, link.at(c, 1))
                pool.tensor_tensor(rstd[:, n, :], veps[:, n, :], half[:, KT:2 * KT], ALU.pow).then_inc(ready.sem, 1)

            def mlp(c, n, step):
                nk, width, _, raw = products[n]
                if step == "stats":
                    inverse_deviation(c, 1, ln2_stats, pool_link[1], rstd2_ready)
                if step == "ratio":
                    pool.wait_ge(ratio.sem, ratio.at(c, n + 1))
                    pool.tensor_tensor(sc[:, 2, 0:nk], sc[:, 1, 0:nk], half[:, 0:nk], ALU.pow).then_inc(root.sem, 1)
                if step == "scale":
                    loaded = (mw_loaded, md_loaded)[n]
                    pool.wait_ge(s_rows.sem, s_rows.at(c, n + 1))
                    pool.wait_ge(loaded.sem, loaded.at(c, 16))
                    pool.tensor_tensor(raw[:, :, :], raw[:, :, :],
                                       rows[:, 0, 0:width].unsqueeze(1).to_broadcast([P, TT, width]),
                                       ALU.mult).then_inc(w_scaled.sem, 1)
                if step == "copy_a":
                    pool.wait_ge(rounded.sem, rounded.at(c, 8 * n + 8))
                    pool.wait_ge(aq_ps.sem, aq_ps.at(c, n + 1))
                    pool.tensor_tensor(w_bf[:, :, 0:width], raw[:, :, :],
                                       magic[:, :].unsqueeze(1).to_broadcast([P, TT, width]), ALU.subtract)\
                        .then_inc(w_q.sem, 1)
                if step == "residual":
                    for tt in range(TT):
                        pool.wait_ge(h_ready.sem, h_ready.at(c, TT + tt + 1))
                        pool.tensor_tensor(hid[:, tt, :], hid[:, tt, :], x1[:, tt, :], ALU.add).then_inc(x2_ready.sem, 1)

            def batch(b, c, first):
                inverse_deviation(b, 0, ln_stats, pool_link[0], rstd_ready)
                if first:
                    for n, (raw, hi, lo, _) in enumerate(weights):
                        pool.wait_ge(w_hi.sem, n + 1)
                        pool.tensor_tensor(lo, raw, hi.bitcast(F32), ALU.subtract).then_inc(w_lo.sem, 1)
                for e in range(KT):
                    mlp_among(mlp, c, "q", e)
                for group in range(1, 23):
                    mlp_among(mlp, c, "max", group)
                for step in range(16):
                    mlp_among(mlp, c, "exp", step, 0)
                    mlp_among(mlp, c, "exp", step, 1)
                    if step >= 7 and step % 4 == 3:
                        low_context(b, (step - 7) // 4)
                pool.wait_ge(res_loaded.sem, res_loaded.at(b, 16))
                pool.tensor_tensor(x1[:, :, :], x1[:, :, :], bo_bc[:, :].unsqueeze(1).to_broadcast([P, TT, D]),
                                   ALU.add).then_inc(xb_ready.sem, 1)
                low_context(b, 3)

            def low_context(b, g):
                pool.wait_ge(cx_hi.sem, cx_hi.at(b, g + 1))
                pool.tensor_tensor(hT_l[:, g, :], cx[:, g % 2, :], hT_h[:, g, :].bitcast(F32), ALU.subtract)\
                    .then_inc(cx_lo.sem, 1)

            pool.wait_ge(c_loaded.sem, 64)
            batch(0, None, True)
            with pool.Fori(1, BATCH) as b:
                batch(b, b - 1, False)
            mlp_alone(mlp, BATCH - 1)

        @block.scalar
        def _(act):
            act.wait_ge(c_loaded.sem, 64)
            act.activation(mask_bf[:, :, :], cst[:, :, :], ACT.Copy).then_inc(masks_ready.sem, 1)
            for raw, hi, _, part in weights:
                act.wait_ge(w_loaded[part].sem, 16)
                act.activation(hi, raw, ACT.Copy).then_inc(w_hi.sem, 1)

            def mlp(c, n, step):
                nk, width, a, w = products[n]
                if step == "tanh":
                    act.wait_ge(h_ready.sem, h_ready.at(c, TT))
                    act.activation(th, hid[:, :, 0:INNER], ACT.Tanh, scale=0.5).then_inc(th_ready.sem, 1)
                if step == "s_rows":
                    act.wait_ge(s_rows_ps.sem, s_rows_ps.at(c, n + 1))
                    act.activation(rows[:, :, 0:width], mlp_ps[:, :, 0:width], ACT.Copy).then_inc(s_rows.sem, 1)
                if step in ("round_a", "round_w"):
                    i, y = (0, a) if step == "round_a" else (1, w)
                    act.wait_ge(q_scale.sem, q_scale.at(c, n + 1))
                    for tt in range(TT):
                        act.activation(y[:, tt, :], y[:, tt, :], ACT.Copy, scale=qi[:, i, tt:tt + 1], bias=MAGIC)\
                            .then_inc(rounded.sem, 1)
                if step in ("copy_a", "copy_w"):
                    turned_, dst, ready = (aq_ps, aT_bf, aqT) if step == "copy_a" else (wq_ps, wT_bf, wqT)
                    act.wait_ge(turned_.sem, turned_.at(c, n + 1))
                    act.activation(dst[:, 0:nk, :],
                                   mlp_ps_bf[:, 0:(nk + 1) // 2, :].rearrange("p a (c t) -> p (a c) t", c=2),
                                   ACT.Copy).then_inc(ready.sem, 1)
                if step == "w_row":
                    act.wait_ge(wrow_ps.sem, wrow_ps.at(c, n + 1))
                    act.activation(wrow[:, :], mlp_ps[:, 0, :], ACT.Copy).then_inc(wrow_ready.sem, 1)
                if step == "residual":
                    act.wait_ge(x2_ready.sem, x2_ready.at(c, TT))
                    act.dma_start(x2[c].rearrange("(a p) d -> p a d", p=P), hid[:, :, :]).then_inc(x2_stored.sem, 16)

            def batch(b, c, first):
                use = [0]

                def slot():
                    use[0] += 1
                    return slots[(use[0] - 1) % 2]

                for s in range(2):
                    act.wait_ge(xT_ps.sem, xT_ps.at(b, s + 1))
                    if not first and s == 0:
                        act.wait_ge(o_ps.sem, o_ps.at(b - 1, 2))
                    act.activation(hT_h[:, 2 * s:2 * s + 2, :], slot()[:, :, :], ACT.Copy).then_inc(xT_hi.sem, 1)
                act.wait_ge(kv_ps.sem, kv_ps.at(b, 1))
                kv = slot()
                act.activation(kst[0:HD, :], kv[0:HD, 0, :], ACT.Identity, bias=bkv_sb[0:HD, :]).then_inc(kv_act.sem, 1)
                act.activation(kst[HD:2 * HD, :], kv[0:HD, 0, :], ACT.Identity, bias=bkv_sb[0:HD, :])\
                    .then_inc(kv_act.sem, 1)
                act.activation(vT[HD:2 * HD, :], kv[HD:2 * HD, 0, :], ACT.Identity, bias=bkv_sb[HD:2 * HD, :])\
                    .then_inc(kv_act.sem, 1)
                for e in range(KT):
                    if e % 2 == 0:
                        ps = slot()
                    act.wait_ge(q_ps.sem, q_ps.at(b, e + 1))
                    act.activation(qT_h[:, e, :], ps[:, e % 2, :], ACT.Identity, bias=bq_sb[:, e:e + 1])\
                        .then_inc(q_hi.sem, 1)
                    mlp_among(mlp, c, "q", e)
                slot()
                for hf in range(2):
                    for group in range(11 * hf + 1, 11 * hf + 12):
                        slot()
                        mlp_among(mlp, c, "max", group)
                    act.wait_ge(m_ps.sem, m_ps.at(b, hf + 1))
                    if not first:
                        act.wait_ge(m_moved[hf].sem, m_moved[hf].at(b - 1, 32))
                    act.activation(negm_h[:, hf, :], slot()[0:HD, 0, 0:P], ACT.Copy).then_inc(m_hi.sem, 1)

                def sums_out(g):
                    act.wait_ge(pv_done.sem, pv_done.at(b, 4 * g + 4))
                    if g:
                        act.wait_ge(cx_ready.sem, cx_ready.at(b, g))
                    act.activation(rden[:, :], den[:, :], ACT.Copy).then_inc(den_out.sem, 1)

                def high_context(g):
                    act.wait_ge(cx_ready.sem, cx_ready.at(b, g + 1))
                    act.activation(hT_h[:, g, :], cx[:, g % 2, :], ACT.Copy).then_inc(cx_hi.sem, 1)

                step = 0
                for g in range(4):
                    for kt in reversed(range(TT)):
                        for pr in range(2):
                            act.wait_ge(t_ps.sem, t_ps.at(b, 2 * step + pr + 1))
                            if step >= 2:
                                act.wait_ge(pv_done.sem, pv_done.at(b, step - 1))
                            n = T - kt * P
                            act.activation(probs[:, 2 * (step % 2) + pr, :, 0:n], slot()[:, :, 0:n], ACT.Exp,
                                           scale=SCALE).then_inc(p_ready.sem, 1)
                        mlp_among(mlp, c, "exp", step, 0)
                        if g and kt == TT - 1:
                            sums_out(g - 1)
                        if g and kt == 1:
                            high_context(g - 1)
                        mlp_among(mlp, c, "exp", step, 1)
                        step += 1
                sums_out(3)
                high_context(3)

            batch(0, None, True)
            with act.Fori(1, BATCH) as b:
                batch(b, b - 1, False)
            mlp_alone(mlp, BATCH - 1)
            act.wait_ge(x2_stored.sem, 16 * BATCH)

        @block.tensor
        def _(pe):
            tenants = Tenants(2)
            pe.wait_ge(c_loaded.sem, 64)
            pe.wait_ge(masks_ready.sem, 1)
            pe.wait_ge(consts_ready.sem, 6)

            def three(out, w_hi_, w_lo_, m_hi_, m_lo_, start, stop):
                pe.matmul(out, w_hi_, m_hi_, start=start, stop=False)
                pe.matmul(out, w_hi_, m_lo_, start=False, stop=False)
                return pe.matmul(out, w_lo_, m_hi_, start=False, stop=stop)

            def mlp(c, n, step):
                nk = products[n][0]
                if step in ("turn0", "turn1"):
                    s = int(step[-1])
                    if s:
                        pe.wait_ge(colmax.sem, colmax.at(c, 1))
                    for j in range(2):
                        for tt in range(TT):
                            if s == 0 and j == 0:
                                pe.wait_ge(xn2_ready.sem, xn2_ready.at(c, tt + 1))
                            k = 2 * s + j
                            mm = pe.transpose(mlp_ps[:, j, tt * P:(tt + 1) * P], xn[:, tt, k * P:(k + 1) * P], ident)
                    mm.then_inc(turned.sem, 1)
                if step == "turn":
                    pe.wait_ge(act_ready.sem, act_ready.at(c, 1))
                    for k in range(IT):
                        for tt in range(TT):
                            mm = pe.transpose(mlp_ps[:, k, tt * P:(tt + 1) * P], hid[:, tt, k * P:(k + 1) * P], ident)
                    mm.then_inc(turned.sem, 1)
                if step == "s_rows_ps":
                    pe.wait_ge(s_cols.sem, s_cols.at(c, n + 1))
                    for i in range(2):
                        for k in range(nk):
                            mm = pe.transpose(mlp_ps[:, i, k * P:(k + 1) * P],
                                              sc[:, 3 + i, k:k + 1].to_broadcast([P, P]), ident)
                    mm.then_inc(s_rows_ps.sem, 1)
                if step in ("turn_a", "turn_w"):
                    src, quantised, turned_, free = ((a_bf, a_q, aq_ps, s_rows) if step == "turn_a"
                                                     else (w_bf, w_q, wq_ps, aqT))
                    pe.wait_ge(free.sem, free.at(c, n + 1))
                    pe.wait_ge(quantised.sem, quantised.at(c, n + 1))
                    for k in range(nk):
                        for tt in range(TT):
                            at = (k % 2) * T + tt * P
                            mm = pe.transpose(mlp_ps_bf[:, k // 2, at:at + P], src[:, tt, k * P:(k + 1) * P],
                                              mask_bf[:, 0, :])
                    mm.then_inc(turned_.sem, 1)
                if step == "w_row_ps":
                    pe.wait_ge(wqT.sem, wqT.at(c, n + 1))
                    for ot in range(TT):
                        mm = pe.transpose(mlp_ps[:, 0, ot * P:(ot + 1) * P], qs[:, 1, ot:ot + 1].to_broadcast([P, P]),
                                          ident)
                    mm.then_inc(wrow_ps.sem, 1)
                if step in ("product0", "product1"):
                    s = int(step[-1])
                    if s:
                        pe.wait_ge(h_ready.sem, h_ready.at(c, TT * n + 2))
                    else:
                        pe.wait_ge(wrow_ready.sem, wrow_ready.at(c, n + 1))
                    for j in range(2):
                        tt = 2 * s + j
                        for k in range(nk):
                            mm = pe.matmul(mlp_ps[:, j, :], aT_bf[:, k, tt * P:(tt + 1) * P], wT_bf[:, k, :],
                                           start=(k == 0), stop=(k == nk - 1))
                    mm.then_inc(h_ps.sem, 1)

            def batch(b, c, first):
                tenants.new_batch(first)
                for s in range(2):
                    ps = slots[tenants.claim(pe, b, xT_lo, s + 1)]
                    for j in range(2):
                        for tt in range(TT):
                            if s == 0 and j == 0:
                                pe.wait_ge(xn_ready.sem, xn_ready.at(b, tt + 1))
                            k = 2 * s + j
                            mm = pe.transpose(ps[:, j, tt * P:(tt + 1) * P], x_in[:, tt, k * P:(k + 1) * P], ident)
                    mm.then_inc(xT_ps.sem, 1)
                ps = slots[tenants.claim(pe, b, kv_lo, 1)]
                for k in range(KT):
                    if k % 2 == 0:
                        pe.wait_ge(xT_lo.sem, xT_lo.at(b, k // 2 + 1))
                    if first:
                        pe.wait_ge(w_lo.sem, k + 1)
                    mm = three(ps[0:2 * HD, 0, :], wqkv_h[:, k, D:QKV], wqkv_l[:, k, D:QKV], hT_h[:, k, :], hT_l[:, k, :],
                               k == 0, k == KT - 1)
                mm.then_inc(kv_ps.sem, 1)
                for e in range(KT):
                    if e % 2 == 0:
                        ps = slots[tenants.claim(pe, b, q_lo, e + 2)]
                    for k in range(KT):
                        mm = three(ps[:, e % 2, :], wqkv_h[:, k, e * P:(e + 1) * P], wqkv_l[:, k, e * P:(e + 1) * P],
                                   hT_h[:, k, :], hT_l[:, k, :], k == 0, k == KT - 1)
                    mm.then_inc(q_ps.sem, 1)
                    mlp_among(mlp, c, "q", e)
                ps = slots[tenants.claim(pe, b, v_ready, 1)]
                pe.wait_ge(kv_act.sem, kv_act.at(b, 3))
                separate(pe, passed[1])
                for kt in range(TT):
                    mm = pe.transpose(ps[:, 0, kt * HD:(kt + 1) * HD], vT[HD:2 * HD, kt * P:(kt + 1) * P],
                                      cst[HD:2 * HD, 0, HD:2 * HD])
                mm.then_inc(v_ps.sem, 1)
                pe.wait_ge(kv_lo.sem, kv_lo.at(b, 1))
                group = 0
                for hf in range(2):
                    pe.wait_ge(q_moved[hf].sem, q_moved[hf].at(b, q_moved[hf].per))
                    for qt in range(TT):
                        n = (qt + 1) * P
                        per_bank = T // n if qt != 2 else 1
                        for h0 in range(8 * hf, 8 * hf + 8, 2 * per_bank):
                            group += 1
                            ps = slots[tenants.claim(pe, b, s_max, group)]
                            for i in range(2 * per_bank):
                                bank, at = i // per_bank, i % per_bank
                                pe.matmul(ps[:, bank, (at + 1) * n - P:(at + 1) * n], mask_bf[:, 0, :],
                                          mask_bf[:, 1, :], start=True, stop=False, skip_group_check=True)
                                mm = pe.matmul(ps[:, bank, at * n:(at + 1) * n],
                                               qst[0:KROWS, h0 + i, qt * P:(qt + 1) * P], kst[0:KROWS, 0:n],
                                               start=False, stop=True, skip_group_check=True)
                            mm.then_inc(s_ps.sem, 1)
                            mlp_among(mlp, c, "max", group)
                    ps = slots[tenants.claim(pe, b, m_lo, hf + 1)]
                    pe.wait_ge(s_max.sem, s_max.at(b, 11 * hf + 11))
                    pe.transpose(ps[0:HD, 0, 0:P], negm[:, 8 * hf:8 * hf + 8, :].rearrange("p h q -> p (h q)"), ident)\
                        .then_inc(m_ps.sem, 1)

                def scores(g, kt, step):
                    n = T - kt * P
                    for pr in range(2):
                        ps = slots[tenants.claim(pe, b, p_ready, 2 * step + pr + 1)]
                        for j in range(2):
                            pe.matmul(ps[:, j, 0:P], mask_bf[:, 0, :], mask_bf[:, 2, :], start=True, stop=False,
                                      skip_group_check=True)
                            mm = pe.matmul(ps[:, j, 0:n], kst[0:KROWS + 2, kt * P:(kt + 1) * P],
                                           qst[0:KROWS + 2, 4 * g + 2 * pr + j, kt * P:T], start=False, stop=True,
                                           skip_group_check=True)
                        mm.then_inc(t_ps.sem, 1)

                def values(g, kt, step):
                    n = T - kt * P
                    pe.wait_ge(p_ready.sem, p_ready.at(b, 2 * step + 2))
                    for out, weights_, read in ((av, v[:, kt, :], av_out), (den, ones[:, :], den_out)):
                        if kt == TT - 1 and g:
                            pe.wait_ge(read.sem, read.at(b, g))
                        elif kt == TT - 1 and not first:
                            pe.wait_ge(read.sem, read.at(b - 1, 4))
                        for c_ in range(4):
                            mm = pe.matmul(out[HD * c_:HD * c_ + HD, kt * P:T], weights_,
                                           probs[:, 2 * (step % 2) + c_ // 2, c_ % 2, 0:n], start=(kt == TT - 1),
                                           stop=(kt == 0), skip_group_check=True)
                    mm.then_inc(pv_done.sem, 1)

                pe.wait_ge(v_ready.sem, v_ready.at(b, 1))
                steps = [(g, kt) for g in range(4) for kt in reversed(range(TT))]
                for step, (g, kt) in enumerate(steps):
                    if kt == TT - 1 and g % 2 == 0:
                        pe.wait_ge(m_moved[g // 2].sem, m_moved[g // 2].at(b, 32))
                    scores(g, kt, step)
                    mlp_among(mlp, c, "exp", step, 0)
                    if step:
                        values(*steps[step - 1], step - 1)
                    mlp_among(mlp, c, "exp", step, 1)
                values(*steps[-1], len(steps) - 1)
                for s in range(2):
                    ps = slots[tenants.claim(pe, b, x1_ready, s + 1)]
                    if first and s == 0:
                        pe.wait_ge(w_lo.sem, 8)
                    for g in range(4):
                        for j in range(2):
                            tt = 2 * s + j
                            if s == 0 and j == 0:
                                pe.wait_ge(cx_lo.sem, cx_lo.at(b, g + 1))
                            mm = three(ps[:, j, :], hT_h[:, g, tt * P:(tt + 1) * P], hT_l[:, g, tt * P:(tt + 1) * P],
                                       wo_h[:, g, :], wo_l[:, g, :], g == 0, g == 3)
                    mm.then_inc(o_ps.sem, 1)

            batch(0, None, True)
            with pe.Fori(1, BATCH) as b:
                batch(b, b - 1, False)
            mlp_alone(mlp, BATCH - 1)

        @block.vector
        def _(dve):
            dve.wait_ge(c_loaded.sem, 64)

            def layernorm(c, n, src, dst, link, stats_ready, deviation_ready, ready, part):
                if part == "stats":
                    for tt in range(TT):
                        ins = dve.bn_stats(stats[:, n, tt, :], src[:, tt, :])
                    link(ins)
                    separate(dve, passed[2])
                    for tt in range(TT):
                        ins = dve.bn_aggr(mv[:, n, tt, :], stats[:, n, tt, :])
                    ins.then_inc(stats_ready.sem, 1)
                else:
                    dve.wait_ge(stats_ready.sem, stats_ready.at(c, 1))
                    dve.wait_ge(deviation_ready.sem, deviation_ready.at(c, 1))
                    for tt in range(TT):
                        dve.tensor_scalar(dst[:, tt, :], src[:, tt, :], mv[:, n, tt, 0:1], rstd[:, n, tt:tt + 1],
                                          ALU.subtract, ALU.mult).then_inc(ready.sem, 1)

            chain = [None]

            def mlp(c, n, step):
                nk, width, a, w = products[n]
                if step == "stats":
                    chain[0] = Link(dve, mlp_link, c)
                    dve.wait_ge(x1_ready.sem, x1_ready.at(c, 2))
                link = chain[0]
                if step in ("stats", "normalise"):
                    layernorm(c, 1, x1, xn, link, ln2_stats, rstd2_ready, xn2_ready, step)
                if step in ("colmax0", "colmax1"):
                    s = int(step[-1])
                    dve.wait_ge(turned.sem, turned.at(c, s + 1))
                    dve.tensor_reduce(amax[:, 0, 2 * s:2 * s + 2], mlp_ps[:, :, :], AX.X, ALU.max,
                                      apply_absolute_value=True).then_inc(colmax.sem, 1)
                if step == "act":
                    dve.wait_ge(th_ready.sem, th_ready.at(c, 1))
                    link(dve.scalar_tensor_tensor(th, th, 1.0, a, ALU.add, ALU.mult))
                    dve.scalar_tensor_tensor(a, th, 0.5, hid[:, :, INNER:D], ALU.mult, ALU.mult)\
                        .then_inc(act_ready.sem, 1)
                if step == "colmax":
                    dve.wait_ge(turned.sem, turned.at(c, 3))
                    dve.tensor_reduce(amax[:, 0, 0:IT], mlp_ps[:, :, :], AX.X, ALU.max,
                                      apply_absolute_value=True).then_inc(colmax.sem, 1)
                if step == "wmax" and n == 0:
                    for wT, loaded, dst in ((wT_raw[:, :, :], mwT_loaded, wmax[:, 0:KT]),
                                            (dT_raw, mdT_loaded, wmax[:, KT:KT + IT])):
                        dve.wait_ge(loaded.sem, loaded.at(c, 16))
                        link(dve.tensor_reduce(dst, wT, AX.X, ALU.max, apply_absolute_value=True))
                    link(dve.tensor_scalar(wmax[:, :], wmax[:, :], QEPS, None, ALU.max))
                    link(dve.reciprocal(wmax[:, :], wmax[:, :]))
                if step == "ratio":
                    dve.wait_ge(colmax.sem, colmax.at(c, 2 + n))
                    dve.scalar_tensor_tensor(sc[:, 1, 0:nk], amax[:, 0, 0:nk], QEPS, wmax[:, KT * n:KT * n + nk],
                                             ALU.max, ALU.mult).then_inc(ratio.sem, 1)
                if step == "s_cols":
                    dve.wait_ge(root.sem, root.at(c, n + 1))
                    link(dve.tensor_scalar(sc[:, 3, 0:nk], sc[:, 2, 0:nk], QEPS, None, ALU.max))
                    dve.reciprocal(sc[:, 4, 0:nk], sc[:, 3, 0:nk]).then_inc(s_cols.sem, 1)
                if step == "scale":
                    dve.wait_ge(s_rows.sem, s_rows.at(c, n + 1))
                    link(dve.tensor_tensor(a[:, :, :], a[:, :, :],
                                           rows[:, 1, 0:width].unsqueeze(1).to_broadcast([P, TT, width]), ALU.mult))
                if step == "rowmax_a":
                    dve.tensor_reduce(qm[:, 0, :], a[:, :, :], AX.X, ALU.max, apply_absolute_value=True)
                if step == "rowmax_w":
                    dve.wait_ge(w_scaled.sem, w_scaled.at(c, n + 1))
                    link(dve.tensor_reduce(qm[:, 1, :], w[:, :, :], AX.X, ALU.max, apply_absolute_value=True))
                    link(dve.tensor_scalar(qs[:, :, :], qm[:, :, :], QEPS, 1.0 / QMAX, ALU.max, ALU.mult))
                    dve.reciprocal(qi[:, :, :], qs[:, :, :]).then_inc(q_scale.sem, 1)
                if step == "integer_a":
                    dve.wait_ge(rounded.sem, rounded.at(c, 8 * n + 4))
                    dve.tensor_scalar(a_bf[:, :, 0:width], a[:, :, :], MAGIC, None, ALU.subtract).then_inc(a_q.sem, 1)
                if step in ("undo0", "undo1"):
                    s = int(step[-1])
                    dve.wait_ge(wrow_ready.sem, wrow_ready.at(c, n + 1))
                    dve.wait_ge(h_ps.sem, h_ps.at(c, 2 * n + s + 1))
                    for j in range(2):
                        tt = 2 * s + j
                        dve.scalar_tensor_tensor(hid[:, tt, :], mlp_ps[:, j, :], qs[:, 0, tt:tt + 1], wrow[:, :],
                                                 ALU.mult, ALU.mult).then_inc(h_ready.sem, 1)
                if step == "residual":
                    dve.wait_ge(h_ready.sem, h_ready.at(c, 2 * TT))
                    link.done()

            def batch(b, c, first):
                use = [0]

                def slot():
                    use[0] += 1
                    return slots[(use[0] - 1) % 2]

                dve.wait_ge(x_loaded.sem, x_loaded.at(b, 16))
                for part in ("stats", "normalise"):
                    layernorm(b, 0, x_in, x_in, Link(dve, ln_link, b), ln_stats, rstd_ready, xn_ready, part)
                for s in range(2):
                    dve.wait_ge(xT_hi.sem, xT_hi.at(b, s + 1))
                    dve.tensor_tensor(hT_l[:, 2 * s:2 * s + 2, :], slot()[:, :, :],
                                      hT_h[:, 2 * s:2 * s + 2, :].bitcast(F32), ALU.subtract).then_inc(xT_lo.sem, 1)
                dve.wait_ge(kv_act.sem, kv_act.at(b, 3))
                dve.scalar_tensor_tensor(kst[2 * HD:KROWS, :], slot()[0:HD, 0, :], bkv_sb[0:HD, :],
                                         kst[0:HD, :].bitcast(F32), ALU.add, ALU.subtract).then_inc(kv_lo.sem, 1)
                for e in range(KT):
                    if e % 2 == 0:
                        ps = slot()
                    dve.wait_ge(q_hi.sem, q_hi.at(b, e + 1))
                    dve.scalar_tensor_tensor(qT_l[:, e, :], ps[:, e % 2, :], bq_sb[:, e:e + 1],
                                             qT_h[:, e, :].bitcast(F32), ALU.add, ALU.subtract).then_inc(q_lo.sem, 1)
                    mlp_among(mlp, c, "q", e)
                dve.wait_ge(v_ps.sem, v_ps.at(b, 1))
                dve.tensor_copy(v[:, :, :], slot()[:, 0, 0:TT * HD].rearrange("p (a d) -> p a d", d=HD))\
                    .then_inc(v_ready.sem, 1)
                group = 0
                for hf in range(2):
                    for qt in range(TT):
                        n = (qt + 1) * P
                        per_bank = T // n if qt != 2 else 1
                        for h0 in range(8 * hf, 8 * hf + 8, 2 * per_bank):
                            group += 1
                            dve.wait_ge(s_ps.sem, s_ps.at(b, group))
                            dve.tensor_reduce(negm[:, h0:h0 + 2 * per_bank, qt].rearrange("p (a c) -> p a c", a=2),
                                              slot()[:, :, 0:per_bank * n].rearrange("p a (c n) -> p a c n", n=n),
                                              AX.X, ALU.max, negate=True).then_inc(s_max.sem, 1)
                            mlp_among(mlp, c, "max", group)
                    dve.wait_ge(m_hi.sem, m_hi.at(b, hf + 1))
                    dve.tensor_tensor(negm_l[:, hf, :], slot()[0:HD, 0, 0:P], negm_h[:, hf, :].bitcast(F32),
                                      ALU.subtract).then_inc(m_lo.sem, 1)
                use[0] += 32

                def context(g):
                    dve.wait_ge(pv_done.sem, pv_done.at(b, 4 * g + 4))
                    if g >= 2:
                        dve.wait_ge(cx_lo.sem, cx_lo.at(b, g - 1))
                    dve.tensor_copy(cx[:, g % 2, :], av[:, :]).then_inc(av_out.sem, 1)
                    dve.wait_ge(den_out.sem, den_out.at(b, g + 1))
                    dve.reciprocal(rden[:, :], rden[:, :]).then_inc(rden_ready.sem, 1)
                    dve.wait_ge(rden_ready.sem, rden_ready.at(b, g + 1))
                    dve.wait_ge(av_out.sem, av_out.at(b, g + 1))
                    dve.tensor_tensor(cx[:, g % 2, :], cx[:, g % 2, :], rden[:, :], ALU.mult).then_inc(cx_ready.sem, 1)

                for step in range(16):
                    mlp_among(mlp, c, "exp", step, 0)
                    if step and step % 4 == 0:
                        context(step // 4 - 1)
                    mlp_among(mlp, c, "exp", step, 1)
                context(3)
                dve.wait_ge(xb_ready.sem, xb_ready.at(b, 1))
                for s in range(2):
                    dve.wait_ge(o_ps.sem, o_ps.at(b, s + 1))
                    dve.tensor_tensor(x1[:, 2 * s:2 * s + 2, :], slot()[:, :, :], x1[:, 2 * s:2 * s + 2, :], ALU.add)\
                        .then_inc(x1_ready.sem, 1)

            batch(0, None, True)
            with dve.Fori(1, BATCH) as b:
                batch(b, b - 1, False)
            mlp_alone(mlp, BATCH - 1)


def feed_forward(nc, x2, wg, wu, wd, ga, ua, da, gb, ub, db, expert_bias, consts, out):
    with ExitStack() as ctx:
        def sb(name, shape, dt=F32):
            return ctx.enter_context(nc.sbuf_tensor(name, shape, dt))

        def sig(name, per=1):
            return Signal(ctx, nc, name, per)

        cst = sb("f_cst", [P, 4, P])
        ident, lower = cst[:, 0, :], cst[:, 3, 0:EXPERTS * EXPERTS]
        half, ln_eps = sb("f_half", [P, TT]), sb("f_ln_eps", [P, TT])
        bias_bc = sb("bias_bc", [P, EXPERTS])
        wg_sb, wu_sb, wd_sb = sb("wg_sb", [P, KT, DFF]), sb("wu_sb", [P, KT, DFF]), sb("wd_sb", [P, FT, D])
        g_h, g_l = sb("g_h", [P, 2, KT, P], F32R), sb("g_l", [P, 2, KT, P], F32R)
        u_h, u_l = sb("u_h", [P, 2, KT, P], F32R), sb("u_l", [P, 2, KT, P], F32R)
        d_h, d_l = sb("d_h", [P, 2, D], F32R), sb("d_l", [P, 2, D], F32R)
        ga_h, ga_l = sb("ga_h", [P, KT, LA], F32R), sb("ga_l", [P, KT, LA], F32R)
        ua_h, ua_l = sb("ua_h", [P, KT, LR], F32R), sb("ua_l", [P, KT, LR], F32R)
        da_h, da_l = sb("da_h", [P, FT, LR], F32R), sb("da_l", [P, FT, LR], F32R)
        gb_h, gb_l = sb("gb_h", [LR, DFF], F32R), sb("gb_l", [LR, DFF], F32R)
        ub_h, ub_l = sb("ub_h", [LR, DFF], F32R), sb("ub_l", [LR, DFF], F32R)
        db_h, db_l = sb("db_h", [LR, D], F32R), sb("db_l", [LR, D], F32R)
        x2_in, x2_res = sb("x2_in", [P, TT, D]), sb("x2_res", [P, TT, D])
        stats, mv = sb("f_stats", [P, TT, 6]), sb("f_mv", [P, TT, 2])
        veps, rstd = sb("f_veps", [P, TT]), sb("f_rstd", [P, TT])
        xT_h, xT_l = sb("xT_h", [P, KT, T], F32R), sb("xT_l", [P, KT, T], F32R)
        a_gate, a_up = sb("a_gate", [LA, T]), sb("a_up", [LR, T])
        prob = sb("prob", [P, TT, EXPERTS])
        biased = sb("biased", [P, TT, EXPERTS])
        beats, ties = sb("beats", [P, TT, EXPERTS, EXPERTS]), sb("ties", [P, TT, EXPERTS, EXPERTS])
        rank, wsum = sb("rank", [P, TT, EXPERTS]), sb("wsum", [P, 2, TT])
        wx, wxT = sb("wx", [P, TT, LR]), sb("wxT", [LR, T])
        y = sb("y", [LR, T])
        yg_h, yg_l = sb("yg_h", [LR, T], F32R), sb("yg_l", [LR, T], F32R)
        yu_h, yu_l = sb("yu_h", [LR, T], F32R), sb("yu_l", [LR, T], F32R)
        work = sb("work", [P, 3, T])
        th, gated, hd = work[:, 0, :], work[:, 1, :], work[:, 2, :]
        hd_h, hd_l = sb("hd_h", [P, 2, T], F32R), sb("hd_l", [P, 2, T], F32R)

        ring = [ctx.enter_context(nc.psum_tensor(f"ring{i}", [P, T], F32)) for i in range(3)]
        down = ctx.enter_context(nc.psum_tensor("down", [P, TT, D], F32))
        adps = ctx.enter_context(nc.psum_tensor("adps", [P, T], F32))

        f_c = sig("f_c")
        ff_loaded = [sig(f"ff_loaded{c}") for c in range(3)]
        lora_loaded, lora_hi, lora_lo = [sig(f"lora_loaded{n}") for n in range(7)], sig("lora_hi"), sig("lora_lo")
        f_consts = sig("f_consts")
        x2_loaded, res_loaded, stored = sig("x2_loaded", 16), sig("res_loaded", 16), sig("stored", 16)
        ln_stats, rstd_ready, xn_ready = sig("f_ln_stats"), sig("f_rstd_ready"), sig("f_xn_ready", TT)
        xT_ps, xT_hi, xT_lo = sig("f_xT_ps", KT), sig("f_xT_hi", KT), sig("f_xT_lo", KT)
        a_ps, a_copied = sig("a_ps", 2), sig("a_copied", 2)
        logits_ps, prob_tanh, wx_ready, wx_ps, wxT_ready = (sig("logits_ps"), sig("prob_tanh"), sig("wx_ready"),
                                                            sig("wx_ps"), sig("wxT_ready"))
        y_ready, y_hi, y_lo = sig("y_ready", 3), sig("y_hi", 3), sig("y_lo", 3)
        gu_hi, gu_lo = sig("gu_hi", 2 * FT), sig("gu_lo", 2 * FT)
        d_hi, d_lo = sig("d_hi", FT), sig("d_lo", FT)
        g_ps, u_ps = sig("g_ps", FT), sig("u_ps", FT)
        tanh_done, gated_done, hd_ready = sig("tanh_done", FT), sig("gated_done", FT), sig("hd_ready", FT)
        hd_hi, hd_lo = sig("hd_hi", FT), sig("hd_lo", FT)
        tile_done = sig("tile_done", FT)
        out_ps, out_ready = sig("out_ps", TT), sig("out_ready", TT)
        dve_link, pool_link = sig("f_dve_link", FF_DVE_LINKS), sig("f_pool_link", 1)
        passed = [sig(f"f_passed_{e}") for e in ("pool", "pe", "dve")]

        ga_end, ua_end, da_end = KT * LA, KT * (LA + LR), KT * (LA + LR) + FT * LR
        res_flat, work_flat = (t[:, :, :].rearrange("p a d -> p (a d)") for t in (x2_res, work))
        last = da_end - LR
        lora = [(ga.rearrange("(k p) n -> p k n", p=P), res_flat[:, 0:ga_end].rearrange("p (k n) -> p k n", k=KT),
                 ga_h[:, :, :], ga_l[:, :, :]),
                (ua.rearrange("(k p) n -> p k n", p=P), res_flat[:, ga_end:ua_end].rearrange("p (k n) -> p k n", k=KT),
                 ua_h[:, :, :], ua_l[:, :, :]),
                (gb, work_flat[0:LR, 0:DFF], gb_h[:, :], gb_l[:, :]),
                (da[0:(FT - 1) * P, :].rearrange("(f p) n -> p f n", p=P),
                 res_flat[:, ua_end:last].rearrange("p (f n) -> p f n", n=LR), da_h[:, 0:FT - 1, :], da_l[:, 0:FT - 1, :]),
                (da[(FT - 1) * P:DFF, :], res_flat[0:FLAST, last:da_end], da_h[0:FLAST, FT - 1, :], da_l[0:FLAST, FT - 1, :]),
                (db, res_flat[0:LR, da_end:da_end + D], db_h[:, :], db_l[:, :]),
                (ub, work_flat[0:LR, 0:DFF], ub_h[:, :], ub_l[:, :])]
        GB, UB = 2, len(lora) - 1

        def weight_parts(f):
            m, at, s = f_rows(f), f * P, f % 2
            return ((wg_sb[:, :, at:at + m], g_h[:, s, :, 0:m], g_l[:, s, :, 0:m]),
                    (wu_sb[:, :, at:at + m], u_h[:, s, :, 0:m], u_l[:, s, :, 0:m]),
                    (wd_sb[0:m, f, :], d_h[0:m, s, :], d_l[0:m, s, :]))

        block = ctx.enter_context(nc.Block())

        @block.sync
        def _(sp):
            sp.dma_start(x2_in[:, :, :], x2[0].rearrange("(a p) d -> p a d", p=P)).then_inc(x2_loaded.sem, 16)
            sp.dma_start(cst[:, :, :], consts).then_inc(f_c.sem, 16)
            sp.dma_start(bias_bc[:, :], expert_bias.partition_broadcast(P)).then_inc(f_c.sem, 16)
            for n, (src, raw, _, _) in enumerate(lora):
                if n == UB:
                    sp.wait_ge(lora_lo.sem, GB + 1)
                sp.dma_start(raw, src).then_inc(lora_loaded[n].sem, 16)

            def batch(b, first):
                if not first:
                    sp.wait_ge(xn_ready.sem, xn_ready.at(b - 1, TT))
                    sp.wait_ge(xT_ps.sem, xT_ps.at(b - 1, KT))
                    sp.dma_start(x2_in[:, :, :], x2[b].rearrange("(a p) d -> p a d", p=P)).then_inc(x2_loaded.sem, 16)
                if first:
                    sp.wait_ge(lora_lo.sem, len(lora))
                else:
                    sp.wait_ge(stored.sem, stored.at(b - 1, 16))
                sp.dma_start(x2_res[:, :, :], x2[b].rearrange("(a p) d -> p a d", p=P)).then_inc(res_loaded.sem, 16)
                sp.wait_ge(out_ready.sem, out_ready.at(b, TT))
                sp.dma_start(out[b].rearrange("(a p) d -> p a d", p=P), x2_res[:, :, :]).then_inc(stored.sem, 16)

            batch(0, True)
            with sp.Fori(1, BATCH) as b:
                batch(b, False)
            sp.wait_ge(stored.sem, 16 * BATCH)

        @block.gpsimd
        def _(pool):
            for n, (dst, value) in enumerate(((half[:, :], -0.5), (wx[:, :, ER:LR], 1.0 / RANK),
                                              (ln_eps[:, :], LN_EPS))):
                pool.memset(dst, value).then_inc(f_consts.sem, 1)
                pool.wait_ge(f_consts.sem, n + 1)

            def batch(b, first):
                link = Link(pool, pool_link, b)
                pool.wait_ge(ln_stats.sem, ln_stats.at(b, 1))
                link(pool.tensor_tensor(veps[:, :], mv[:, :, 1], ln_eps[:, :], ALU.add))
                pool.tensor_tensor(rstd[:, :], veps[:, :], half[:, :], ALU.pow).then_inc(rstd_ready.sem, 1)

                def split_gate_up(f):
                    for i, (w, hi, lo) in enumerate(weight_parts(f)[0:2]):
                        pool.wait_ge(gu_hi.sem, gu_hi.at(b, 2 * f + i + 1))
                        pool.tensor_tensor(lo, w, hi.bitcast(F32), ALU.subtract).then_inc(gu_lo.sem, 1)

                def split_down(f):
                    w, hi, lo = weight_parts(f)[2]
                    pool.wait_ge(d_hi.sem, d_hi.at(b, f + 1))
                    pool.tensor_tensor(lo, w, hi.bitcast(F32), ALU.subtract).then_inc(d_lo.sem, 1)

                split_gate_up(0)
                split_gate_up(1)
                split_down(0)
                for f in range(FT):
                    if f + 2 < FT:
                        split_gate_up(f + 2)
                    pool.wait_ge(hd_hi.sem, hd_hi.at(b, f + 1))
                    m = f_rows(f)
                    pool.tensor_tensor(hd_l[0:m, f % 2, :], hd[0:m, :], hd_h[0:m, f % 2, :].bitcast(F32), ALU.subtract)\
                        .then_inc(hd_lo.sem, 1)
                    if f + 1 < FT:
                        split_down(f + 1)
                link.done()

            batch(0, True)
            with pool.Fori(1, BATCH) as b:
                batch(b, False)

        @block.scalar
        def _(act):
            for c in range(3):
                cols = slice(4 * P * c, min(4 * P * (c + 1), DFF))
                act.dma_start(wg_sb[:, :, cols], wg[:, :, cols]).then_inc(ff_loaded[c].sem, 16)
                act.dma_start(wu_sb[:, :, cols], wu[:, :, cols]).then_inc(ff_loaded[c].sem, 16)
                full = min(4 * (c + 1), FT - 1)
                act.dma_start(wd_sb[:, 4 * c:full, :], wd[4 * c * P:full * P, :].rearrange("(f p) d -> p f d", p=P))\
                   .then_inc(ff_loaded[c].sem, 16)
            act.dma_start(wd_sb[0:FLAST, FT - 1, :], wd[(FT - 1) * P:DFF, :]).then_inc(ff_loaded[2].sem, 16)
            for n, (_, raw, hi, _) in enumerate(lora):
                act.wait_ge(lora_loaded[n].sem, 16)
                act.activation(hi, raw, ACT.Copy).then_inc(lora_hi.sem, 1)

            def batch(b, first):
                def split(f, i):
                    w, hi, _ = weight_parts(f)[i]
                    done, ready = ((g_ps, gu_hi), (u_ps, gu_hi), (tile_done, d_hi))[i]
                    if f >= 2:
                        act.wait_ge(done.sem, done.at(b, f - 1))
                    elif not first:
                        act.wait_ge(done.sem, done.at(b - 1, FT - (FT - 1 - f) % 2))
                    if first:
                        act.wait_ge(ff_loaded[f // 4].sem, 64 if f >= 8 else 48)
                    act.activation(hi, w, ACT.Copy).then_inc(ready.sem, 1)

                for f, i in ((0, 0), (0, 1), (1, 0), (1, 1), (0, 2)):
                    split(f, i)
                for k in range(KT):
                    act.wait_ge(xT_ps.sem, xT_ps.at(b, k + 1))
                    act.activation(xT_h[:, k, :], ring[k % 3][:, :], ACT.Copy).then_inc(xT_hi.sem, 1)
                act.wait_ge(a_ps.sem, a_ps.at(b, 1))
                act.activation(a_gate[:, :], ring[KT % 3][0:LA, :], ACT.Copy).then_inc(a_copied.sem, 1)
                act.wait_ge(a_ps.sem, a_ps.at(b, 2))
                act.activation(a_up[:, :], ring[(KT + 1) % 3][0:LR, :], ACT.Copy).then_inc(a_copied.sem, 1)
                act.wait_ge(logits_ps.sem, logits_ps.at(b, 1))
                act.activation(prob[:, :, :], adps[:, 0:TT * EXPERTS].rearrange("p (a e) -> p a e", e=EXPERTS),
                               ACT.Tanh, scale=0.5).then_inc(prob_tanh.sem, 1)
                act.wait_ge(wx_ps.sem, wx_ps.at(b, 1))
                act.activation(wxT[:, :], adps[0:LR, :], ACT.Copy).then_inc(wxT_ready.sem, 1)
                for n, hi in enumerate((yg_h, yu_h)):
                    act.wait_ge(y_ready.sem, y_ready.at(b, n + 1))
                    act.activation(hi[:, :], y[:, :], ACT.Copy).then_inc(y_hi.sem, 1)
                for f in range(FT):
                    m = f_rows(f)
                    act.wait_ge(g_ps.sem, g_ps.at(b, f + 1))
                    if f:
                        act.wait_ge(gated_done.sem, gated_done.at(b, f))
                    act.activation(th[0:m, :], ring[(KT + 2 + 2 * f) % 3][0:m, :], ACT.Tanh, scale=0.5)\
                        .then_inc(tanh_done.sem, 1)
                    if f + 2 < FT:
                        split(f + 2, 0)
                        split(f + 2, 1)
                    act.wait_ge(hd_ready.sem, hd_ready.at(b, f + 1))
                    if f >= 2:
                        act.wait_ge(tile_done.sem, tile_done.at(b, f - 1))
                    act.activation(hd_h[0:m, f % 2, :], hd[0:m, :], ACT.Copy).then_inc(hd_hi.sem, 1)
                    if f + 1 < FT:
                        split(f + 1, 2)
                act.wait_ge(y_ready.sem, y_ready.at(b, 3))
                act.activation(yg_h[:, :], y[:, :], ACT.Copy).then_inc(y_hi.sem, 1)

            batch(0, True)
            with act.Fori(1, BATCH) as b:
                batch(b, False)

        @block.tensor
        def _(pe):
            tenants = Tenants(3)
            pe.wait_ge(f_c.sem, 32)

            def three(out_, w_hi, w_lo, m_hi, m_lo, start, stop):
                pe.matmul(out_, w_hi, m_hi, start=start, stop=False, skip_group_check=True)
                pe.matmul(out_, w_hi, m_lo, start=False, stop=False, skip_group_check=True)
                return pe.matmul(out_, w_lo, m_hi, start=False, stop=stop, skip_group_check=True)

            def batch(b, first):
                tenants.new_batch(first)
                for k in range(KT):
                    ps = ring[tenants.claim(pe, b, xT_lo, k + 1)]
                    for tt in range(TT):
                        if k == 0:
                            pe.wait_ge(xn_ready.sem, xn_ready.at(b, tt + 1))
                        mm = pe.transpose(ps[:, tt * P:(tt + 1) * P], x2_in[:, tt, k * P:(k + 1) * P], ident)
                    mm.then_inc(xT_ps.sem, 1)
                if first:
                    pe.wait_ge(lora_lo.sem, len(lora))
                for n, (hi, lo, width) in enumerate(((ga_h, ga_l, LA), (ua_h, ua_l, LR))):
                    ps = ring[tenants.claim(pe, b, a_copied, n + 1)]
                    for k in range(KT):
                        pe.wait_ge(xT_lo.sem, xT_lo.at(b, k + 1))
                        mm = three(ps[0:width, :], hi[:, k, :], lo[:, k, :], xT_h[:, k, :], xT_l[:, k, :],
                                   k == 0, k == KT - 1)
                    mm.then_inc(a_ps.sem, 1)
                pe.wait_ge(a_copied.sem, a_copied.at(b, 1))
                if not first:
                    pe.wait_ge(y_ready.sem, y_ready.at(b - 1, 3))
                separate(pe, passed[1])
                for tt in range(TT):
                    mm = pe.transpose(adps[:, tt * EXPERTS:(tt + 1) * EXPERTS], a_gate[ROUTE:LA, tt * P:(tt + 1) * P],
                                      cst[ROUTE:LA, 0, ROUTE:LA])
                mm.then_inc(logits_ps.sem, 1)

                held = {}

                def base(side, f):
                    m = f_rows(f)
                    hi, lo, freed = ((g_h, g_l, gated_done), (u_h, u_l, hd_ready))[side]
                    ps = held[side, f] = ring[tenants.claim(pe, b, freed, f + 1)]
                    pe.wait_ge(gu_lo.sem, gu_lo.at(b, 2 * f + side + 1))
                    for k in range(KT):
                        three(ps[0:m, :], hi[:, f % 2, k, 0:m], lo[:, f % 2, k, 0:m], xT_h[:, k, :], xT_l[:, k, :],
                              k == 0, False)

                def low_rank(side, f):
                    m = f_rows(f)
                    hi, lo, yh, yl, ready = ((gb_h, gb_l, yg_h, yg_l, g_ps), (ub_h, ub_l, yu_h, yu_l, u_ps))[side]
                    cols = slice(f * P, f * P + m)
                    if f == 0:
                        pe.wait_ge(y_lo.sem, y_lo.at(b, side + 1))
                    three(held[side, f][0:m, :], hi[:, cols], lo[:, cols], yh[:, :], yl[:, :], False, True)\
                        .then_inc(ready.sem, 1)

                def project(f):
                    m, s = f_rows(f), f % 2
                    pe.wait_ge(hd_lo.sem, hd_lo.at(b, f + 1))
                    pe.wait_ge(d_lo.sem, d_lo.at(b, f + 1))
                    if f == 0 and not first:
                        pe.wait_ge(out_ready.sem, out_ready.at(b - 1, TT))
                    for tt in range(TT):
                        cols = slice(tt * P, (tt + 1) * P)
                        three(down[:, tt, :], hd_h[0:m, s, cols], hd_l[0:m, s, cols], d_h[0:m, s, :], d_l[0:m, s, :],
                              f == 0, False)
                    three(adps[0:LR, :], da_h[0:m, f, :], da_l[0:m, f, :], hd_h[0:m, s, :], hd_l[0:m, s, :],
                          f == 0, f == FT - 1).then_inc(tile_done.sem, 1)

                base(0, 0)
                base(1, 0)
                pe.wait_ge(wx_ready.sem, wx_ready.at(b, 1))
                for tt in range(TT):
                    mm = pe.transpose(adps[0:LR, tt * P:(tt + 1) * P], wx[:, tt, :], ident)
                mm.then_inc(wx_ps.sem, 1)
                base(0, 1)
                low_rank(0, 0)
                low_rank(1, 0)
                low_rank(0, 1)
                base(1, 1)
                low_rank(1, 1)
                project(0)
                for f in range(2, FT):
                    for side in range(2):
                        base(side, f)
                        low_rank(side, f)
                    project(f - 1)
                project(FT - 1)
                pe.wait_ge(y_lo.sem, y_lo.at(b, 3))
                for tt in range(TT):
                    cols = slice(tt * P, (tt + 1) * P)
                    three(down[:, tt, :], yg_h[:, cols], yg_l[:, cols], db_h[:, :], db_l[:, :], False, True)\
                        .then_inc(out_ps.sem, 1)

            batch(0, True)
            with pe.Fori(1, BATCH) as b:
                batch(b, False)

        @block.vector
        def _(dve):
            dve.wait_ge(f_c.sem, 32)
            dve.wait_ge(f_consts.sem, 3)
            for n, (_, raw, hi, lo) in enumerate(lora):
                dve.wait_ge(lora_hi.sem, n + 1)
                dve.tensor_tensor(lo, raw, hi.bitcast(F32), ALU.subtract).then_inc(lora_lo.sem, 1)

            def batch(b, first):
                link = Link(dve, dve_link, b)
                dve.wait_ge(x2_loaded.sem, x2_loaded.at(b, 16))
                for tt in range(TT):
                    ins = dve.bn_stats(stats[:, tt, :], x2_in[:, tt, :])
                link(ins)
                separate(dve, passed[2])
                for tt in range(TT):
                    ins = dve.bn_aggr(mv[:, tt, :], stats[:, tt, :])
                ins.then_inc(ln_stats.sem, 1)
                dve.wait_ge(ln_stats.sem, ln_stats.at(b, 1))
                dve.wait_ge(rstd_ready.sem, rstd_ready.at(b, 1))
                for tt in range(TT):
                    dve.tensor_scalar(x2_in[:, tt, :], x2_in[:, tt, :], mv[:, tt, 0:1], rstd[:, tt:tt + 1],
                                      ALU.subtract, ALU.mult).then_inc(xn_ready.sem, 1)
                for k in range(KT):
                    dve.wait_ge(xT_hi.sem, xT_hi.at(b, k + 1))
                    dve.tensor_tensor(xT_l[:, k, :], ring[k % 3][:, :], xT_h[:, k, :].bitcast(F32), ALU.subtract)\
                        .then_inc(xT_lo.sem, 1)
                dve.wait_ge(prob_tanh.sem, prob_tanh.at(b, 1))
                link(dve.tensor_scalar(prob[:, :, :], prob[:, :, :], 0.5, 0.5, ALU.mult, ALU.add))
                link(dve.tensor_tensor(biased[:, :, :], prob[:, :, :],
                                       bias_bc[:, :].unsqueeze(1).to_broadcast([P, TT, EXPERTS]), ALU.add))
                shape = [P, TT, EXPERTS, EXPERTS]
                others, own = biased[:, :, :].unsqueeze(2).to_broadcast(shape), biased[:, :, :].unsqueeze(3).to_broadcast(shape)
                dve.tensor_tensor(beats[:, :, :, :], others, own, ALU.is_gt)
                link(dve.tensor_tensor(ties[:, :, :, :], others, own, ALU.is_equal))
                pairs = ties[:, :, :, :].rearrange("p a e j -> p a (e j)")
                link(dve.tensor_tensor(pairs, pairs, lower.unsqueeze(1).to_broadcast([P, TT, EXPERTS * EXPERTS]), ALU.mult))
                link(dve.tensor_tensor(beats[:, :, :, :], beats[:, :, :, :], ties[:, :, :, :], ALU.add))
                link(dve.tensor_reduce(rank[:, :, :], beats[:, :, :, :], AX.X, ALU.add))
                link(dve.scalar_tensor_tensor(prob[:, :, :], rank[:, :, :], 1.5, prob[:, :, :], ALU.is_lt, ALU.mult))
                link(dve.tensor_reduce(wsum[:, 0, :], prob[:, :, :], AX.X, ALU.add))
                link(dve.tensor_scalar(wsum[:, 0, :], wsum[:, 0, :], 1e-8, float(RANK), ALU.add, ALU.mult))
                link(dve.reciprocal(wsum[:, 1, :], wsum[:, 0, :]))
                dve.tensor_tensor(wx[:, :, 0:ER].rearrange("p a (e r) -> p a e r", r=RANK),
                                  prob[:, :, :].unsqueeze(3).to_broadcast([P, TT, EXPERTS, RANK]),
                                  wsum[:, 1, :].unsqueeze(2).unsqueeze(3).to_broadcast([P, TT, EXPERTS, RANK]),
                                  ALU.mult).then_inc(wx_ready.sem, 1)
                dve.wait_ge(wxT_ready.sem, wxT_ready.at(b, 1))
                for n, (a, hi, lo) in enumerate(((a_gate, yg_h, yg_l), (a_up, yu_h, yu_l))):
                    dve.wait_ge(a_copied.sem, a_copied.at(b, n + 1))
                    dve.tensor_tensor(y[:, :], a[0:LR, :], wxT[:, :], ALU.mult).then_inc(y_ready.sem, 1)
                    dve.wait_ge(y_hi.sem, y_hi.at(b, n + 1))
                    dve.tensor_tensor(lo[:, :], y[:, :], hi[:, :].bitcast(F32), ALU.subtract).then_inc(y_lo.sem, 1)
                    dve.wait_ge(y_lo.sem, y_lo.at(b, n + 1))
                for f in range(FT):
                    m = f_rows(f)
                    dve.wait_ge(tanh_done.sem, tanh_done.at(b, f + 1))
                    dve.scalar_tensor_tensor(gated[0:m, :], th[0:m, :], 1.0, ring[(KT + 2 + 2 * f) % 3][0:m, :],
                                             ALU.add, ALU.mult).then_inc(gated_done.sem, 1)
                    dve.wait_ge(gated_done.sem, gated_done.at(b, f + 1))
                    dve.wait_ge(u_ps.sem, u_ps.at(b, f + 1))
                    if f:
                        dve.wait_ge(hd_lo.sem, hd_lo.at(b, f))
                    elif not first:
                        dve.wait_ge(hd_lo.sem, hd_lo.at(b - 1, FT))
                    dve.scalar_tensor_tensor(hd[0:m, :], gated[0:m, :], 0.5, ring[(KT + 3 + 2 * f) % 3][0:m, :],
                                             ALU.mult, ALU.mult).then_inc(hd_ready.sem, 1)
                dve.wait_ge(tile_done.sem, tile_done.at(b, FT))
                dve.tensor_tensor(y[:, :], adps[0:LR, :], wxT[:, :], ALU.mult).then_inc(y_ready.sem, 1)
                dve.wait_ge(y_hi.sem, y_hi.at(b, 3))
                dve.tensor_tensor(yg_l[:, :], y[:, :], yg_h[:, :].bitcast(F32), ALU.subtract).then_inc(y_lo.sem, 1)
                dve.wait_ge(res_loaded.sem, res_loaded.at(b, 16))
                for tt in range(TT):
                    dve.wait_ge(out_ps.sem, out_ps.at(b, tt + 1))
                    dve.tensor_tensor(x2_res[:, tt, :], down[:, tt, :], x2_res[:, tt, :], ALU.add)\
                        .then_inc(out_ready.sem, 1)
                link.done()

            batch(0, True)
            with dve.Fori(1, BATCH) as b:
                batch(b, False)


FF_DVE_LINKS = 1 + 10


def build(nc, arrays):
    ap = {n: nc.dram_tensor(n, a.shape, F32, kind="ExternalInput").ap() for n, a in arrays.items()}
    x2 = nc.dram_tensor("x2", (BATCH, T, D), F32, kind="Internal").ap()
    out = nc.dram_tensor("out", (BATCH, T, D), F32, kind="ExternalOutput").ap()
    attention_and_mlp(nc, ap["x"], ap["wqkvT"].rearrange("(k p) e -> p k e", p=P), ap["bq"], ap["bkv"],
                      ap["woT"].rearrange("(k p) e -> p k e", p=P), ap["bo"], ap["w"], ap["wT"], ap["d"], ap["dT"],
                      ap["consts"][:, 0:3, :], x2)
    feed_forward(nc, x2, ap["wg"].rearrange("(k p) f -> p k f", p=P), ap["wu"].rearrange("(k p) f -> p k f", p=P),
                 ap["wd"], ap["ga"], ap["ua"], ap["da"], ap["gb"], ap["ub"], ap["db"], ap["expert_bias"],
                 ap["consts"], out)


def kernel(x, fside_BxS2xS2_0, ctx_1024, L0_attn_Wqkv_w, L0_attn_Wqkv_b, L0_attn_out_w, L0_attn_out_b,
           L0_ffn_W_router, L0_ffn_W_gate, L0_ffn_W_up, L0_ffn_W_down, L0_ffn_sA_gate, L0_ffn_sB_gate,
           L0_ffn_sA_up, L0_ffn_sB_up, L0_ffn_sA_down, L0_ffn_sB_down, L0_ffn_A_gate, L0_ffn_B_gate,
           L0_ffn_A_up, L0_ffn_B_up, L0_ffn_A_down, L0_ffn_B_down, L0_ffn_expert_bias):
    import concourse.bacc as bacc
    from concourse.bass_utils import run_bass_kernel_spmd

    def host(a):
        return np.ascontiguousarray(np.asarray(a))

    def lora_in(routed, shared, *more):
        routed = host(routed)
        return host(np.concatenate([routed.transpose(1, 0, 2).reshape(routed.shape[1], ER), host(shared), *more], axis=1))

    def lora_out(routed, shared):
        return host(np.concatenate([host(routed).reshape(ER, -1), host(shared)], axis=0))

    consts = np.zeros((P, 4, P), np.float32)
    consts[:, 0, :] = np.eye(P, dtype=np.float32)
    consts[:, 1, :] = np.triu(np.full((P, P), NEG, np.float32), 1)
    consts[:, 2, :] = np.tril(np.full((P, P), NEG, np.float32), -1)
    consts[:, 3, 0:EXPERTS * EXPERTS] = np.tril(np.ones((EXPERTS, EXPERTS), np.float32), -1).reshape(-1)
    bqkv = host(L0_attn_Wqkv_b)
    arrays = {
        "x": host(x), "wqkvT": host(host(L0_attn_Wqkv_w).T), "woT": host(host(L0_attn_out_w).T),
        "bq": host(bqkv[0:D].reshape(KT, P).T), "bkv": host(bqkv[D:QKV].reshape(2 * HD, 1)), "bo": host(L0_attn_out_b),
        "w": host(fside_BxS2xS2_0), "wT": host(host(fside_BxS2xS2_0).transpose(0, 2, 1)),
        "d": host(ctx_1024), "dT": host(host(ctx_1024).transpose(0, 2, 1)),
        "wg": host(L0_ffn_W_gate), "wu": host(L0_ffn_W_up), "wd": host(L0_ffn_W_down),
        "ga": lora_in(L0_ffn_A_gate, L0_ffn_sA_gate, np.zeros((D, ROUTE - LR), np.float32), host(L0_ffn_W_router)),
        "ua": lora_in(L0_ffn_A_up, L0_ffn_sA_up), "da": lora_in(L0_ffn_A_down, L0_ffn_sA_down),
        "gb": lora_out(L0_ffn_B_gate, L0_ffn_sB_gate), "ub": lora_out(L0_ffn_B_up, L0_ffn_sB_up),
        "db": lora_out(L0_ffn_B_down, L0_ffn_sB_down), "expert_bias": host(L0_ffn_expert_bias), "consts": consts,
    }
    nc = bacc.Bacc("TRN2", target_bir_lowering=False, num_devices=1)
    build(nc, arrays)
    got = run_bass_kernel_spmd(nc, [arrays], core_ids=[0])
    return got.results[0]["out"]
```

```python
from contextlib import ExitStack

import numpy as np

import concourse.bass as bass
from concourse import mybir

F32 = mybir.dt.float32
F32R = mybir.dt.float32r
BF16 = mybir.dt.bfloat16
ALU = mybir.AluOpType
ACT = mybir.ActivationFunctionType
AX = mybir.AxisListType

P = 128
BATCH, T, D = 4, 512, 512
HEADS, HD = 16, 32
KT = D // P
TT = T // P
QKV = D + 2 * HD
INNER = 256
IT = INNER // P
DFF, RANK, EXPERTS = 1376, 8, 8
FT = -(-DFF // P)
FLAST = DFF - (FT - 1) * P
ER = EXPERTS * RANK
LR = ER + RANK
ROUTE = 96
LA = ROUTE + EXPERTS
LN_EPS, QEPS, QMAX = 1e-5, 1e-6, 127.0
MAGIC = 1.5 * 2.0 ** 23
NEG = -1e38
SCALE = HD ** -0.5
KROWS = 3 * HD


MLP_LINKS = 1 + 2 * (3 + 1 + 1 + 4) + 1


def f_rows(f):
    return P if f < FT - 1 else FLAST


class Signal:

    def __init__(self, ctx, nc, name, per):
        self.sem, self.per = ctx.enter_context(nc.semaphore(name)), per

    def at(self, b, n):
        assert 1 <= n <= self.per
        return b * self.per + n


class Link:

    def __init__(self, eng, signal, b):
        self.eng, self.chain, self.b, self.n = eng, signal, b, 0

    def __call__(self, ins):
        self.n += 1
        ins.then_inc(self.chain.sem, 1)
        self.eng.wait_ge(self.chain.sem, self.chain.at(self.b, self.n))

    def done(self):
        assert self.n == self.chain.per, (self.n, self.chain.per)


def separate(eng, passed):
    eng.sem_inc(passed.sem, 1)


class Tenants:

    def __init__(self, slots):
        self.slots, self.last, self.n = slots, {}, 0

    def new_batch(self, first):
        self.n, self.old, self.last = 0, dict(self.last), {}

    def claim(self, eng, b, signal, count, ahead=0):
        slot = self.n % self.slots
        self.n += 1
        if slot in self.last:
            before, at, next_one = self.last[slot]
            eng.wait_ge(before.sem, before.at(b + next_one, at))
        elif slot in self.old:
            before, at, next_one = self.old[slot]
            eng.wait_ge(before.sem, before.at(b - 1 + next_one, at))
        self.last[slot] = (signal, count, ahead)
        return slot


MAX_GROUPS = ((0, 0, 4), (1, 0, 4), (2, 0, 2), (2, 2, 2), (3, 0, 2), (3, 2, 2))
MG = len(MAX_GROUPS)
MAX_AMONG = (((1, 3), (1, 4), (1, 5)), (), ((2, 0), (2, 1)), ((2, 2),))
MAX_BEFORE = (0, 1, 2)
LN1_STEP = 10
ROWS_STEP = 2


def maxima_among(g, idx):
    return [(g + ahead, i) for ahead, i in MAX_AMONG[idx] if g + ahead < 4]


def slots_of_tenants():
    order = [("xT", 0), ("xT", 1), ("kv",), ("q", 0), ("q", 1), ("v",)]
    order += [("max", 0, i) for i in range(MG)] + [("rows", 0)] + [("max", 1, i) for i in MAX_BEFORE]
    for g in range(4):
        for idx in range(TT):
            if idx == ROWS_STEP and g < 3:
                order.append(("rows", g + 1))
            order += [("scores", TT * g + idx, 0), ("scores", TT * g + idx, 1)]
            order += [("max", *key) for key in maxima_among(g, idx)]
    order += [("out", 0), ("out", 1)]
    return {key: n % 2 for n, key in enumerate(order)}


SLOT = slots_of_tenants()

MLP_AMONG = {
    ('q', 0): ((0, 'stats'),),
    ('q', 1): ((0, 'normalise'),),
    ('q', 2): ((0, 'xmax'),),
    ('q', 3): ((0, 'turn'),),
    ('max', 0): ((0, 'colmax'),),
    ('max', 2): ((0, 'ratio'),),
    ('max', 4): ((0, 's_cols'),),
    ('max', 5): ((0, 's_rows_ps'),),
    ('exp', 0, 0): ((0, 's_rows'),),
    ('exp', 0, 2): ((0, 'scale'),),
    ('exp', 2, 1): ((0, 'rowmax_a'),),
    ('exp', 2, 2): ((0, 'rowmax_w'),),
    ('exp', 3, 1): ((0, 'round_a'),),
    ('exp', 3, 2): ((0, 'integer_a'),),
    ('exp', 4, 0): ((0, 'round_w'),),
    ('exp', 4, 1): ((0, 'turn_a'),),
    ('exp', 4, 2): ((0, 'copy_a'),),
    ('exp', 5, 1): ((0, 'turn_w'),),
    ('exp', 5, 2): ((0, 'copy_w'),),
    ('exp', 6, 0): ((0, 'w_row_ps'),),
    ('exp', 6, 1): ((0, 'w_row'),),
    ('exp', 6, 2): ((0, 'product0'),),
    ('exp', 7, 0): ((0, 'undo0'),),
    ('exp', 7, 1): ((0, 'product1'),),
    ('exp', 7, 2): ((0, 'undo1'),),
    ('exp', 8, 0): ((1, 'tanh'), (1, 'wmax'), (1, 'act')),
    ('exp', 8, 2): ((1, 'xmax'),),
    ('exp', 9, 1): ((1, 'turn'),),
    ('exp', 9, 2): ((1, 'colmax'),),
    ('exp', 10, 0): ((1, 'ratio'),),
    ('exp', 10, 2): ((1, 's_cols'),),
    ('exp', 11, 0): ((1, 's_rows_ps'), (1, 's_rows')),
    ('exp', 11, 1): ((1, 'scale'),),
    ('exp', 11, 2): ((1, 'rowmax_a'), (1, 'rowmax_w')),
    ('exp', 12, 0): ((1, 'round_a'),),
    ('exp', 12, 1): ((1, 'integer_a'), (1, 'round_w')),
    ('exp', 12, 2): ((1, 'turn_a'), (1, 'copy_a')),
    ('exp', 13, 2): ((1, 'turn_w'), (1, 'copy_w')),
    ('exp', 14, 0): ((1, 'w_row_ps'),),
    ('exp', 14, 1): ((1, 'w_row'),),
    ('exp', 14, 2): ((1, 'product0'), (1, 'undo0')),
    ('exp', 15, 1): ((1, 'product1'),),
    ('exp', 15, 2): ((1, 'undo1'), (1, 'residual')),
}


def mlp_among(mlp, c, *where):
    if c is not None:
        for n, step in MLP_AMONG.get(where, ()):
            mlp(c, n, step)


def mlp_alone(mlp, c):
    for steps in MLP_AMONG.values():
        for n, step in steps:
            mlp(c, n, step)


def attention_and_mlp(nc, x, wqkv, bq, bkv, wo, bo, mlp_w, mlp_d, consts, x2):
    with ExitStack() as ctx:
        def sb(name, shape, dt=F32):
            return ctx.enter_context(nc.sbuf_tensor(name, shape, dt))

        def sig(name, per=1):
            return Signal(ctx, nc, name, per)

        cst = sb("cst", [P, 3, P])
        ident = cst[:, 0, :]
        mask_bf = sb("mask_bf", [P, 3, P], BF16)
        ones = sb("ones", [P, HD])
        half = sb("half", [P, 2 * KT])
        ln_eps = sb("ln_eps", [P, TT])
        wqkv_h, wqkv_l = sb("wqkv_h", [P, KT, QKV], F32R), sb("wqkv_l", [P, KT, QKV], F32R)
        wo_h, wo_l = sb("wo_h", [P, KT, D], F32R), sb("wo_l", [P, KT, D], F32R)
        bq_sb, bkv_sb = sb("bq_sb", [P, KT]), sb("bkv_sb", [2 * HD, 1])
        bo_bc = sb("bo_bc", [P, D])
        x_in = sb("x_in", [P, TT, D])
        stats, mv = sb("stats", [P, 2, TT, 6]), sb("mv", [P, 2, TT, 2])
        veps, rstd = sb("veps", [P, 2, TT]), sb("rstd", [P, 2, TT])
        hT_h, hT_l = sb("hT_h", [P, KT, T], F32R), sb("hT_l", [P, KT, T], F32R)
        with ExitStack() as early:
            qT_h = early.enter_context(nc.sbuf_tensor("qT_h", [P, KT, T], F32R))
            qT_l = early.enter_context(nc.sbuf_tensor("qT_l", [P, KT, T], F32R))
        probs = sb("probs", [P, 4, 2, T])
        kst = sb("kst", [P, T], F32R)
        qst = sb("qst", [P, HEADS, T], F32R)
        v = sb("v", [P, TT, HD])
        negm = sb("negm", [P, HEADS, TT])
        negm_h, negm_l = sb("negm_h", [4 * TT, 4, P], F32R), sb("negm_l", [4 * TT, 4, P], F32R)
        rden, cx = sb("rden", [P, T]), sb("cx", [P, 2, T])
        vT = rden
        x1 = sb("x1", [P, TT, D])
        xn = sb("xn", [P, TT, D])
        w_raw, d_raw = sb("w_raw", [P, TT, D]), sb("d_raw", [P, TT, INNER])
        hid = sb("hid", [P, TT, D])
        th = sb("th", [P, TT, INNER])[:, :, :]
        a_bf, wT_bf, aT_bf = sb("a_bf", [P, TT, D], BF16), sb("wT_bf", [P, KT, D], BF16), sb("aT_bf", [P, KT, D], BF16)
        w_bf = a_bf
        tile_max = sb("tile_max", [P, 2, D])
        amax, sc = sb("amax", [P, 2, KT]), sb("sc", [P, 5, KT])
        rows, wrow = sb("rows", [P, 2, D]), sb("wrow", [P, D])
        qm, qs, qi = sb("qm", [P, 2, TT]), sb("qs", [P, 2, TT]), sb("qi", [P, 2, TT])

        slots = [ctx.enter_context(nc.psum_tensor(f"slot{i}", [P, 2, T], F32)) for i in range(2)]
        mlp_ps = ctx.enter_context(nc.psum_tensor("mlp_ps", [P, 2, T], F32))
        mlp_ps_bf = mlp_ps[:, :, :].bitcast(BF16)
        av = ctx.enter_context(nc.psum_tensor("av", [P, T], F32))
        den = ctx.enter_context(nc.psum_tensor("den", [P, T], F32))

        c_loaded, w_loaded = sig("c_loaded"), [sig(f"w_loaded{i}") for i in range(3)]
        masks_ready, consts_ready = sig("masks_ready"), sig("consts_ready", 5)
        w_hi, w_lo = sig("w_hi", 8), sig("w_lo", 8)
        x_loaded, res_loaded = sig("x_loaded", 16), sig("xres_loaded", 16)
        ln_stats, rstd_ready, xn_ready = sig("ln_stats"), sig("rstd_ready"), sig("xn_ready", TT)
        xT_ps, xT_hi, xT_lo = sig("xT_ps", 2), sig("xT_hi", 2), sig("xT_lo", 2)
        xb_ready = sig("xb_ready")
        kv_ps, kv_act, kv_lo = sig("kv_ps"), sig("kv_act", 3), sig("kv_lo")
        q_ps, q_hi, q_lo = sig("q_ps", KT), sig("q_hi", KT), sig("q_lo", KT)
        v_ps, v_ready = sig("v_ps"), sig("v_ready")
        q_moved = [sig(f"q_moved{i}", 16 * 12) for i in range(2)]
        s_ps, s_max = sig("s_ps", 4 * MG), sig("s_max", 4 * MG)
        m_ps, m_hi, m_lo = sig("m_ps", 4), sig("m_hi", 4), sig("m_lo", 4)
        m_moved = [sig(f"m_moved{i}", 32) for i in range(4)]
        t_ps, p_ready, pv_done = sig("t_ps", 32), sig("p_ready", 32), sig("pv_done", 16)
        av_out, den_out, rden_ready = sig("av_out", 4), sig("den_out", 4), sig("rden_ready", 5)
        cx_ready, cx_hi, cx_lo = sig("cx_ready", 5), sig("cx_hi", 5), sig("cx_lo", 5)
        o_ps, x1_ready = sig("o_ps", 2), sig("x1_ready", 2)
        ln_link = sig("ln_link")
        mw_loaded, md_loaded = sig("mw_loaded", 16), sig("md_loaded", 16)
        ln2_stats, rstd2_ready, xn2_ready = sig("ln2_stats"), sig("rstd2_ready"), sig("xn2_ready", TT)
        tile_max_ready, turned = sig("tile_max_ready", 2), sig("turned", 2)
        ratio, root, s_cols = sig("ratio", 2), sig("root", 2), sig("s_cols", 2)
        s_rows_ps, s_rows = sig("s_rows_ps", 2), sig("s_rows", 2)
        w_scaled, q_scale = sig("w_scaled", 2), sig("q_scale", 4)
        rounded, a_q, w_q = sig("rounded", 16), sig("a_q", 2), sig("w_q", 2)
        aq_ps, aqT, wq_ps, wqT = sig("aq_ps", 2), sig("aqT", 2), sig("wq_ps", 2), sig("wqT", 2)
        wrow_ps, wrow_ready = sig("wrow_ps", 2), sig("wrow_ready", 2)
        h_ps, h_ready, th_ready, act_ready = sig("h_ps", 4), sig("h_ready", 8), sig("th_ready"), sig("act_ready")
        x2_ready, x2_stored = sig("x2_ready", TT), sig("x2_stored", 16)
        mlp_link, pool_link = sig("mlp_link", MLP_LINKS), [sig("pool_link1"), sig("pool_link2")]
        passed = [sig(f"passed_{e}") for e in ("sp", "pe", "dve")]

        hid_flat, d_flat = hid[:, :, :].rearrange("p a d -> p (a d)"), d_raw[:, :, :].rearrange("p a d -> p (a d)")
        wq_stage, wq_last = hid_flat[:, 0:3 * QKV].rearrange("p (k n) -> p k n", n=QKV), d_flat[:, 0:QKV]
        weights = ([(wq_stage[:, k, :], wqkv_h[:, k, :], wqkv_l[:, k, :], 0) for k in range(3)]
                   + [(wq_last, wqkv_h[:, 3, :], wqkv_l[:, 3, :], 1)]
                   + [(w_raw[:, k, :], wo_h[:, k, :], wo_l[:, k, :], 2) for k in range(KT)])
        products = ((KT, D, xn, w_raw), (IT, INNER, hid[:, :, 0:INNER], d_raw))

        block = ctx.enter_context(nc.Block())

        @block.sync
        def _(sp):
            def load_x(b):
                return sp.dma_start(x_in[:, :, :], x[b].rearrange("(a p) d -> p a d", p=P))

            load_x(0).then_inc(x_loaded.sem, 16)
            sp.dma_start(cst[:, :, :], consts).then_inc(c_loaded.sem, 16)
            sp.dma_start(wq_stage, wqkv[:, 0:3, :]).then_inc(w_loaded[0].sem, 16)
            sp.dma_start(wq_last, wqkv[:, 3, :]).then_inc(w_loaded[1].sem, 16)
            sp.dma_start(bq_sb[:, :], bq).then_inc(c_loaded.sem, 16)
            sp.dma_start(bkv_sb[:, :], bkv).then_inc(c_loaded.sem, 16)
            sp.dma_start(bo_bc[:, :], bo.partition_broadcast(P)).then_inc(c_loaded.sem, 16)
            sp.dma_start(w_raw[:, :, :], wo).then_inc(w_loaded[2].sem, 16)

            def batch(b, first, last):
                qst_by_quadrant = qst[:, :, :].rearrange("p (e j) t -> p e j t", j=4)
                for ep in range(2):
                    if not first:
                        sp.wait_ge(pv_done.sem, pv_done.at(b - 1, 16))
                        separate(sp, passed[0])
                    sp.wait_ge(q_hi.sem, q_hi.at(b, 2 * ep + 2))
                    sp.wait_ge(q_lo.sem, q_lo.at(b, 2 * ep + 2))
                    for j in range(4):
                        for src, row in ((qT_h, 0), (qT_l, HD), (qT_h, 2 * HD)):
                            sp.dma_start(qst_by_quadrant[row:row + HD, 2 * ep:2 * ep + 2, j, :].bitcast(F32),
                                         src[HD * j:HD * j + HD, 2 * ep:2 * ep + 2, :].bitcast(F32))\
                              .then_inc(q_moved[ep].sem, 16)
                if not last:
                    sp.wait_ge(xT_ps.sem, xT_ps.at(b, 2))
                    load_x(b + 1).then_inc(x_loaded.sem, 16)
                for g in range(4):
                    if g == 2:
                        if not first:
                            sp.wait_ge(a_q.sem, a_q.at(b - 1, 1))
                        sp.dma_start(xn[:, :, :], x[b].rearrange("(a p) d -> p a d", p=P)).then_inc(res_loaded.sem, 16)
                    if g == 3:
                        if first:
                            sp.wait_ge(w_lo.sem, 8)
                        else:
                            sp.wait_ge(w_q.sem, w_q.at(b - 1, 1))
                        sp.dma_start(w_raw[:, :, :], mlp_w[b].rearrange("(a p) d -> p a d", p=P))\
                          .then_inc(mw_loaded.sem, 16)
                    sp.wait_ge(m_hi.sem, m_hi.at(b, g + 1))
                    sp.wait_ge(m_lo.sem, m_lo.at(b, g + 1))
                    for src, row in ((negm_h, KROWS), (negm_l, KROWS + 1)):
                        sp.dma_start(qst[row:row + 1, 4 * g:4 * g + 4, :].bitcast(F32), src[:, g, :].bitcast(F32))\
                          .then_inc(m_moved[g].sem, 16)
                if not first:
                    sp.wait_ge(w_q.sem, w_q.at(b - 1, 2))
                    sp.wait_ge(x2_stored.sem, x2_stored.at(b - 1, 16))
                sp.dma_start(d_raw[:, :, :], mlp_d[b].rearrange("(a p) d -> p a d", p=P)).then_inc(md_loaded.sem, 16)

            batch(0, True, False)
            with sp.Fori(1, BATCH - 1) as b:
                batch(b, False, False)
            batch(BATCH - 1, False, True)

        @block.gpsimd
        def _(pool):
            for n, (dst, value) in enumerate(((ones[:, :], 1.0), (half[:, 0:KT], 0.5), (half[:, KT:2 * KT], -0.5),
                                              (kst[KROWS:P, :].bitcast(F32), 1.0), (ln_eps[:, :], LN_EPS))):
                pool.memset(dst, value).then_inc(consts_ready.sem, 1)
                pool.wait_ge(consts_ready.sem, n + 1)

            def inverse_deviation(c, n, stats_ready, link, ready):
                pool.wait_ge(stats_ready.sem, stats_ready.at(c, 1))
                pool.tensor_tensor(veps[:, n, :], mv[:, n, :, 1], ln_eps[:, :], ALU.add).then_inc(link.sem, 1)
                pool.wait_ge(link.sem, link.at(c, 1))
                pool.tensor_tensor(rstd[:, n, :], veps[:, n, :], half[:, KT:2 * KT], ALU.pow).then_inc(ready.sem, 1)

            def mlp(c, n, step):
                nk, width, _, raw = products[n]
                if step == "stats":
                    inverse_deviation(c, 1, ln2_stats, pool_link[1], rstd2_ready)
                if step == "ratio":
                    pool.wait_ge(ratio.sem, ratio.at(c, n + 1))
                    pool.tensor_tensor(sc[:, 2, 0:nk], sc[:, 1, 0:nk], half[:, 0:nk], ALU.pow).then_inc(root.sem, 1)
                if step == "scale":
                    loaded = (mw_loaded, md_loaded)[n]
                    pool.wait_ge(s_rows.sem, s_rows.at(c, n + 1))
                    pool.wait_ge(loaded.sem, loaded.at(c, 16))
                    pool.tensor_tensor(raw[:, :, :], raw[:, :, :],
                                       rows[:, 0, 0:width].unsqueeze(1).to_broadcast([P, TT, width]),
                                       ALU.mult).then_inc(w_scaled.sem, 1)
                if n == 1 and step in ("product1", "residual"):
                    for tt in ((0, 1) if step == "product1" else (2, 3)):
                        pool.wait_ge(h_ready.sem, h_ready.at(c, TT + tt + 1))
                        pool.tensor_tensor(hid[:, tt, :], hid[:, tt, :], x1[:, tt, :], ALU.add).then_inc(x2_ready.sem, 1)

            def batch(b, c, first, last):
                if first:
                    inverse_deviation(b, 0, ln_stats, pool_link[0], rstd_ready)
                    for n, (raw, hi, lo, _) in enumerate(weights):
                        pool.wait_ge(w_hi.sem, n + 1)
                        pool.tensor_tensor(lo, raw, hi.bitcast(F32), ALU.subtract).then_inc(w_lo.sem, 1)
                for e in range(KT):
                    mlp_among(mlp, c, "q", e)
                for i in range(MG):
                    mlp_among(mlp, c, "max", i)
                for step in range(16):
                    for part in range(3):
                        mlp_among(mlp, c, "exp", step, part)
                    if step >= 7 and step % 4 == 3:
                        low_context(b, (step - 7) // 4)
                    if step == 10:
                        pool.wait_ge(res_loaded.sem, res_loaded.at(b, 16))
                        pool.tensor_tensor(xn[:, :, :], xn[:, :, :], bo_bc[:, :].unsqueeze(1).to_broadcast([P, TT, D]),
                                           ALU.add).then_inc(xb_ready.sem, 1)
                    if step == LN1_STEP and not last:
                        inverse_deviation(b + 1, 0, ln_stats, pool_link[0], rstd_ready)
                for hf in range(2):
                    low_context(b, 3, hf)

            def low_context(b, g, hf=None):
                cols = slice(0, T) if hf is None else slice(T // 2 * hf, T // 2 * (hf + 1))
                pool.wait_ge(cx_hi.sem, cx_hi.at(b, g + 1 + (hf or 0)))
                pool.tensor_tensor(hT_l[:, g, cols], cx[:, g % 2, cols], hT_h[:, g, cols].bitcast(F32), ALU.subtract)\
                    .then_inc(cx_lo.sem, 1)

            pool.wait_ge(c_loaded.sem, 64)
            batch(0, None, True, False)
            with pool.Fori(1, BATCH - 1) as b:
                batch(b, b - 1, False, False)
            batch(BATCH - 1, BATCH - 2, False, True)
            mlp_alone(mlp, BATCH - 1)

        @block.scalar
        def _(act):
            act.wait_ge(c_loaded.sem, 64)
            act.activation(mask_bf[:, :, :], cst[:, :, :], ACT.Copy).then_inc(masks_ready.sem, 1)
            for raw, hi, _, part in weights:
                act.wait_ge(w_loaded[part].sem, 16)
                act.activation(hi, raw, ACT.Copy).then_inc(w_hi.sem, 1)

            def mlp(c, n, step):
                nk, width, a, w = products[n]
                if step == "tanh":
                    act.wait_ge(h_ready.sem, h_ready.at(c, TT))
                    act.activation(th, hid[:, :, 0:INNER], ACT.Tanh, scale=0.5).then_inc(th_ready.sem, 1)
                if step == "s_rows":
                    act.wait_ge(s_rows_ps.sem, s_rows_ps.at(c, n + 1))
                    act.activation(rows[:, :, 0:width], mlp_ps[:, :, 0:width], ACT.Copy).then_inc(s_rows.sem, 1)
                if step in ("round_a", "round_w"):
                    i, y = (0, a) if step == "round_a" else (1, w)
                    act.wait_ge(q_scale.sem, q_scale.at(c, 2 * n + i + 1))
                    for tt in range(TT):
                        act.activation(y[:, tt, :], y[:, tt, :], ACT.Copy, scale=qi[:, i, tt:tt + 1], bias=MAGIC)\
                            .then_inc(rounded.sem, 1)
                if step in ("copy_a", "copy_w"):
                    turned_, dst, ready = (aq_ps, aT_bf, aqT) if step == "copy_a" else (wq_ps, wT_bf, wqT)
                    act.wait_ge(turned_.sem, turned_.at(c, n + 1))
                    act.activation(dst[:, 0:nk, :],
                                   mlp_ps_bf[:, 0:(nk + 1) // 2, :].rearrange("p a (c t) -> p (a c) t", c=2),
                                   ACT.Copy).then_inc(ready.sem, 1)
                if step == "w_row":
                    act.wait_ge(wrow_ps.sem, wrow_ps.at(c, n + 1))
                    act.activation(wrow[:, :], mlp_ps[:, 0, :], ACT.Copy).then_inc(wrow_ready.sem, 1)
                if step == "residual":
                    act.wait_ge(x2_ready.sem, x2_ready.at(c, TT))
                    act.dma_start(x2[c].rearrange("(a p) d -> p a d", p=P), hid[:, :, :]).then_inc(x2_stored.sem, 16)

            def batch(b, c, first, last):
                for s in range(2):
                    act.wait_ge(xT_ps.sem, xT_ps.at(b, s + 1))
                    if not first and s == 0:
                        act.wait_ge(o_ps.sem, o_ps.at(b - 1, 2))
                    act.activation(hT_h[:, 2 * s:2 * s + 2, :], slots[SLOT["xT", s]][:, :, :], ACT.Copy).then_inc(xT_hi.sem, 1)
                act.wait_ge(kv_ps.sem, kv_ps.at(b, 1))
                kv = slots[SLOT["kv",]]
                act.activation(kst[0:HD, :], kv[0:HD, 0, :], ACT.Identity, bias=bkv_sb[0:HD, :]).then_inc(kv_act.sem, 1)
                act.activation(kst[HD:2 * HD, :], kv[0:HD, 0, :], ACT.Identity, bias=bkv_sb[0:HD, :])\
                    .then_inc(kv_act.sem, 1)
                act.activation(vT[HD:2 * HD, :], kv[HD:2 * HD, 0, :], ACT.Identity, bias=bkv_sb[HD:2 * HD, :])\
                    .then_inc(kv_act.sem, 1)
                for e in range(KT):
                    ps = slots[SLOT["q", e // 2]]
                    act.wait_ge(q_ps.sem, q_ps.at(b, e + 1))
                    act.activation(qT_h[:, e, :], ps[:, e % 2, :], ACT.Identity, bias=bq_sb[:, e:e + 1])\
                        .then_inc(q_hi.sem, 1)
                    mlp_among(mlp, c, "q", e)

                def high_maxima(g):
                    act.wait_ge(m_ps.sem, m_ps.at(b, g + 1))
                    if not first:
                        act.wait_ge(m_moved[g].sem, m_moved[g].at(b - 1, 32))
                    act.activation(negm_h[:, g, :], slots[SLOT["rows", g]][0:4 * TT, 0, 0:P], ACT.Copy).then_inc(m_hi.sem, 1)

                for i in range(MG):
                    mlp_among(mlp, c, "max", i)
                high_maxima(0)

                def sums_out(g):
                    act.wait_ge(pv_done.sem, pv_done.at(b, 4 * g + 4))
                    if g:
                        act.wait_ge(cx_ready.sem, cx_ready.at(b, g))
                    act.activation(rden[:, :], den[:, :], ACT.Copy).then_inc(den_out.sem, 1)

                def high_context(g, hf=None):
                    cols = slice(0, T) if hf is None else slice(T // 2 * hf, T // 2 * (hf + 1))
                    act.wait_ge(cx_ready.sem, cx_ready.at(b, g + 1 + (hf or 0)))
                    act.activation(hT_h[:, g, cols], cx[:, g % 2, cols], ACT.Copy).then_inc(cx_hi.sem, 1)

                step = 0
                for g in range(4):
                    for kt in reversed(range(TT)):
                        if kt == TT - 1 - ROWS_STEP and g < 3:
                            high_maxima(g + 1)
                        for pr in range(2):
                            act.wait_ge(t_ps.sem, t_ps.at(b, 2 * step + pr + 1))
                            if step >= 2:
                                act.wait_ge(pv_done.sem, pv_done.at(b, step - 1))
                            n = T - kt * P
                            act.activation(probs[:, 2 * (step % 2) + pr, :, 0:n],
                                           slots[SLOT["scores", step, pr]][:, :, 0:n], ACT.Exp, scale=SCALE).then_inc(p_ready.sem, 1)
                        mlp_among(mlp, c, "exp", step, 0)
                        if g and kt == TT - 1:
                            sums_out(g - 1)
                        if g and kt == 1:
                            high_context(g - 1)
                        mlp_among(mlp, c, "exp", step, 1)
                        mlp_among(mlp, c, "exp", step, 2)
                        step += 1
                sums_out(3)
                for hf in range(2):
                    high_context(3, hf)

            batch(0, None, True, False)
            with act.Fori(1, BATCH - 1) as b:
                batch(b, b - 1, False, False)
            batch(BATCH - 1, BATCH - 2, False, True)
            mlp_alone(mlp, BATCH - 1)
            act.wait_ge(x2_stored.sem, 16 * BATCH)

        @block.tensor
        def _(pe):
            tenants = Tenants(2)
            pe.wait_ge(c_loaded.sem, 64)
            pe.wait_ge(masks_ready.sem, 1)
            pe.wait_ge(consts_ready.sem, 5)

            def three(out, w_hi_, w_lo_, m_hi_, m_lo_, start, stop):
                pe.matmul(out, w_hi_, m_hi_, start=start, stop=False)
                pe.matmul(out, w_hi_, m_lo_, start=False, stop=False)
                return pe.matmul(out, w_lo_, m_hi_, start=False, stop=stop)

            def mlp(c, n, step):
                nk = products[n][0]
                if step == "turn":
                    pe.wait_ge(tile_max_ready.sem, tile_max_ready.at(c, n + 1))
                    for i in range(2):
                        for k in range(nk):
                            mm = pe.transpose(mlp_ps[:, i, k * P:(k + 1) * P], tile_max[:, i, k * P:(k + 1) * P], ident)
                    mm.then_inc(turned.sem, 1)
                if step == "s_rows_ps":
                    pe.wait_ge(s_cols.sem, s_cols.at(c, n + 1))
                    for i in range(2):
                        for k in range(nk):
                            mm = pe.transpose(mlp_ps[:, i, k * P:(k + 1) * P],
                                              sc[:, 3 + i, k:k + 1].to_broadcast([P, P]), ident)
                    mm.then_inc(s_rows_ps.sem, 1)
                if step in ("turn_a", "turn_w"):
                    src, quantised, turned_, free = ((a_bf, a_q, aq_ps, s_rows) if step == "turn_a"
                                                     else (w_bf, w_q, wq_ps, aqT))
                    pe.wait_ge(free.sem, free.at(c, n + 1))
                    pe.wait_ge(quantised.sem, quantised.at(c, n + 1))
                    for k in range(nk):
                        for tt in range(TT):
                            at = (k % 2) * T + tt * P
                            mm = pe.transpose(mlp_ps_bf[:, k // 2, at:at + P], src[:, tt, k * P:(k + 1) * P],
                                              mask_bf[:, 0, :])
                    mm.then_inc(turned_.sem, 1)
                if step == "w_row_ps":
                    pe.wait_ge(wqT.sem, wqT.at(c, n + 1))
                    for ot in range(TT):
                        mm = pe.transpose(mlp_ps[:, 0, ot * P:(ot + 1) * P], qs[:, 1, ot:ot + 1].to_broadcast([P, P]),
                                          ident)
                    mm.then_inc(wrow_ps.sem, 1)
                if step in ("product0", "product1"):
                    s = int(step[-1])
                    if s:
                        pe.wait_ge(h_ready.sem, h_ready.at(c, TT * n + 2))
                    else:
                        pe.wait_ge(wrow_ready.sem, wrow_ready.at(c, n + 1))
                    for j in range(2):
                        tt = 2 * s + j
                        for k in range(nk):
                            mm = pe.matmul(mlp_ps[:, j, :], aT_bf[:, k, tt * P:(tt + 1) * P], wT_bf[:, k, :],
                                           start=(k == 0), stop=(k == nk - 1))
                    mm.then_inc(h_ps.sem, 1)

            def batch(b, c, first, last):
                tenants.new_batch(first)

                def claim(freed, count, *key):
                    assert tenants.n % 2 == SLOT[key], key
                    return slots[tenants.claim(pe, b, freed, count)]

                for s in range(2):
                    ps = claim(xT_lo, s + 1, "xT", s)
                    for j in range(2):
                        for tt in range(TT):
                            if s == 0 and j == 0:
                                pe.wait_ge(xn_ready.sem, xn_ready.at(b, tt + 1))
                            k = 2 * s + j
                            mm = pe.transpose(ps[:, j, tt * P:(tt + 1) * P], x_in[:, tt, k * P:(k + 1) * P], ident)
                    mm.then_inc(xT_ps.sem, 1)
                ps = claim(kv_lo, 1, "kv")
                for k in range(KT):
                    if k % 2 == 0:
                        pe.wait_ge(xT_lo.sem, xT_lo.at(b, k // 2 + 1))
                    if first:
                        pe.wait_ge(w_lo.sem, k + 1)
                    mm = three(ps[0:2 * HD, 0, :], wqkv_h[:, k, D:QKV], wqkv_l[:, k, D:QKV], hT_h[:, k, :], hT_l[:, k, :],
                               k == 0, k == KT - 1)
                mm.then_inc(kv_ps.sem, 1)
                for e in range(KT):
                    if e % 2 == 0:
                        ps = claim(q_lo, e + 2, "q", e // 2)
                    for k in range(KT):
                        mm = three(ps[:, e % 2, :], wqkv_h[:, k, e * P:(e + 1) * P], wqkv_l[:, k, e * P:(e + 1) * P],
                                   hT_h[:, k, :], hT_l[:, k, :], k == 0, k == KT - 1)
                    mm.then_inc(q_ps.sem, 1)
                    mlp_among(mlp, c, "q", e)
                ps = claim(v_ready, 1, "v")
                pe.wait_ge(kv_act.sem, kv_act.at(b, 3))
                separate(pe, passed[1])
                for kt in range(TT):
                    mm = pe.transpose(ps[:, 0, kt * HD:(kt + 1) * HD], vT[HD:2 * HD, kt * P:(kt + 1) * P],
                                      cst[HD:2 * HD, 0, HD:2 * HD])
                mm.then_inc(v_ps.sem, 1)
                pe.wait_ge(kv_lo.sem, kv_lo.at(b, 1))

                def maxima(g, i):
                    if i == 0 and g % 2 == 0:
                        moved = q_moved[g // 2]
                        pe.wait_ge(moved.sem, moved.at(b, moved.per))
                    qt, h0, heads = MAX_GROUPS[i]
                    n, per_bank = (qt + 1) * P, heads // 2
                    ps = claim(s_max, MG * g + i + 1, "max", g, i)
                    for bank in range(2):
                        diagonal = ps[:, bank, 0:per_bank * n].rearrange("p (h n) -> p h n", n=n)[:, :, n - P:n]
                        pe.matmul(diagonal, mask_bf[:, 0, :], mask_bf[:, 1:2, :].to_broadcast([P, per_bank, P]),
                                  start=True, stop=False, skip_group_check=True)
                    for h in range(heads):
                        bank, at = h // per_bank, h % per_bank
                        mm = pe.matmul(ps[:, bank, at * n:(at + 1) * n],
                                       qst[0:KROWS, 4 * g + h0 + h, qt * P:(qt + 1) * P], kst[0:KROWS, 0:n],
                                       start=False, stop=True, skip_group_check=True)
                    mm.then_inc(s_ps.sem, 1)

                def maxima_rows(g):
                    ps = claim(m_lo, g + 1, "rows", g)
                    pe.wait_ge(s_max.sem, s_max.at(b, MG * g + MG))
                    pe.transpose(ps[0:4 * TT, 0, 0:P], negm[:, 4 * g:4 * g + 4, :].rearrange("p h q -> p (h q)"), ident)\
                        .then_inc(m_ps.sem, 1)

                for i in range(MG):
                    maxima(0, i)
                    mlp_among(mlp, c, "max", i)
                maxima_rows(0)
                for i in MAX_BEFORE:
                    maxima(1, i)

                def scores(g, kt, step):
                    n = T - kt * P
                    for pr in range(2):
                        ps = claim(p_ready, 2 * step + pr + 1, "scores", step, pr)
                        for j in range(2):
                            pe.matmul(ps[:, j, 0:P], mask_bf[:, 0, :], mask_bf[:, 2, :], start=True, stop=False,
                                      skip_group_check=True)
                        for j in range(2):
                            mm = pe.matmul(ps[:, j, 0:n], kst[0:KROWS + 2, kt * P:(kt + 1) * P],
                                           qst[0:KROWS + 2, 4 * g + 2 * pr + j, kt * P:T], start=False, stop=True,
                                           skip_group_check=True)
                        mm.then_inc(t_ps.sem, 1)

                def values(g, kt, step, out):
                    n = T - kt * P
                    pe.wait_ge(p_ready.sem, p_ready.at(b, 2 * step + 2))
                    weights_, read = (v[:, kt, :], av_out) if out is av else (ones[:, :], den_out)
                    if kt == TT - 1 and g:
                        pe.wait_ge(read.sem, read.at(b, g))
                    elif kt == TT - 1 and not first:
                        pe.wait_ge(read.sem, read.at(b - 1, 4))
                    for c_ in range(4):
                        mm = pe.matmul(out[HD * c_:HD * c_ + HD, kt * P:T], weights_,
                                       probs[:, 2 * (step % 2) + c_ // 2, c_ % 2, 0:n], start=(kt == TT - 1),
                                       stop=(kt == 0), skip_group_check=True)
                    if out is den:
                        mm.then_inc(pv_done.sem, 1)

                pe.wait_ge(v_ready.sem, v_ready.at(b, 1))
                steps = [(g, kt) for g in range(4) for kt in reversed(range(TT))]
                for step, (g, kt) in enumerate(steps):
                    idx = TT - 1 - kt
                    among = maxima_among(g, idx)
                    if kt == TT - 1:
                        pe.wait_ge(m_moved[g].sem, m_moved[g].at(b, 32))
                    if idx == ROWS_STEP and g < 3:
                        maxima_rows(g + 1)
                    scores(g, kt, step)
                    mlp_among(mlp, c, "exp", step, 0)
                    if step:
                        values(*steps[step - 1], step - 1, av)
                    for key in among[0:1]:
                        maxima(*key)
                    mlp_among(mlp, c, "exp", step, 1)
                    if step:
                        values(*steps[step - 1], step - 1, den)
                    for key in among[1:]:
                        maxima(*key)
                    mlp_among(mlp, c, "exp", step, 2)
                for out in (av, den):
                    values(*steps[-1], len(steps) - 1, out)
                for s in range(2):
                    ps = claim(x1_ready, s + 1, "out", s)
                    if first and s == 0:
                        pe.wait_ge(w_lo.sem, 8)
                    for g in range(4):
                        for j in range(2):
                            tt = 2 * s + j
                            if j == 0 and (s == 0 or g == 3):
                                pe.wait_ge(cx_lo.sem, cx_lo.at(b, g + 1 + s))
                            mm = three(ps[:, j, :], hT_h[:, g, tt * P:(tt + 1) * P], hT_l[:, g, tt * P:(tt + 1) * P],
                                       wo_h[:, g, :], wo_l[:, g, :], g == 0, g == 3)
                    mm.then_inc(o_ps.sem, 1)

            batch(0, None, True, False)
            with pe.Fori(1, BATCH - 1) as b:
                batch(b, b - 1, False, False)
            batch(BATCH - 1, BATCH - 2, False, True)
            mlp_alone(mlp, BATCH - 1)

        @block.vector
        def _(dve):
            dve.wait_ge(c_loaded.sem, 64)

            def layernorm(c, n, src, dst, link, stats_ready, deviation_ready, ready, part):
                if part == "stats":
                    for tt in range(TT):
                        ins = dve.bn_stats(stats[:, n, tt, :], src[:, tt, :])
                    link(ins)
                    separate(dve, passed[2])
                    for tt in range(TT):
                        ins = dve.bn_aggr(mv[:, n, tt, :], stats[:, n, tt, :])
                    ins.then_inc(stats_ready.sem, 1)
                else:
                    dve.wait_ge(stats_ready.sem, stats_ready.at(c, 1))
                    dve.wait_ge(deviation_ready.sem, deviation_ready.at(c, 1))
                    for tt in range(TT):
                        dve.tensor_scalar(dst[:, tt, :], src[:, tt, :], mv[:, n, tt, 0:1], rstd[:, n, tt:tt + 1],
                                          ALU.subtract, ALU.mult).then_inc(ready.sem, 1)

            chain = [None]

            def mlp(c, n, step):
                nk, width, a, w = products[n]
                if step == "stats":
                    chain[0] = Link(dve, mlp_link, c)
                    dve.wait_ge(x1_ready.sem, x1_ready.at(c, 2))
                link = chain[0]
                if step in ("stats", "normalise"):
                    layernorm(c, 1, x1, xn, link, ln2_stats, rstd2_ready, xn2_ready, step)
                if step == "xmax":
                    if n == 0:
                        dve.wait_ge(xn2_ready.sem, xn2_ready.at(c, TT))
                    else:
                        dve.wait_ge(act_ready.sem, act_ready.at(c, 1))
                    dve.tensor_reduce(tile_max[:, 0, 0:width], a[:, :, :].rearrange("p a d -> p d a"), AX.X, ALU.max,
                                      apply_absolute_value=True).then_inc(tile_max_ready.sem, 1)
                if step == "wmax":
                    loaded = (mw_loaded, md_loaded)[n]
                    dve.wait_ge(loaded.sem, loaded.at(c, 16))
                    dve.tensor_reduce(tile_max[:, 1, 0:width], w[:, :, :].rearrange("p a d -> p d a"), AX.X, ALU.max,
                                      apply_absolute_value=True)
                if step == "act":
                    dve.wait_ge(th_ready.sem, th_ready.at(c, 1))
                    link(dve.scalar_tensor_tensor(th, th, 1.0, a, ALU.add, ALU.mult))
                    dve.scalar_tensor_tensor(a, th, 0.5, hid[:, :, INNER:D], ALU.mult, ALU.mult)\
                        .then_inc(act_ready.sem, 1)
                if step == "colmax":
                    dve.wait_ge(turned.sem, turned.at(c, n + 1))
                    link(dve.tensor_reduce(amax[:, :, 0:nk],
                                           mlp_ps[:, :, 0:width].rearrange("p i (k d) -> p i k d", d=P), AX.X, ALU.max))
                    link(dve.tensor_scalar(amax[:, 1, 0:nk], amax[:, 1, 0:nk], QEPS, None, ALU.max))
                    link(dve.reciprocal(amax[:, 1, 0:nk], amax[:, 1, 0:nk]))
                if step == "ratio":
                    dve.scalar_tensor_tensor(sc[:, 1, 0:nk], amax[:, 0, 0:nk], QEPS, amax[:, 1, 0:nk],
                                             ALU.max, ALU.mult).then_inc(ratio.sem, 1)
                if step == "s_cols":
                    dve.wait_ge(root.sem, root.at(c, n + 1))
                    link(dve.tensor_scalar(sc[:, 3, 0:nk], sc[:, 2, 0:nk], QEPS, None, ALU.max))
                    dve.reciprocal(sc[:, 4, 0:nk], sc[:, 3, 0:nk]).then_inc(s_cols.sem, 1)
                if step == "scale":
                    dve.wait_ge(s_rows.sem, s_rows.at(c, n + 1))
                    link(dve.tensor_tensor(a[:, :, :], a[:, :, :],
                                           rows[:, 1, 0:width].unsqueeze(1).to_broadcast([P, TT, width]), ALU.mult))
                if step in ("rowmax_a", "rowmax_w"):
                    i, y = (0, a) if step == "rowmax_a" else (1, w)
                    if i:
                        dve.wait_ge(w_scaled.sem, w_scaled.at(c, n + 1))
                    link(dve.tensor_reduce(qm[:, i, :], y[:, :, :], AX.X, ALU.max, apply_absolute_value=True))
                    link(dve.tensor_scalar(qs[:, i, :], qm[:, i, :], QEPS, 1.0 / QMAX, ALU.max, ALU.mult))
                    dve.reciprocal(qi[:, i, :], qs[:, i, :]).then_inc(q_scale.sem, 1)
                if step == "integer_a":
                    dve.wait_ge(rounded.sem, rounded.at(c, 8 * n + 4))
                    dve.tensor_scalar(a_bf[:, :, 0:width], a[:, :, :], MAGIC, None, ALU.subtract).then_inc(a_q.sem, 1)
                if step == "copy_a":
                    dve.wait_ge(rounded.sem, rounded.at(c, 8 * n + 8))
                    dve.wait_ge(aq_ps.sem, aq_ps.at(c, n + 1))
                    dve.tensor_scalar(w_bf[:, :, 0:width], w[:, :, :], MAGIC, None, ALU.subtract).then_inc(w_q.sem, 1)
                if step in ("undo0", "undo1"):
                    s = int(step[-1])
                    dve.wait_ge(md_loaded.sem, md_loaded.at(c, 16))
                    dve.wait_ge(wrow_ready.sem, wrow_ready.at(c, n + 1))
                    dve.wait_ge(h_ps.sem, h_ps.at(c, 2 * n + s + 1))
                    for j in range(2):
                        tt = 2 * s + j
                        dve.scalar_tensor_tensor(hid[:, tt, :], mlp_ps[:, j, :], qs[:, 0, tt:tt + 1], wrow[:, :],
                                                 ALU.mult, ALU.mult).then_inc(h_ready.sem, 1)
                if step == "residual":
                    dve.wait_ge(h_ready.sem, h_ready.at(c, 2 * TT))
                    link.done()

            def batch(b, c, first, last):
                def layernorm1(n, part):
                    if part == "stats":
                        dve.wait_ge(x_loaded.sem, x_loaded.at(n, 16))
                    layernorm(n, 0, x_in, x_in, Link(dve, ln_link, n), ln_stats, rstd_ready, xn_ready, part)

                if first:
                    layernorm1(b, "stats")
                    layernorm1(b, "normalise")
                for s in range(2):
                    dve.wait_ge(xT_hi.sem, xT_hi.at(b, s + 1))
                    dve.tensor_tensor(hT_l[:, 2 * s:2 * s + 2, :], slots[SLOT["xT", s]][:, :, :],
                                      hT_h[:, 2 * s:2 * s + 2, :].bitcast(F32), ALU.subtract).then_inc(xT_lo.sem, 1)
                dve.wait_ge(kv_act.sem, kv_act.at(b, 3))
                dve.scalar_tensor_tensor(kst[2 * HD:KROWS, :], slots[SLOT["kv",]][0:HD, 0, :], bkv_sb[0:HD, :],
                                         kst[0:HD, :].bitcast(F32), ALU.add, ALU.subtract).then_inc(kv_lo.sem, 1)
                for e in range(KT):
                    ps = slots[SLOT["q", e // 2]]
                    dve.wait_ge(q_hi.sem, q_hi.at(b, e + 1))
                    dve.scalar_tensor_tensor(qT_l[:, e, :], ps[:, e % 2, :], bq_sb[:, e:e + 1],
                                             qT_h[:, e, :].bitcast(F32), ALU.add, ALU.subtract).then_inc(q_lo.sem, 1)
                    mlp_among(mlp, c, "q", e)
                dve.wait_ge(v_ps.sem, v_ps.at(b, 1))
                dve.tensor_copy(v[:, :, :], slots[SLOT["v",]][:, 0, 0:TT * HD].rearrange("p (a d) -> p a d", d=HD))\
                    .then_inc(v_ready.sem, 1)

                def maxima(g, i):
                    qt, h0, heads = MAX_GROUPS[i]
                    n, h0 = (qt + 1) * P, 4 * g + h0
                    dve.wait_ge(s_ps.sem, s_ps.at(b, MG * g + i + 1))
                    dve.tensor_reduce(negm[:, h0:h0 + heads, qt].rearrange("p (a c) -> p a c", a=2),
                                      slots[SLOT["max", g, i]][:, :, 0:heads // 2 * n].rearrange("p a (c n) -> p a c n", n=n),
                                      AX.X, ALU.max, negate=True).then_inc(s_max.sem, 1)

                def low_maxima(g):
                    dve.wait_ge(m_hi.sem, m_hi.at(b, g + 1))
                    dve.tensor_tensor(negm_l[:, g, :], slots[SLOT["rows", g]][0:4 * TT, 0, 0:P],
                                      negm_h[:, g, :].bitcast(F32), ALU.subtract).then_inc(m_lo.sem, 1)

                for i in range(MG):
                    maxima(0, i)
                    mlp_among(mlp, c, "max", i)
                low_maxima(0)
                for i in MAX_BEFORE:
                    maxima(1, i)

                def sums_out(g):
                    dve.wait_ge(pv_done.sem, pv_done.at(b, 4 * g + 4))
                    if g >= 2:
                        dve.wait_ge(cx_lo.sem, cx_lo.at(b, g - 1))
                    dve.tensor_copy(cx[:, g % 2, :], av[:, :]).then_inc(av_out.sem, 1)

                def context(g, hf=None):
                    cols = slice(0, T) if hf is None else slice(T // 2 * hf, T // 2 * (hf + 1))
                    n = g + 1 + (hf or 0)
                    dve.wait_ge(den_out.sem, den_out.at(b, g + 1))
                    dve.reciprocal(rden[:, cols], rden[:, cols]).then_inc(rden_ready.sem, 1)
                    dve.wait_ge(rden_ready.sem, rden_ready.at(b, n))
                    dve.wait_ge(av_out.sem, av_out.at(b, g + 1))
                    dve.tensor_tensor(cx[:, g % 2, cols], cx[:, g % 2, cols], rden[:, cols], ALU.mult)\
                        .then_inc(cx_ready.sem, 1)

                for step in range(16):
                    g, idx = divmod(step, TT)
                    among = maxima_among(g, idx)
                    if idx == ROWS_STEP and g < 3:
                        low_maxima(g + 1)
                    mlp_among(mlp, c, "exp", step, 0)
                    if idx == 0 and g:
                        sums_out(g - 1)
                    for key in among[0:1]:
                        maxima(*key)
                    mlp_among(mlp, c, "exp", step, 1)
                    for key in among[1:]:
                        maxima(*key)
                    if idx == 1 and g:
                        context(g - 1)
                    mlp_among(mlp, c, "exp", step, 2)
                    if step == LN1_STEP and not last:
                        layernorm1(b + 1, "stats")
                    if step == LN1_STEP + 1 and not last:
                        layernorm1(b + 1, "normalise")
                sums_out(3)
                for hf in range(2):
                    context(3, hf)
                mlp(b, 0, "wmax")
                dve.wait_ge(xb_ready.sem, xb_ready.at(b, 1))
                if not first:
                    dve.wait_ge(x2_ready.sem, x2_ready.at(c, TT))
                for s in range(2):
                    dve.wait_ge(o_ps.sem, o_ps.at(b, s + 1))
                    dve.tensor_tensor(x1[:, 2 * s:2 * s + 2, :], slots[SLOT["out", s]][:, :, :], xn[:, 2 * s:2 * s + 2, :], ALU.add)\
                        .then_inc(x1_ready.sem, 1)

            batch(0, None, True, False)
            with dve.Fori(1, BATCH - 1) as b:
                batch(b, b - 1, False, False)
            batch(BATCH - 1, BATCH - 2, False, True)
            mlp_alone(mlp, BATCH - 1)


def feed_forward(nc, x2, wg, wu, wd, ga, ua, da, gb, ub, db, expert_bias, consts, out):
    with ExitStack() as ctx:
        def sb(name, shape, dt=F32):
            return ctx.enter_context(nc.sbuf_tensor(name, shape, dt))

        def sig(name, per=1):
            return Signal(ctx, nc, name, per)

        cst = sb("f_cst", [P, 4, P])
        ident, lower = cst[:, 0, :], cst[:, 3, 0:EXPERTS * EXPERTS]
        half, ln_eps = sb("f_half", [P, TT]), sb("f_ln_eps", [P, TT])
        bias_bc = sb("bias_bc", [P, EXPERTS])
        wg_sb, wu_sb, wd_sb = sb("wg_sb", [P, KT, DFF]), sb("wu_sb", [P, KT, DFF]), sb("wd_sb", [P, FT, D])
        g_h, g_l = sb("g_h", [P, 2, KT, P], F32R), sb("g_l", [P, 2, KT, P], F32R)
        u_h, u_l = sb("u_h", [P, 2, KT, P], F32R), sb("u_l", [P, 2, KT, P], F32R)
        d_h, d_l = sb("d_h", [P, 2, D], F32R), sb("d_l", [P, 2, D], F32R)
        ga_h, ga_l = sb("ga_h", [P, KT, LA], F32R), sb("ga_l", [P, KT, LA], F32R)
        ua_h, ua_l = sb("ua_h", [P, KT, LR], F32R), sb("ua_l", [P, KT, LR], F32R)
        da_h, da_l = sb("da_h", [P, FT, LR], F32R), sb("da_l", [P, FT, LR], F32R)
        gb_h, gb_l = sb("gb_h", [LR, DFF], F32R), sb("gb_l", [LR, DFF], F32R)
        ub_h, ub_l = sb("ub_h", [LR, DFF], F32R), sb("ub_l", [LR, DFF], F32R)
        db_h, db_l = sb("db_h", [LR, D], F32R), sb("db_l", [LR, D], F32R)
        x2_in, x2_res = sb("x2_in", [P, TT, D]), sb("x2_res", [P, TT, D])
        stats, mv = sb("f_stats", [P, TT, 6]), sb("f_mv", [P, TT, 2])
        veps, rstd = sb("f_veps", [P, TT]), sb("f_rstd", [P, TT])
        xT_h, xT_l = sb("xT_h", [P, KT, T], F32R), sb("xT_l", [P, KT, T], F32R)
        a_gate, a_up = sb("a_gate", [LA, T]), sb("a_up", [LR, T])
        prob = sb("prob", [P, TT, EXPERTS])
        biased = sb("biased", [P, TT, EXPERTS])
        beats, ties = sb("beats", [P, TT, EXPERTS, EXPERTS]), sb("ties", [P, TT, EXPERTS, EXPERTS])
        rank, wsum = sb("rank", [P, TT, EXPERTS]), sb("wsum", [P, 2, TT])
        wx, wxT = sb("wx", [P, TT, LR]), sb("wxT", [LR, T])
        y = sb("y", [LR, T])
        yg_h, yg_l = sb("yg_h", [LR, T], F32R), sb("yg_l", [LR, T], F32R)
        yu_h, yu_l = sb("yu_h", [LR, T], F32R), sb("yu_l", [LR, T], F32R)
        work = sb("work", [P, 3, T])
        th, gated, hd = work[:, 0, :], work[:, 1, :], work[:, 2, :]
        hd_h, hd_l = sb("hd_h", [P, 2, T], F32R), sb("hd_l", [P, 2, T], F32R)

        ring = [ctx.enter_context(nc.psum_tensor(f"ring{i}", [P, T], F32)) for i in range(3)]
        down = ctx.enter_context(nc.psum_tensor("down", [P, TT, D], F32))
        adps = ctx.enter_context(nc.psum_tensor("adps", [P, T], F32))

        f_c = sig("f_c")
        gate_up_loaded, down_loaded = ([sig(f"{name}_loaded{i}") for i in range(3)] for name in ("gate_up", "down"))
        lora_loaded, lora_hi, lora_lo = [sig(f"lora_loaded{n}") for n in range(7)], sig("lora_hi"), sig("lora_lo")
        f_consts = sig("f_consts")
        x2_loaded, res_loaded, stored = sig("x2_loaded", 16), sig("res_loaded", 16), sig("stored", 16)
        ln_stats, rstd_ready, xn_ready = sig("f_ln_stats"), sig("f_rstd_ready"), sig("f_xn_ready", TT)
        xT_ps, xT_hi, xT_lo = sig("f_xT_ps", KT), sig("f_xT_hi", KT), sig("f_xT_lo", KT)
        a_ps, a_copied = sig("a_ps", 2), sig("a_copied", 2)
        logits_ps, prob_tanh, wx_ready, wx_ps, wxT_ready = (sig("logits_ps"), sig("prob_tanh"), sig("wx_ready"),
                                                            sig("wx_ps"), sig("wxT_ready"))
        y_ready, y_hi, y_lo = sig("y_ready", 3), sig("y_hi", 3), sig("y_lo", 3)
        gu_hi, gu_lo = sig("gu_hi", 2 * FT), sig("gu_lo", 2 * FT)
        d_hi, d_lo = sig("d_hi", FT), sig("d_lo", FT)
        g_ps, u_ps = sig("g_ps", FT), sig("u_ps", FT)
        tanh_done, gated_done, hd_ready = sig("tanh_done", FT), sig("gated_done", FT), sig("hd_ready", FT)
        hd_hi, hd_lo = sig("hd_hi", FT), sig("hd_lo", FT)
        tile_done = sig("tile_done", FT)
        out_ps, out_ready = sig("out_ps", TT), sig("out_ready", TT)
        dve_link, pool_link, ln_link = sig("f_dve_link", FF_DVE_LINKS), sig("f_pool_link", 1), sig("f_ln_link")
        passed = [sig(f"f_passed_{e}") for e in ("pool", "pe", "dve")]

        ga_end, ua_end, da_end = KT * LA, KT * (LA + LR), KT * (LA + LR) + FT * LR
        res_flat, work_flat = (t[:, :, :].rearrange("p a d -> p (a d)") for t in (x2_res, work))
        last = da_end - LR
        lora = [(ga.rearrange("(k p) n -> p k n", p=P), res_flat[:, 0:ga_end].rearrange("p (k n) -> p k n", k=KT),
                 ga_h[:, :, :], ga_l[:, :, :]),
                (ua.rearrange("(k p) n -> p k n", p=P), res_flat[:, ga_end:ua_end].rearrange("p (k n) -> p k n", k=KT),
                 ua_h[:, :, :], ua_l[:, :, :]),
                (gb, work_flat[0:LR, 0:DFF], gb_h[:, :], gb_l[:, :]),
                (da[0:(FT - 1) * P, :].rearrange("(f p) n -> p f n", p=P),
                 res_flat[:, ua_end:last].rearrange("p (f n) -> p f n", n=LR), da_h[:, 0:FT - 1, :], da_l[:, 0:FT - 1, :]),
                (da[(FT - 1) * P:DFF, :], res_flat[0:FLAST, last:da_end], da_h[0:FLAST, FT - 1, :], da_l[0:FLAST, FT - 1, :]),
                (db, res_flat[0:LR, da_end:da_end + D], db_h[:, :], db_l[:, :]),
                (ub, work_flat[0:LR, 0:DFF], ub_h[:, :], ub_l[:, :])]
        GB, UB = 2, len(lora) - 1

        def weight_parts(f):
            m, at, s = f_rows(f), f * P, f % 2
            return ((wg_sb[:, :, at:at + m], g_h[:, s, :, 0:m], g_l[:, s, :, 0:m]),
                    (wu_sb[:, :, at:at + m], u_h[:, s, :, 0:m], u_l[:, s, :, 0:m]),
                    (wd_sb[0:m, f, :], d_h[0:m, s, :], d_l[0:m, s, :]))

        block = ctx.enter_context(nc.Block())

        @block.sync
        def _(sp):
            sp.dma_start(x2_in[:, :, :], x2[0].rearrange("(a p) d -> p a d", p=P)).then_inc(x2_loaded.sem, 16)
            sp.dma_start(cst[:, :, :], consts).then_inc(f_c.sem, 16)
            sp.dma_start(bias_bc[:, :], expert_bias.partition_broadcast(P)).then_inc(f_c.sem, 16)

            def load_lora(*which):
                for n in which:
                    src, raw, _, _ = lora[n]
                    sp.dma_start(raw, src).then_inc(lora_loaded[n].sem, 16)

            def load_gate_up(part):
                for dst, src in ((wg_sb, wg), (wu_sb, wu)):
                    cols = slice(P * FF_PARTS[part], min(P * FF_PARTS[part + 1], DFF))
                    sp.dma_start(dst[:, :, cols], src[:, :, cols]).then_inc(gate_up_loaded[part].sem, 16)

            def load_down(part):
                f0, f1 = FF_PARTS[part], min(FF_PARTS[part + 1], FT - 1)
                sp.dma_start(wd_sb[:, f0:f1, :], wd[f0 * P:f1 * P, :].rearrange("(f p) d -> p f d", p=P))\
                  .then_inc(down_loaded[part].sem, 16)

            load_lora(0, 1)
            load_gate_up(0)
            load_lora(GB)
            load_down(0)
            load_lora(*range(GB + 1, UB))
            load_gate_up(1)
            sp.wait_ge(lora_lo.sem, GB + 1)
            load_lora(UB)
            load_down(1)
            load_gate_up(2)
            load_down(2)
            sp.dma_start(wd_sb[0:FLAST, FT - 1, :], wd[(FT - 1) * P:DFF, :]).then_inc(down_loaded[2].sem, 16)

            def batch(b, first, last):
                if not last:
                    sp.wait_ge(xn_ready.sem, xn_ready.at(b, TT))
                    sp.wait_ge(xT_ps.sem, xT_ps.at(b, KT))
                    sp.dma_start(x2_in[:, :, :], x2[b + 1].rearrange("(a p) d -> p a d", p=P)).then_inc(x2_loaded.sem, 16)
                if first:
                    sp.wait_ge(lora_lo.sem, len(lora))
                else:
                    sp.wait_ge(stored.sem, stored.at(b - 1, 16))
                sp.dma_start(x2_res[:, :, :], x2[b].rearrange("(a p) d -> p a d", p=P)).then_inc(res_loaded.sem, 16)
                sp.wait_ge(out_ready.sem, out_ready.at(b, TT))
                sp.dma_start(out[b].rearrange("(a p) d -> p a d", p=P), x2_res[:, :, :]).then_inc(stored.sem, 16)

            batch(0, True, False)
            with sp.Fori(1, BATCH - 1) as b:
                batch(b, False, False)
            batch(BATCH - 1, False, True)
            sp.wait_ge(stored.sem, 16 * BATCH)

        @block.gpsimd
        def _(pool):
            for n, (dst, value) in enumerate(((half[:, :], -0.5), (wx[:, :, ER:LR], 1.0 / RANK),
                                              (ln_eps[:, :], LN_EPS))):
                pool.memset(dst, value).then_inc(f_consts.sem, 1)
                pool.wait_ge(f_consts.sem, n + 1)

            def inverse_deviation(b):
                pool.wait_ge(ln_stats.sem, ln_stats.at(b, 1))
                pool.tensor_tensor(veps[:, :], mv[:, :, 1], ln_eps[:, :], ALU.add).then_inc(pool_link.sem, 1)
                pool.wait_ge(pool_link.sem, pool_link.at(b, 1))
                pool.tensor_tensor(rstd[:, :], veps[:, :], half[:, :], ALU.pow).then_inc(rstd_ready.sem, 1)

            def split_gate_up(b, f):
                for i, (w, hi, lo) in enumerate(weight_parts(f)[0:2]):
                    pool.wait_ge(gu_hi.sem, gu_hi.at(b, 2 * f + i + 1))
                    pool.tensor_tensor(lo, w, hi.bitcast(F32), ALU.subtract).then_inc(gu_lo.sem, 1)

            def split_down(b, f):
                w, hi, lo = weight_parts(f)[2]
                pool.wait_ge(d_hi.sem, d_hi.at(b, f + 1))
                pool.tensor_tensor(lo, w, hi.bitcast(F32), ALU.subtract).then_inc(d_lo.sem, 1)

            def first_splits(b):
                split_gate_up(b, 0)
                split_gate_up(b, 1)
                split_down(b, 0)

            def batch(b, first, last):
                for f in range(FT):
                    if f + 2 < FT:
                        split_gate_up(b, f + 2)
                    pool.wait_ge(hd_hi.sem, hd_hi.at(b, f + 1))
                    m = f_rows(f)
                    pool.tensor_tensor(hd_l[0:m, f % 2, :], hd[0:m, :], hd_h[0:m, f % 2, :].bitcast(F32), ALU.subtract)\
                        .then_inc(hd_lo.sem, 1)
                    if f + 1 < FT:
                        split_down(b, f + 1)
                    if f == LN3_TILE and not last:
                        inverse_deviation(b + 1)
                if not last:
                    first_splits(b + 1)

            inverse_deviation(0)
            first_splits(0)
            batch(0, True, False)
            with pool.Fori(1, BATCH - 1) as b:
                batch(b, False, False)
            batch(BATCH - 1, False, True)

        @block.scalar
        def _(act):
            def split_lora(which):
                for n in which:
                    _, raw, hi, _ = lora[n]
                    act.wait_ge(lora_loaded[n].sem, 16)
                    act.activation(hi, raw, ACT.Copy).then_inc(lora_hi.sem, 1)

            def split(b, f, i, loading=False, free=None):
                w, hi, _ = weight_parts(f)[i]
                if free is not None:
                    done = (g_ps, u_ps, tile_done)[i]
                    act.wait_ge(done.sem, done.at(*free))
                if loading:
                    part = 0 if f < FF_PARTS[1] else 1 if f < FF_PARTS[2] else 2
                    if i < 2:
                        act.wait_ge(gate_up_loaded[part].sem, 32)
                    else:
                        act.wait_ge(down_loaded[part].sem, 32 if part == 2 else 16)
                act.activation(hi, w, ACT.Copy).then_inc((gu_hi, gu_hi, d_hi)[i].sem, 1)

            def transposed(b):
                for k in range(KT):
                    act.wait_ge(xT_ps.sem, xT_ps.at(b, k + 1))
                    act.activation(xT_h[:, k, :], ring[(TURN_AT + k) % 3][:, :], ACT.Copy).then_inc(xT_hi.sem, 1)

            def low_rank_inputs(b):
                for n, (dst, rows) in enumerate(((a_gate, LA), (a_up, LR))):
                    act.wait_ge(a_ps.sem, a_ps.at(b, n + 1))
                    act.activation(dst[:, :], ring[(TURN_AT + KT + n) % 3][0:rows, :], ACT.Copy).then_inc(a_copied.sem, 1)

            def batch(b, first, last):
                act.wait_ge(logits_ps.sem, logits_ps.at(b, 1))
                act.activation(prob[:, :, :], adps[:, 0:TT * EXPERTS].rearrange("p (a e) -> p a e", e=EXPERTS),
                               ACT.Tanh, scale=0.5).then_inc(prob_tanh.sem, 1)
                if first:
                    split_lora(range(GB + 1, UB + 1))
                    split(0, 0, 2, loading=True)
                act.wait_ge(wx_ps.sem, wx_ps.at(b, 1))
                act.activation(wxT[:, :], adps[0:LR, :], ACT.Copy).then_inc(wxT_ready.sem, 1)
                for n, hi in enumerate((yg_h, yu_h)):
                    act.wait_ge(y_ready.sem, y_ready.at(b, n + 1))
                    act.activation(hi[:, :], y[:, :], ACT.Copy).then_inc(y_hi.sem, 1)
                for f in range(FT):
                    m = f_rows(f)
                    act.wait_ge(g_ps.sem, g_ps.at(b, f + 1))
                    if f:
                        act.wait_ge(gated_done.sem, gated_done.at(b, f))
                    act.activation(th[0:m, :], ring[2 * f % 3][0:m, :], ACT.Tanh, scale=0.5).then_inc(tanh_done.sem, 1)
                    if f + 2 < FT:
                        split(b, f + 2, 0, first, (b, f + 1))
                        split(b, f + 2, 1, first, (b, f + 1))
                    act.wait_ge(hd_ready.sem, hd_ready.at(b, f + 1))
                    if f >= 2:
                        act.wait_ge(tile_done.sem, tile_done.at(b, f - 1))
                    act.activation(hd_h[0:m, f % 2, :], hd[0:m, :], ACT.Copy).then_inc(hd_hi.sem, 1)
                    if f + 1 < FT:
                        split(b, f + 1, 2, first, (b, f) if f >= 1 else None if first else (b - 1, FT - 1))
                if not last:
                    transposed(b + 1)
                    for f in range(2):
                        for i in range(2):
                            split(b + 1, f, i, free=(b, FT - (FT - 1 - f) % 2))
                    low_rank_inputs(b + 1)
                act.wait_ge(y_ready.sem, y_ready.at(b, 3))
                act.activation(yg_h[:, :], y[:, :], ACT.Copy).then_inc(y_hi.sem, 1)
                if not last:
                    split(b + 1, 0, 2, free=(b, FT))

            split_lora(range(GB))
            transposed(0)
            for i in range(2):
                split(0, 0, i, loading=True)
            split_lora((GB,))
            low_rank_inputs(0)
            for i in range(2):
                split(0, 1, i, loading=True)
            batch(0, True, False)
            with act.Fori(1, BATCH - 1) as b:
                batch(b, False, False)
            batch(BATCH - 1, False, True)

        @block.tensor
        def _(pe):
            tenants = Tenants(3)
            pe.wait_ge(f_c.sem, 32)

            def three(out_, w_hi, w_lo, m_hi, m_lo, start, stop):
                pe.matmul(out_, w_hi, m_hi, start=start, stop=False, skip_group_check=True)
                pe.matmul(out_, w_hi, m_lo, start=False, stop=False, skip_group_check=True)
                return pe.matmul(out_, w_lo, m_hi, start=False, stop=stop, skip_group_check=True)

            def turn(b, at, ahead):
                for k in range(KT):
                    assert tenants.n % 3 == (TURN_AT + k) % 3
                    ps = ring[tenants.claim(pe, at, xT_lo, k + 1, ahead)]
                    for tt in range(TT):
                        if k == 0:
                            pe.wait_ge(xn_ready.sem, xn_ready.at(b, tt + 1))
                        mm = pe.transpose(ps[:, tt * P:(tt + 1) * P], x2_in[:, tt, k * P:(k + 1) * P], ident)
                    mm.then_inc(xT_ps.sem, 1)

            def low_rank_inputs(b, at, ahead):
                for n, (hi, lo, width) in enumerate(((ga_h, ga_l, LA), (ua_h, ua_l, LR))):
                    ps = ring[tenants.claim(pe, at, a_copied, n + 1, ahead)]
                    for k in range(KT):
                        pe.wait_ge(xT_lo.sem, xT_lo.at(b, k + 1))
                        mm = three(ps[0:width, :], hi[:, k, :], lo[:, k, :], xT_h[:, k, :], xT_l[:, k, :],
                                   k == 0, k == KT - 1)
                    mm.then_inc(a_ps.sem, 1)

            def batch(b, first, last):
                tenants.new_batch(first)
                pe.wait_ge(a_copied.sem, a_copied.at(b, 1))
                if not first:
                    pe.wait_ge(y_ready.sem, y_ready.at(b - 1, 3))
                separate(pe, passed[1])
                for tt in range(TT):
                    mm = pe.transpose(adps[:, tt * EXPERTS:(tt + 1) * EXPERTS], a_gate[ROUTE:LA, tt * P:(tt + 1) * P],
                                      cst[ROUTE:LA, 0, ROUTE:LA])
                mm.then_inc(logits_ps.sem, 1)

                held = {}

                def base(side, f):
                    m = f_rows(f)
                    hi, lo, freed = ((g_h, g_l, gated_done), (u_h, u_l, hd_ready))[side]
                    ps = held[side, f] = ring[tenants.claim(pe, b, freed, f + 1)]
                    pe.wait_ge(gu_lo.sem, gu_lo.at(b, 2 * f + side + 1))
                    for k in range(KT):
                        three(ps[0:m, :], hi[:, f % 2, k, 0:m], lo[:, f % 2, k, 0:m], xT_h[:, k, :], xT_l[:, k, :],
                              k == 0, False)

                def low_rank(side, f):
                    m = f_rows(f)
                    hi, lo, yh, yl, ready = ((gb_h, gb_l, yg_h, yg_l, g_ps), (ub_h, ub_l, yu_h, yu_l, u_ps))[side]
                    cols = slice(f * P, f * P + m)
                    if f == 0:
                        if first:
                            pe.wait_ge(lora_lo.sem, len(lora))
                        pe.wait_ge(y_lo.sem, y_lo.at(b, side + 1))
                    three(held[side, f][0:m, :], hi[:, cols], lo[:, cols], yh[:, :], yl[:, :], False, True)\
                        .then_inc(ready.sem, 1)

                def project(f):
                    m, s = f_rows(f), f % 2
                    pe.wait_ge(hd_lo.sem, hd_lo.at(b, f + 1))
                    pe.wait_ge(d_lo.sem, d_lo.at(b, f + 1))
                    if f == 0 and not first:
                        pe.wait_ge(out_ready.sem, out_ready.at(b - 1, TT))
                    for tt in range(TT):
                        cols = slice(tt * P, (tt + 1) * P)
                        three(down[:, tt, :], hd_h[0:m, s, cols], hd_l[0:m, s, cols], d_h[0:m, s, :], d_l[0:m, s, :],
                              f == 0, False)
                    three(adps[0:LR, :], da_h[0:m, f, :], da_l[0:m, f, :], hd_h[0:m, s, :], hd_l[0:m, s, :],
                          f == 0, f == FT - 1).then_inc(tile_done.sem, 1)

                base(0, 0)
                base(1, 0)
                pe.wait_ge(wx_ready.sem, wx_ready.at(b, 1))
                for tt in range(TT):
                    mm = pe.transpose(adps[0:LR, tt * P:(tt + 1) * P], wx[:, tt, :], ident)
                mm.then_inc(wx_ps.sem, 1)
                base(0, 1)
                low_rank(0, 0)
                low_rank(1, 0)
                low_rank(0, 1)
                base(1, 1)
                low_rank(1, 1)
                project(0)
                for f in range(2, FT):
                    for side in range(2):
                        base(side, f)
                        low_rank(side, f)
                    if f == FT - 1 and not last:
                        turn(b + 1, b, 1)
                    project(f - 1)
                project(FT - 1)
                if not last:
                    low_rank_inputs(b + 1, b, 1)
                pe.wait_ge(y_lo.sem, y_lo.at(b, 3))
                for tt in range(TT):
                    cols = slice(tt * P, (tt + 1) * P)
                    three(down[:, tt, :], yg_h[:, cols], yg_l[:, cols], db_h[:, :], db_l[:, :], False, True)\
                        .then_inc(out_ps.sem, 1)

            tenants.new_batch(True)
            tenants.n = TURN_AT
            turn(0, -1, 1)
            pe.wait_ge(lora_lo.sem, GB)
            low_rank_inputs(0, -1, 1)
            batch(0, True, False)
            with pe.Fori(1, BATCH - 1) as b:
                batch(b, False, False)
            batch(BATCH - 1, False, True)

        @block.vector
        def _(dve):
            def split_lora(which):
                for n in which:
                    _, raw, hi, lo = lora[n]
                    dve.wait_ge(lora_hi.sem, n + 1)
                    dve.tensor_tensor(lo, raw, hi.bitcast(F32), ALU.subtract).then_inc(lora_lo.sem, 1)

            def statistics(b):
                dve.wait_ge(x2_loaded.sem, x2_loaded.at(b, 16))
                for tt in range(TT):
                    ins = dve.bn_stats(stats[:, tt, :], x2_in[:, tt, :])
                Link(dve, ln_link, b)(ins)
                separate(dve, passed[2])
                for tt in range(TT):
                    ins = dve.bn_aggr(mv[:, tt, :], stats[:, tt, :])
                ins.then_inc(ln_stats.sem, 1)

            def normalise(b):
                dve.wait_ge(ln_stats.sem, ln_stats.at(b, 1))
                dve.wait_ge(rstd_ready.sem, rstd_ready.at(b, 1))
                for tt in range(TT):
                    dve.tensor_scalar(x2_in[:, tt, :], x2_in[:, tt, :], mv[:, tt, 0:1], rstd[:, tt:tt + 1],
                                      ALU.subtract, ALU.mult).then_inc(xn_ready.sem, 1)

            def transposed(b):
                for k in range(KT):
                    dve.wait_ge(xT_hi.sem, xT_hi.at(b, k + 1))
                    dve.tensor_tensor(xT_l[:, k, :], ring[(TURN_AT + k) % 3][:, :], xT_h[:, k, :].bitcast(F32),
                                      ALU.subtract).then_inc(xT_lo.sem, 1)

            def batch(b, first, last):
                link = Link(dve, dve_link, b)
                dve.wait_ge(prob_tanh.sem, prob_tanh.at(b, 1))
                link(dve.tensor_scalar(prob[:, :, :], prob[:, :, :], 0.5, 0.5, ALU.mult, ALU.add))
                link(dve.tensor_tensor(biased[:, :, :], prob[:, :, :],
                                       bias_bc[:, :].unsqueeze(1).to_broadcast([P, TT, EXPERTS]), ALU.add))
                shape = [P, TT, EXPERTS, EXPERTS]
                others, own = biased[:, :, :].unsqueeze(2).to_broadcast(shape), biased[:, :, :].unsqueeze(3).to_broadcast(shape)
                dve.tensor_tensor(beats[:, :, :, :], others, own, ALU.is_gt)
                link(dve.tensor_tensor(ties[:, :, :, :], others, own, ALU.is_equal))
                pairs = ties[:, :, :, :].rearrange("p a e j -> p a (e j)")
                link(dve.tensor_tensor(pairs, pairs, lower.unsqueeze(1).to_broadcast([P, TT, EXPERTS * EXPERTS]), ALU.mult))
                link(dve.tensor_tensor(beats[:, :, :, :], beats[:, :, :, :], ties[:, :, :, :], ALU.add))
                link(dve.tensor_reduce(rank[:, :, :], beats[:, :, :, :], AX.X, ALU.add))
                link(dve.scalar_tensor_tensor(prob[:, :, :], rank[:, :, :], 1.5, prob[:, :, :], ALU.is_lt, ALU.mult))
                link(dve.tensor_reduce(wsum[:, 0, :], prob[:, :, :], AX.X, ALU.add))
                link(dve.tensor_scalar(wsum[:, 0, :], wsum[:, 0, :], 1e-8, float(RANK), ALU.add, ALU.mult))
                link(dve.reciprocal(wsum[:, 1, :], wsum[:, 0, :]))
                dve.tensor_tensor(wx[:, :, 0:ER].rearrange("p a (e r) -> p a e r", r=RANK),
                                  prob[:, :, :].unsqueeze(3).to_broadcast([P, TT, EXPERTS, RANK]),
                                  wsum[:, 1, :].unsqueeze(2).unsqueeze(3).to_broadcast([P, TT, EXPERTS, RANK]),
                                  ALU.mult).then_inc(wx_ready.sem, 1)
                if first:
                    split_lora(range(GB + 1, UB + 1))
                dve.wait_ge(wxT_ready.sem, wxT_ready.at(b, 1))
                for n, (a, hi, lo) in enumerate(((a_gate, yg_h, yg_l), (a_up, yu_h, yu_l))):
                    dve.wait_ge(a_copied.sem, a_copied.at(b, n + 1))
                    dve.tensor_tensor(y[:, :], a[0:LR, :], wxT[:, :], ALU.mult).then_inc(y_ready.sem, 1)
                    dve.wait_ge(y_hi.sem, y_hi.at(b, n + 1))
                    dve.tensor_tensor(lo[:, :], y[:, :], hi[:, :].bitcast(F32), ALU.subtract).then_inc(y_lo.sem, 1)
                    dve.wait_ge(y_lo.sem, y_lo.at(b, n + 1))
                for f in range(FT):
                    m = f_rows(f)
                    dve.wait_ge(tanh_done.sem, tanh_done.at(b, f + 1))
                    dve.scalar_tensor_tensor(gated[0:m, :], th[0:m, :], 1.0, ring[2 * f % 3][0:m, :],
                                             ALU.add, ALU.mult).then_inc(gated_done.sem, 1)
                    dve.wait_ge(gated_done.sem, gated_done.at(b, f + 1))
                    dve.wait_ge(u_ps.sem, u_ps.at(b, f + 1))
                    if f:
                        dve.wait_ge(hd_lo.sem, hd_lo.at(b, f))
                    elif not first:
                        dve.wait_ge(hd_lo.sem, hd_lo.at(b - 1, FT))
                    dve.scalar_tensor_tensor(hd[0:m, :], gated[0:m, :], 0.5, ring[(2 * f + 1) % 3][0:m, :],
                                             ALU.mult, ALU.mult).then_inc(hd_ready.sem, 1)
                    if f == LN3_TILE and not last:
                        statistics(b + 1)
                    if f == LN3_TILE + 1 and not last:
                        normalise(b + 1)
                if not last:
                    transposed(b + 1)
                dve.wait_ge(tile_done.sem, tile_done.at(b, FT))
                dve.tensor_tensor(y[:, :], adps[0:LR, :], wxT[:, :], ALU.mult).then_inc(y_ready.sem, 1)
                dve.wait_ge(y_hi.sem, y_hi.at(b, 3))
                dve.tensor_tensor(yg_l[:, :], y[:, :], yg_h[:, :].bitcast(F32), ALU.subtract).then_inc(y_lo.sem, 1)
                dve.wait_ge(res_loaded.sem, res_loaded.at(b, 16))
                for tt in range(TT):
                    dve.wait_ge(out_ps.sem, out_ps.at(b, tt + 1))
                    dve.tensor_tensor(x2_res[:, tt, :], down[:, tt, :], x2_res[:, tt, :], ALU.add)\
                        .then_inc(out_ready.sem, 1)
                link.done()

            statistics(0)
            normalise(0)
            split_lora(range(GB))
            transposed(0)
            split_lora((GB,))
            dve.wait_ge(f_c.sem, 32)
            dve.wait_ge(f_consts.sem, 3)
            batch(0, True, False)
            with dve.Fori(1, BATCH - 1) as b:
                batch(b, False, False)
            batch(BATCH - 1, False, True)


FF_DVE_LINKS = 10
TURN_AT = 2 * FT
FF_PARTS = (0, 2, 6, FT)
LN3_TILE = 5


def build(nc, arrays):
    ap = {n: nc.dram_tensor(n, a.shape, F32, kind="ExternalInput").ap() for n, a in arrays.items()}
    x2 = nc.dram_tensor("x2", (BATCH, T, D), F32, kind="Internal").ap()
    out = nc.dram_tensor("out", (BATCH, T, D), F32, kind="ExternalOutput").ap()
    attention_and_mlp(nc, ap["x"], ap["wqkvT"].rearrange("(k p) e -> p k e", p=P), ap["bq"], ap["bkv"],
                      ap["woT"].rearrange("(k p) e -> p k e", p=P), ap["bo"], ap["w"], ap["d"],
                      ap["consts"][:, 0:3, :], x2)
    feed_forward(nc, x2, ap["wg"].rearrange("(k p) f -> p k f", p=P), ap["wu"].rearrange("(k p) f -> p k f", p=P),
                 ap["wd"], ap["ga"], ap["ua"], ap["da"], ap["gb"], ap["ub"], ap["db"], ap["expert_bias"],
                 ap["consts"], out)


def kernel(x, fside_BxS2xS2_0, ctx_1024, L0_attn_Wqkv_w, L0_attn_Wqkv_b, L0_attn_out_w, L0_attn_out_b,
           L0_ffn_W_router, L0_ffn_W_gate, L0_ffn_W_up, L0_ffn_W_down, L0_ffn_sA_gate, L0_ffn_sB_gate,
           L0_ffn_sA_up, L0_ffn_sB_up, L0_ffn_sA_down, L0_ffn_sB_down, L0_ffn_A_gate, L0_ffn_B_gate,
           L0_ffn_A_up, L0_ffn_B_up, L0_ffn_A_down, L0_ffn_B_down, L0_ffn_expert_bias):
    import concourse.bacc as bacc
    from concourse.bass_utils import run_bass_kernel_spmd

    def host(a):
        return np.ascontiguousarray(np.asarray(a))

    def lora_in(routed, shared, *more):
        routed = host(routed)
        return host(np.concatenate([routed.transpose(1, 0, 2).reshape(routed.shape[1], ER), host(shared), *more], axis=1))

    def lora_out(routed, shared):
        return host(np.concatenate([host(routed).reshape(ER, -1), host(shared)], axis=0))

    consts = np.zeros((P, 4, P), np.float32)
    consts[:, 0, :] = np.eye(P, dtype=np.float32)
    consts[:, 1, :] = np.triu(np.full((P, P), NEG, np.float32), 1)
    consts[:, 2, :] = np.tril(np.full((P, P), NEG, np.float32), -1)
    consts[:, 3, 0:EXPERTS * EXPERTS] = np.tril(np.ones((EXPERTS, EXPERTS), np.float32), -1).reshape(-1)
    bqkv = host(L0_attn_Wqkv_b)
    arrays = {
        "x": host(x), "wqkvT": host(host(L0_attn_Wqkv_w).T), "woT": host(host(L0_attn_out_w).T),
        "bq": host(bqkv[0:D].reshape(KT, P).T), "bkv": host(bqkv[D:QKV].reshape(2 * HD, 1)), "bo": host(L0_attn_out_b),
        "w": host(fside_BxS2xS2_0), "d": host(ctx_1024),
        "wg": host(L0_ffn_W_gate), "wu": host(L0_ffn_W_up), "wd": host(L0_ffn_W_down),
        "ga": lora_in(L0_ffn_A_gate, L0_ffn_sA_gate, np.zeros((D, ROUTE - LR), np.float32), host(L0_ffn_W_router)),
        "ua": lora_in(L0_ffn_A_up, L0_ffn_sA_up), "da": lora_in(L0_ffn_A_down, L0_ffn_sA_down),
        "gb": lora_out(L0_ffn_B_gate, L0_ffn_sB_gate), "ub": lora_out(L0_ffn_B_up, L0_ffn_sB_up),
        "db": lora_out(L0_ffn_B_down, L0_ffn_sB_down), "expert_bias": host(L0_ffn_expert_bias), "consts": consts,
    }
    nc = bacc.Bacc("TRN2", target_bir_lowering=False, num_devices=1)
    build(nc, arrays)
    got = run_bass_kernel_spmd(nc, [arrays], core_ids=[0])
    return got.results[0]["out"]
```
